# Optimizing a Trainium2 kernel written in Bass

```python
import numpy as np
import jax
import jax.numpy as jnp

def _softmax(x, axis=-1):
    return jax.nn.softmax(x, axis=axis)

def _gelu(x):
    return jax.nn.gelu(x, approximate=True)

def _silu(x):
    return jax.nn.silu(x)

def _sigmoid(x):
    return jax.nn.sigmoid(x)

def _layernorm(x, axis=-1, eps=1e-05):
    m = jnp.mean(x, axis=axis, keepdims=True)
    v = jnp.var(x, axis=axis, keepdims=True)
    return (x - m) / jnp.sqrt(v + eps)

def _scatter_add(tgt, idx, src, axis=0):
    return tgt.at[idx].add(src)

def _segment_sum(src, seg, n):
    return jax.ops.segment_sum(src, seg, n)
kernel_name = 'mk_adj_ffn_d2_adj_r2_5d8412'

def setup_inputs(seed: int=0):
    np.random.seed(seed)
    _w = jnp.asarray

    def _rec_inputs():
        import jax
        import jax.numpy as jnp
        _gk = jax.random.key(seed)
        x = -0.0002928 + 1 * jax.random.normal(jax.random.fold_in(_gk, 1), (8, 1024, 128), jnp.float32)
        _w = (1.0 + jnp.arange(1024, dtype=jnp.float32)) ** (-0.5)
        _w = _w / _w.mean()
        _pij = jnp.clip(0.00390625 * _w[:, None] * _w[None, :], 0.0, 1.0)
        _a = jax.random.uniform(jax.random.fold_in(_gk, 2), (1024, 1024)) < _pij
        _a = jnp.logical_or(_a, jnp.eye(1024, dtype=bool))
        _af = _a.astype(jnp.float32)
        adj = _af
        return (x, adj)
    x, adj = _rec_inputs()

    def _L0_gnn_setup():
        import jax, jax.numpy as jnp
        import numpy as np
        ALPHA = 0.2
        key = jax.random.key(seed)
        k1, k2, k3, k4 = jax.random.split(key, 4)
        B, N, Fin, Fout = (8, 1024, 128, 128)
        h = jax.random.normal(k1, (B, N, Fin), dtype=jnp.float32)
        adj = jax.random.randint(k2, (N, N), 0, 2).astype(jnp.float32)
        adj = jnp.maximum(adj, jnp.eye(N, dtype=jnp.float32))

        def xavier(k, shape, gain=1.414):
            fan_in, fan_out = (shape[0], shape[1])
            a = gain * np.sqrt(6.0 / (fan_in + fan_out))
            return jax.random.uniform(k, shape, dtype=jnp.float32, minval=-a, maxval=a)
        W = xavier(k3, (Fin, Fout))
        a = xavier(k4, (2 * Fout, 1))
        return {'h': h, 'adj_matrix': adj, 'W': W, 'a': a}
    _L0_gnn_all = _L0_gnn_setup()
    _L0_gnn_in = {k: v for k, v in _L0_gnn_all.items() if k in ('W', 'a')}
    del _L0_gnn_all

    def _L0_ffn_setup():
        import jax, jax.numpy as jnp
        import numpy as np
        E = 8
        K = 2
        D = 128
        H = 256
        DOUT = 128
        EPS = 1e-05
        key = jax.random.key(seed)
        ks = jax.random.split(key, 9)
        s = 0.02
        return {'x': jax.random.normal(ks[0], (4, 4096, D), jnp.float32), 'gamma': 1.0 + 0.05 * jax.random.normal(ks[1], (D,), jnp.float32), 'beta': 0.05 * jax.random.normal(ks[2], (D,), jnp.float32), 'Wr': 0.01 * jax.random.normal(ks[3], (D, E), jnp.float32), 'br': jnp.zeros((E,), jnp.float32), 'W1': s * jax.random.normal(ks[4], (E, D, H), jnp.float32), 'b1': s * jax.random.normal(ks[5], (E, H), jnp.float32), 'W2': s * jax.random.normal(ks[6], (E, H, DOUT), jnp.float32), 'b2': s * jax.random.normal(ks[7], (E, DOUT), jnp.float32)}
    _L0_ffn_all = _L0_ffn_setup()
    _L0_ffn_in = {k: v for k, v in _L0_ffn_all.items() if k in ('gamma', 'beta', 'Wr', 'br', 'W1', 'b1', 'W2', 'b2')}
    del _L0_ffn_all

    def _L1_gnn_setup():
        import jax, jax.numpy as jnp
        import numpy as np
        B, T, D, H = (64, 1024, 128, 128)
        MAX_SKIP = 4

        def _lstm_last(Wih, Whh, bih, bhh, xs):
            N, _, Hd = xs.shape
            bias = bih + bhh

            def step(carry, x_t):
                h, c = carry
                g = x_t @ Wih.T + h @ Whh.T + bias
                i, f, gg, o = jnp.split(g, 4, axis=-1)
                c = jax.nn.sigmoid(f) * c + jax.nn.sigmoid(i) * jnp.tanh(gg)
                h = jax.nn.sigmoid(o) * jnp.tanh(c)
                return ((h, c), None)
            init = (jnp.zeros((N, Hd), xs.dtype), jnp.zeros((N, Hd), xs.dtype))
            (h_last, _), _ = jax.lax.scan(step, init, jnp.swapaxes(xs, 0, 1))
            return h_last
        key = jax.random.key(seed)
        ks = jax.random.split(key, 8)
        s = 0.05
        x = jax.random.normal(ks[0], (B, T, D), jnp.float32)
        adj = jax.random.uniform(ks[1], (T, T), jnp.float32) / T
        Wg0 = jax.random.normal(ks[2], (D, H), jnp.float32) * s
        bg0 = jnp.zeros((H,), jnp.float32)
        Wg1 = jax.random.normal(ks[3], (H, H), jnp.float32) * s
        bg1 = jnp.zeros((H,), jnp.float32)
        Wih = jax.random.normal(ks[4], (MAX_SKIP, 4 * H, H), jnp.float32) * s
        Whh = jax.random.normal(ks[5], (MAX_SKIP, 4 * H, H), jnp.float32) * s
        bih = jax.random.normal(ks[6], (MAX_SKIP, 4 * H), jnp.float32) * s
        bhh = jax.random.normal(ks[7], (MAX_SKIP, 4 * H), jnp.float32) * s
        return dict(x=x, adj=adj, Wg0=Wg0, bg0=bg0, Wg1=Wg1, bg1=bg1, Wih=Wih, Whh=Whh, bih=bih, bhh=bhh)
    _L1_gnn_all = _L1_gnn_setup()
    _L1_gnn_in = {k: v for k, v in _L1_gnn_all.items() if k in ('Wg0', 'bg0', 'Wg1', 'bg1', 'Wih', 'Whh', 'bih', 'bhh')}
    del _L1_gnn_all

    def _L1_ffn_setup():
        import jax, jax.numpy as jnp
        import numpy as np
        B, S, D, H, E, K = (8, 4096, 128, 512, 8, 2)
        key = jax.random.key(seed)
        ks = jax.random.split(key, 7)
        s_in = 1.0 / np.sqrt(D)
        s_hid = 1.0 / np.sqrt(H)
        return {'x': jax.random.normal(ks[0], (B, S, D), dtype=jnp.float32), 'Wg': jax.random.uniform(ks[1], (E, D), jnp.float32, -s_in, s_in), 'bg': jax.random.uniform(ks[2], (E,), jnp.float32, -s_in, s_in), 'W1': jax.random.uniform(ks[3], (E, H, D), jnp.float32, -s_in, s_in), 'b1': jax.random.uniform(ks[4], (E, H), jnp.float32, -s_in, s_in), 'W2': jax.random.uniform(ks[5], (E, D, H), jnp.float32, -s_hid, s_hid), 'b2': jax.random.uniform(ks[6], (E, D), jnp.float32, -s_hid, s_hid)}
    _L1_ffn_all = _L1_ffn_setup()
    _L1_ffn_in = {k: v for k, v in _L1_ffn_all.items() if k in ('Wg', 'bg', 'W1', 'b1', 'W2', 'b2')}
    del _L1_ffn_all
    return {'x': x, 'adj': adj, 'L0_gnn_W': _L0_gnn_in['W'], 'L0_gnn_a': _L0_gnn_in['a'], 'L0_ffn_gamma': _L0_ffn_in['gamma'], 'L0_ffn_beta': _L0_ffn_in['beta'], 'L0_ffn_Wr': _L0_ffn_in['Wr'], 'L0_ffn_br': _L0_ffn_in['br'], 'L0_ffn_W1': _L0_ffn_in['W1'], 'L0_ffn_b1': _L0_ffn_in['b1'], 'L0_ffn_W2': _L0_ffn_in['W2'], 'L0_ffn_b2': _L0_ffn_in['b2'], 'L1_gnn_Wg0': _L1_gnn_in['Wg0'], 'L1_gnn_bg0': _L1_gnn_in['bg0'], 'L1_gnn_Wg1': _L1_gnn_in['Wg1'], 'L1_gnn_bg1': _L1_gnn_in['bg1'], 'L1_gnn_Wih': _L1_gnn_in['Wih'], 'L1_gnn_Whh': _L1_gnn_in['Whh'], 'L1_gnn_bih': _L1_gnn_in['bih'], 'L1_gnn_bhh': _L1_gnn_in['bhh'], 'L1_ffn_Wg': _L1_ffn_in['Wg'], 'L1_ffn_bg': _L1_ffn_in['bg'], 'L1_ffn_W1': _L1_ffn_in['W1'], 'L1_ffn_b1': _L1_ffn_in['b1'], 'L1_ffn_W2': _L1_ffn_in['W2'], 'L1_ffn_b2': _L1_ffn_in['b2']}

def reference(x, adj, L0_gnn_W, L0_gnn_a, L0_ffn_gamma, L0_ffn_beta, L0_ffn_Wr, L0_ffn_br, L0_ffn_W1, L0_ffn_b1, L0_ffn_W2, L0_ffn_b2, L1_gnn_Wg0, L1_gnn_bg0, L1_gnn_Wg1, L1_gnn_bg1, L1_gnn_Wih, L1_gnn_Whh, L1_gnn_bih, L1_gnn_bhh, L1_ffn_Wg, L1_ffn_bg, L1_ffn_W1, L1_ffn_b1, L1_ffn_W2, L1_ffn_b2):
    import jax
    import jax.numpy as jnp

    def _L0_gnn_ref(h, adj_matrix, W, a):
        import jax, jax.numpy as jnp
        import numpy as np
        ALPHA = 0.2
        Fout = W.shape[1]
        Wh = jnp.einsum('bnf,fo->bno', h, W)
        a1, a2 = (a[:Fout, 0], a[Fout:, 0])
        s1 = Wh @ a1
        s2 = Wh @ a2
        e = s1[:, :, None] + s2[:, None, :]
        e = jnp.where(e >= 0, e, ALPHA * e)
        e = jnp.where(adj_matrix[None] == 0, -jnp.inf, e)
        attention = jax.nn.softmax(e, axis=-1)
        h_prime = jnp.einsum('bij,bjo->bio', attention, Wh)
        return h_prime

    def _L0_ffn_ref(x, gamma, beta, Wr, br, W1, b1, W2, b2):
        import jax, jax.numpy as jnp
        import numpy as np
        E = 8
        K = 2
        D = 128
        H = 256
        DOUT = 128
        EPS = 1e-05
        mu = jnp.mean(x, axis=-1, keepdims=True)
        var = jnp.mean(jnp.square(x - mu), axis=-1, keepdims=True)
        xn = (x - mu) * jax.lax.rsqrt(var + EPS) * gamma + beta
        logits = jnp.einsum('bsd,de->bse', xn, Wr) + br
        top_vals, top_idx = jax.lax.top_k(logits, K)
        w = jax.nn.softmax(top_vals, axis=-1)
        w_full = jnp.einsum('bsk,bske->bse', w, jax.nn.one_hot(top_idx, E, dtype=w.dtype))
        y = jnp.zeros(x.shape[:-1] + (DOUT,), x.dtype)
        for e in range(E):
            h = jax.nn.gelu(jnp.einsum('bsd,dh->bsh', xn, W1[e]) + b1[e], approximate=False)
            y_e = jnp.einsum('bsh,hd->bsd', h, W2[e]) + b2[e]
            y = y + y_e * w_full[..., e, None]
        return y

    def _L1_gnn_ref(x, adj, Wg0, bg0, Wg1, bg1, Wih, Whh, bih, bhh):
        import jax, jax.numpy as jnp
        import numpy as np
        B, T, D, H = (64, 1024, 128, 128)
        MAX_SKIP = 4

        def _lstm_last(Wih, Whh, bih, bhh, xs):
            N, _, Hd = xs.shape
            bias = bih + bhh

            def step(carry, x_t):
                h, c = carry
                g = x_t @ Wih.T + h @ Whh.T + bias
                i, f, gg, o = jnp.split(g, 4, axis=-1)
                c = jax.nn.sigmoid(f) * c + jax.nn.sigmoid(i) * jnp.tanh(gg)
                h = jax.nn.sigmoid(o) * jnp.tanh(c)
                return ((h, c), None)
            init = (jnp.zeros((N, Hd), xs.dtype), jnp.zeros((N, Hd), xs.dtype))
            (h_last, _), _ = jax.lax.scan(step, init, jnp.swapaxes(xs, 0, 1))
            return h_last
        h = jax.nn.relu(jnp.einsum('ts,bsh->bth', adj, x @ Wg0 + bg0))
        h = jax.nn.relu(jnp.einsum('ts,bsh->bth', adj, h @ Wg1 + bg1))
        Bv, Tv, Hd = h.shape
        for p in range(1, MAX_SKIP + 1):
            nw = Tv // p
            wins = h[:, :nw * p, :].reshape(Bv * nw, p, Hd)
            last = _lstm_last(Wih[p - 1], Whh[p - 1], bih[p - 1], bhh[p - 1], wins)
            idx = jnp.arange(nw) * p + (p - 1)
            h = h.at[:, idx, :].set(last.reshape(Bv, nw, Hd))
        return h

    def _L1_ffn_ref(x, Wg, bg, W1, b1, W2, b2):
        import jax, jax.numpy as jnp
        import numpy as np
        B, S, D, H, E, K = (8, 4096, 128, 512, 8, 2)
        gate_scores = jnp.einsum('bsd,ed->bse', x, Wg) + bg
        topk_scores, topk_idx = jax.lax.top_k(gate_scores, K)
        topk_probs = jax.nn.softmax(topk_scores, axis=-1)
        combine = jnp.sum(topk_probs[..., None] * jax.nn.one_hot(topk_idx, E, dtype=x.dtype), axis=-2)
        out = jnp.zeros_like(x)
        for e in range(E):
            h = jax.nn.relu(jnp.einsum('bsd,hd->bsh', x, W1[e]) + b1[e])
            y = jnp.einsum('bsh,dh->bsd', h, W2[e]) + b2[e]
            out = out + combine[..., e:e + 1] * y
        return out
    x = x + _L0_gnn_ref(_layernorm(x, axis=-1), adj, L0_gnn_W, L0_gnn_a)
    x = x + _L0_ffn_ref(_layernorm(x, axis=-1), L0_ffn_gamma, L0_ffn_beta, L0_ffn_Wr, L0_ffn_br, L0_ffn_W1, L0_ffn_b1, L0_ffn_W2, L0_ffn_b2)
    x = x + _L1_gnn_ref(_layernorm(x, axis=-1), adj, L1_gnn_Wg0, L1_gnn_bg0, L1_gnn_Wg1, L1_gnn_bg1, L1_gnn_Wih, L1_gnn_Whh, L1_gnn_bih, L1_gnn_bhh)
    x = x + _L1_ffn_ref(_layernorm(x, axis=-1), L1_ffn_Wg, L1_ffn_bg, L1_ffn_W1, L1_ffn_b1, L1_ffn_W2, L1_ffn_b2)
    return x

_drawn_inputs = setup_inputs


def setup_inputs(seed=0):
    import zlib

    import numpy as np

    out = dict(_drawn_inputs(seed))
    spreads = {'L0_ffn_br': (0.0, 0.304), 'L1_gnn_bg0': (0.0, 0.1), 'L1_gnn_bg1': (0.0, 0.394)}
    factors = {'L0_ffn_gamma': 8.0,
     'L0_ffn_beta': 8.0,
     'L0_ffn_Wr': 3.652,
     'L0_ffn_b1': 8.0,
     'L0_ffn_b2': 3.832,
     'L1_gnn_Whh': 8.0,
     'L1_gnn_bih': 3.266,
     'L1_gnn_bhh': 3.415,
     'L1_ffn_b1': 5.379,
     'L1_ffn_b2': 4.271}
    for name, (base, spread) in spreads.items():
        noise = np.random.default_rng([zlib.crc32(name.encode()), seed]).standard_normal(out[name].shape)
        drawn = base * np.exp(spread * noise) if base else spread * noise
        out[name] = jnp.asarray(drawn.astype(out[name].dtype))
    for name, factor in factors.items():
        out[name] = (out[name] * factor).astype(out[name].dtype)
    return out
```

```python
from contextlib import ExitStack

import concourse.bass as bass
from concourse import mybir

P = 128
ALU = mybir.AluOpType
ACT = mybir.ActivationFunctionType
AX = mybir.AxisListType
F32 = mybir.dt.float32
F32R = mybir.dt.float32r
EPS = 1e-5
ALPHA = 0.2
MASKED = -1e30
GT = 4
GN = GT * P
RETIRED = []


def ds(at, size, step=1):
    return bass.ds(at, size) if step == 1 else bass.ds(at, size, step)


class Core:
    pass


def semaphores(nc, ctx, stage, names):
    made = {n: nc.alloc_semaphore(f"{stage}_{n}") for n in names.split()}
    ctx.callback(RETIRED.extend, made.values())
    return made


def recycle_semaphores(nc):
    with nc.Block() as block:
        @block.gpsimd
        def _(pool):
            for sem in RETIRED:
                pool.sem_clear(sem)
    for sem in RETIRED:
        nc.release_semaphore(sem)
    RETIRED.clear()


def passes(hi_lo_stationary, hi_lo_moving):
    (wh, wl), (mh, ml) = hi_lo_stationary, hi_lo_moving
    return ((wh, mh), (wh, ml), (wl, mh))


def before(n):
    return n + 1


def done(n):
    return n + 3


NORM_SEMS = "xn_ready transposed"


def norm_buffers(nc, ctx, stage):
    return [ctx.enter_context(nc.sbuf_tensor(f"{stage}_xn{i}", [P, GN], F32)) for i in range(2)]


def normalise_group(dve, c, xn, s, g, par):
    dve.wait_ge(s["transposed"], before(g))
    for k in range(GT):
        last = dve.tensor_scalar(xn[par][:, k * P:(k + 1) * P], c.x[:, ds(g * GN + k * P, P)],
                                 c.mean[:, ds(g * GT + k, 1)], c.rstd[:, ds(g * GT + k, 1)], ALU.subtract, ALU.mult)
    last.then_inc(s["xn_ready"], 1)


def transpose_group(pe, c, xn, s, g, par, psum):
    pe.wait_ge(s["xn_ready"], g + 1)
    pe.wait_ge(s["hT_ready"], before(g))
    for k in range(GT):
        m = pe.transpose(psum[:, k * P:(k + 1) * P], xn[par][:, k * P:(k + 1) * P], c.ident[:, :])
    m.then_inc(s["transposed"], 1)


def stage_load(c):
    nc = c.nc
    with ExitStack() as ctx:
        s = semaphores(nc, ctx, "load", "zeroed x_in")
        block = ctx.enter_context(nc.Block())

        @block.sync
        def _(sp):
            n = c.T // 4
            for q in range(4):
                sp.dma_start(c.x[:, q * n:(q + 1) * n], c.ins["x"][:, q * n:(q + 1) * n]).then_inc(s["x_in"], 16)
            sp.wait_ge(s["x_in"], 64)

        @block.vector
        def _(dve):
            dve.memset(c.ones[:, :], 1.0)

        @block.gpsimd
        def _(pool):
            pool.memset(c.ident[:, :], 0.0).then_inc(s["zeroed"], 1)
            pool.wait_ge(s["zeroed"], 1)
            pool.affine_select(out=c.ident[:, :], in_=c.ident[:, :], compare_op=ALU.not_equal, fill=1.0,
                               base=0, pattern=[[-1, P]], channel_multiplier=1)


def stage_row_stats(c, stage, twice):
    nc = c.nc
    NT = c.TILES
    with ExitStack() as ctx:
        halves = ctx.enter_context(nc.sbuf_tensor(stage + "_halves", [P, NT, 6], F32))
        mean2, half, sq, m2, var, sd, v2 = (ctx.enter_context(nc.sbuf_tensor(f"{stage}_{n}", [P, NT], F32))
                                            for n in ("mean2", "half", "sq", "m2", "var", "sd", "v2"))
        s = semaphores(nc, ctx, stage, "stats step deviation")
        rounds = 2 if twice else 1
        block = ctx.enter_context(nc.Block())

        @block.vector
        def _(dve):
            with dve.Fori(0, NT // 4) as it:
                for k in range(4):
                    last = dve.bn_stats(halves[:, :, :].rearrange("p t s -> p (t s)")[:, ds((it * 4 + k) * 6, 6)],
                                        c.x[:, ds((it * 4 + k) * P, P)])
                last.then_inc(s["stats"], 1)
            dve.wait_ge(s["stats"], NT // 4)
            me, mo, qe, qo = (halves[:, :, j] for j in (1, 4, 2, 5))
            dve.tensor_tensor(mean2[:, :], me, mo, ALU.add)
            dve.tensor_tensor(half[:, :], me, mo, ALU.subtract)
            dve.tensor_tensor(m2[:, :], qe, qo, ALU.add).then_inc(s["step"], 1)
            dve.wait_ge(s["step"], 1)
            dve.tensor_scalar(c.mean[:, :], mean2[:, :], 0.5, None, ALU.mult)
            dve.scalar_tensor_tensor(sq[:, :], half[:, :], 0.25, half[:, :], ALU.mult, ALU.mult).then_inc(s["step"], 1)
            dve.wait_ge(s["step"], 2)
            dve.scalar_tensor_tensor(var[:, :], m2[:, :], 1.0 / P, sq[:, :], ALU.mult, ALU.add).then_inc(s["step"], 1)
            dve.wait_ge(s["step"], 3)
            dve.tensor_scalar(v2[:, :], var[:, :], EPS, None, ALU.add).then_inc(s["step"], 1)
            dve.wait_ge(s["deviation"], 1)
            dve.reciprocal(c.rstd[:, :], sd[:, :]).then_inc(s["step"], 1)
            if twice:
                dve.wait_ge(s["step"], 5)
                dve.tensor_tensor(sq[:, :], var[:, :], c.rstd[:, :], ALU.mult).then_inc(s["step"], 1)
                dve.wait_ge(s["step"], 6)
                dve.tensor_tensor(m2[:, :], sq[:, :], c.rstd[:, :], ALU.mult).then_inc(s["step"], 1)
                dve.wait_ge(s["step"], 7)
                dve.tensor_scalar(v2[:, :], m2[:, :], EPS, None, ALU.add).then_inc(s["step"], 1)
                dve.wait_ge(s["deviation"], 2)
                dve.reciprocal(half[:, :], sd[:, :]).then_inc(s["step"], 1)
                dve.wait_ge(s["step"], 9)
                dve.tensor_tensor(c.rstd[:, :], c.rstd[:, :], half[:, :], ALU.mult)

        @block.scalar
        def _(act):
            for n in range(rounds):
                act.wait_ge(s["step"], (4, 8)[n])
                act.activation(sd[:, :], v2[:, :], ACT.Sqrt).then_inc(s["deviation"], 1)


def stage_attention(c):
    nc = c.nc
    N, B, NT = c.N, c.B, c.N // P
    with ExitStack() as outer:
        def sbo(name, shape, dt=F32):
            return outer.enter_context(nc.sbuf_tensor("att_" + name, shape, dt))
        Wh = sbo("Wh", [P, c.T])
        s2row = sbo("s2row", [P, c.T])
        s1col = sbo("s1col", [P, c.TILES])
        s1col8 = sbo("s1col8", [P, c.TILES])
        mask = sbo("mask", [P, NT, N])

        with ExitStack() as ctx:
            def sb(name, shape, dt=F32):
                return ctx.enter_context(nc.sbuf_tensor("prj_" + name, shape, dt))
            xn = norm_buffers(nc, ctx, "prj")
            W = sb("W", [P, P])
            WT = sb("WT", [P, P])
            a12 = sb("a12", [P, 2])
            Wa = sb("Wa", [P, 2])
            Wa2rep = sb("Wa2rep", [P, P])
            hT = [sb(f"hT{i}", [P, GN]) for i in range(2)]
            ps = ctx.enter_context(nc.psum_tensor("prj_ps", [P, 8, 512], F32))
            psT, psW, psR, psS = (lambda i: ps[:, i, :]), (lambda i: ps[:, 2 + i, :]), (lambda i: ps[:, 4 + i, :]), (lambda i: ps[:, 6 + i, 0:8])
            s = semaphores(nc, ctx, "prj", NORM_SEMS + " w_in adj_in wa wa_sb wrep "
                           "hT_ready projected Wh_out row_out s1_out")
            block = ctx.enter_context(nc.Block())

            @block.sync
            def _(sp):
                sp.dma_start(W[:, :], c.ins["L0_gnn_W"]).then_inc(s["w_in"], 16)
                sp.dma_start(WT[:, :], c.ins["L0_gnn_WT"]).then_inc(s["w_in"], 16)
                sp.dma_start(a12[:, :], c.ins["L0_gnn_a"]).then_inc(s["w_in"], 16)
                sp.dma_start(mask[:, :, :], c.ins["adj"]).then_inc(s["adj_in"], 16)

            @block.gpsimd
            def _(pool):
                pool.wait_ge(s["adj_in"], 16)
                for t in range(NT):
                    pool.tensor_scalar(mask[:, t, :], mask[:, t, :], 0.0, MASKED, ALU.is_equal, ALU.mult)

            @block.tensor
            def _(pe):
                pe.wait_ge(s["w_in"], 48)
                pe.matmul(ps[:, 1, 0:2], WT[:, :], a12[:, :], start=True, stop=True).then_inc(s["wa"], 1)
                pe.wait_ge(s["wrep"], 1)
                pe.sem_inc(s["transposed"], 2)
                with pe.Fori(0, c.GROUPS // 2) as it:
                    for par in range(2):
                        transpose_group(pe, c, xn, s, it * 2 + par, par, psT(par))
                    for par in range(2):
                        g = it * 2 + par
                        pe.wait_ge(s["hT_ready"], done(g))
                        pe.wait_ge(s["Wh_out"], before(g))
                        pe.wait_ge(s["row_out"], before(g))
                        pe.wait_ge(s["s1_out"], before(g))
                        for k in range(GT):
                            pe.matmul(psW(par)[:, k * P:(k + 1) * P], hT[par][:, k * P:(k + 1) * P], W[:, :], start=True, stop=True)
                        for k in range(GT):
                            pe.matmul(psS(par)[:, 2 * k:2 * k + 2], hT[par][:, k * P:(k + 1) * P], Wa[:, :], start=True, stop=True)
                        pe.matmul(psR(par), Wa2rep[:, :], hT[par][:, :], start=True, stop=True).then_inc(s["projected"], 1)

            @block.scalar
            def _(act):
                act.sem_inc(s["hT_ready"], 2)
                act.sem_inc(s["row_out"], 2)
                with act.Fori(0, c.GROUPS // 2) as it:
                    for par in range(2):
                        g = it * 2 + par
                        act.wait_ge(s["transposed"], done(g))
                        act.wait_ge(s["row_out"], before(g))
                        act.copy(hT[par][:, :], psT(par)).then_inc(s["hT_ready"], 1)
                    for par in range(2):
                        g = it * 2 + par
                        act.wait_ge(s["projected"], g + 1)
                        act.copy(s2row[:, ds(g * GN, GN)], psR(par)).then_inc(s["row_out"], 1)

            @block.vector
            def _(dve):
                dve.sem_inc(s["Wh_out"], 2)
                dve.sem_inc(s["s1_out"], 2)
                dve.wait_ge(s["wa"], 1)
                dve.tensor_copy(Wa[:, :], ps[:, 1, 0:2]).then_inc(s["wa_sb"], 1)
                dve.wait_ge(s["wa_sb"], 1)
                dve.tensor_scalar(Wa2rep[:, :], c.ones[:, :], Wa[:, 1:2], None, ALU.mult).then_inc(s["wrep"], 1)
                with dve.Fori(0, c.GROUPS // 2) as it:
                    for par in range(2):
                        normalise_group(dve, c, xn, s, it * 2 + par, par)
                    for par in range(2):
                        g = it * 2 + par
                        dve.wait_ge(s["projected"], g + 1)
                        dve.tensor_copy(Wh[:, ds(g * GN, GN)], psW(par)).then_inc(s["Wh_out"], 1)
                        dve.tensor_copy(s1col[:, ds(g * GT, GT)], psS(par).rearrange("p (k c) -> p k c", c=2)[:, :, 0]).then_inc(s["s1_out"], 1)
                dve.wait_ge(s["s1_out"], done(c.GROUPS - 1))
                dve.tensor_scalar(s1col8[:, :], s1col[:, :], 1 - ALPHA, None, ALU.mult)

        with ExitStack() as ctx:
            def sb(name, shape, dt=F32):
                return [ctx.enter_context(nc.sbuf_tensor(f"att_{name}{i}", shape, dt)) for i in range(2)]
            q = sb("q", [P, N])
            e = sb("e", [P, N])
            p = sb("p", [P, N])
            pT = sb("pT", [P, N])
            M, m8, m2, bias, den, rden = (sb(n, [P, 1]) for n in ("M", "m8", "m2", "bias", "den", "rden"))
            ps = ctx.enter_context(nc.psum_tensor("att_ps", [P, 8, 512], F32))
            s = semaphores(nc, ctx, "att", "q_ready max_ready small bias_ready relu_ready e_ready p_ready "
                           "transposed pT_lo pT_hi attended rden_ready x_out")
            H2 = N // 2
            block = ctx.enter_context(nc.Block())

            @block.gpsimd
            def _(pool):
                pool.sem_inc(s["q_ready"], 2)
                with pool.Fori(0, c.TILES // 2) as it:
                    for par in range(2):
                        i = it * 2 + par
                        pool.wait_ge(s["e_ready"], before(i))
                        pool.tensor_tensor(q[par][:, :], s2row[:, ds(it // (NT // 2) * N, N)],
                                           mask[:, :, :].rearrange("p t n -> p (t n)")[:, ds((it * 2 + par) % NT * N, N)],
                                           ALU.add).then_inc(s["q_ready"], 1)

            @block.vector
            def _(dve):
                for sem in (s["e_ready"], s["bias_ready"], s["pT_hi"], s["x_out"]):
                    dve.sem_inc(sem, 2)
                with dve.Fori(0, c.TILES // 2) as it:
                    for par in range(2):
                        i = it * 2 + par
                        dve.wait_ge(s["q_ready"], done(i))
                        dve.wait_ge(s["p_ready"], before(i))
                        dve.tensor_reduce(M[par][:, :], q[par][:, :], AX.X, ALU.max).then_inc(s["max_ready"], 1)
                        dve.wait_ge(s["max_ready"], i + 1)
                        dve.tensor_scalar(m8[par][:, :], M[par][:, :], s1col[:, ds(i, 1)], 0.0, ALU.add, ALU.max).then_inc(s["small"], 1)
                        dve.tensor_scalar(m2[par][:, :], M[par][:, :], -ALPHA, None, ALU.mult).then_inc(s["small"], 1)
                        dve.wait_ge(s["small"], i * 2 + 2)
                        dve.scalar_tensor_tensor(bias[par][:, :], m8[par][:, :], -(1 - ALPHA), m2[par][:, :],
                                                 ALU.mult, ALU.add).then_inc(s["bias_ready"], 1)
                    for par in range(2):
                        i = it * 2 + par
                        dve.wait_ge(s["relu_ready"], i + 1)
                        dve.scalar_tensor_tensor(e[par][:, :], q[par][:, :], ALPHA, e[par][:, :], ALU.mult, ALU.add).then_inc(s["e_ready"], 1)
                    for par in range(2):
                        i = it * 2 + par
                        dve.wait_ge(s["transposed"], done(i))
                        dve.wait_ge(s["attended"], before(i))
                        dve.tensor_copy(pT[par][:, H2:], ps[:, 2 * par + 1, :]).then_inc(s["pT_hi"], 1)
                    for par in range(2):
                        i = it * 2 + par
                        dve.wait_ge(s["p_ready"], done(i))
                        dve.reciprocal(rden[par][:, :], den[par][:, :]).then_inc(s["rden_ready"], 1)
                        dve.wait_ge(s["rden_ready"], i + 1)
                        dve.wait_ge(s["attended"], done(i))
                        xt = c.x[:, ds(i * P, P)]
                        dve.scalar_tensor_tensor(xt, ps[:, 4 + par, 0:P], rden[par][:, 0:1], xt, ALU.mult, ALU.add).then_inc(s["x_out"], 1)

            @block.scalar
            def _(act):
                act.sem_inc(s["p_ready"], 2)
                act.sem_inc(s["pT_lo"], 2)
                with act.Fori(0, c.TILES // 2) as it:
                    for par in range(2):
                        i = it * 2 + par
                        act.wait_ge(s["q_ready"], done(i))
                        act.wait_ge(s["p_ready"], before(i))
                        act.activation(e[par][:, :], q[par][:, :], ACT.Relu, bias=s1col8[:, ds(i, 1)], scale=1 - ALPHA).then_inc(s["relu_ready"], 1)
                    for par in range(2):
                        i = it * 2 + par
                        act.wait_ge(s["e_ready"], done(i))
                        act.wait_ge(s["bias_ready"], done(i))
                        act.wait_ge(s["transposed"], before(i))
                        act.wait_ge(s["x_out"], before(i))
                        act.activation(p[par][:, :], e[par][:, :], ACT.Exp, bias=bias[par][:, 0:1], accum_out=den[par][:, 0:1]).then_inc(s["p_ready"], 1)
                    for par in range(2):
                        i = it * 2 + par
                        act.wait_ge(s["transposed"], done(i))
                        act.wait_ge(s["attended"], before(i))
                        act.copy(pT[par][:, 0:H2], ps[:, 2 * par, :]).then_inc(s["pT_lo"], 1)

            @block.tensor
            def _(pe):
                pe.sem_inc(s["transposed"], 2)
                pe.sem_inc(s["attended"], 2)
                with pe.Fori(0, c.TILES // 2) as it:
                    for par in range(2):
                        i = it * 2 + par
                        pe.wait_ge(s["p_ready"], done(i))
                        pe.wait_ge(s["pT_lo"], before(i))
                        pe.wait_ge(s["pT_hi"], before(i))
                        for j in range(NT):
                            m = pe.transpose(ps[:, 2 * par + j // 4, j % 4 * P:(j % 4 + 1) * P], p[par][:, j * P:(j + 1) * P], c.ident[:, :])
                        m.then_inc(s["transposed"], 1)
                    for par in range(2):
                        i = it * 2 + par
                        pe.wait_ge(s["pT_lo"], done(i))
                        pe.wait_ge(s["pT_hi"], done(i))
                        pe.wait_ge(s["x_out"], before(i))
                        for j in range(NT):
                            m = pe.matmul(ps[:, 4 + par, 0:P], pT[par][:, j * P:(j + 1) * P],
                                          Wh[:, ds((it // (NT // 2) * NT + j) * P, P)], start=(j == 0), stop=(j == NT - 1))
                        m.then_inc(s["attended"], 1)


def stage_experts(c, layer):
    nc = c.nc
    L = f"L{layer}_"
    W1, b1, W2, b2, Wr, br = (c.ins[L + n] for n in ("W1", "b1", "W2", "b2", "Wr", "br"))
    E, _, H = W1.shape
    HC = H // P
    act_fn = (ACT.Gelu, ACT.Relu)[layer]
    affine = layer == 0
    T, TILES, GROUPS = c.T, c.TILES, c.GROUPS
    with ExitStack() as outer:
        def sbo(name, shape, dt=F32):
            return outer.enter_context(nc.sbuf_tensor(L + name, shape, dt))
        h_hi = sbo("h_hi", [P, T], F32R)
        h_lo = sbo("h_lo", [P, T], F32R)
        scores = sbo("scores", [P, TILES, E])
        weight = sbo("weight", [P, TILES, E])
        b1col = sbo("b1col", [P, E * HC])
        b2row = sbo("b2row", [E, P])

        with ExitStack() as ctx:
            def sb(name, shape, dt=F32):
                return ctx.enter_context(nc.sbuf_tensor(L + name, shape, dt))
            xn = norm_buffers(nc, ctx, L + "rt")
            h = [sb(f"h{i}", [P, GN]) for i in range(2)]
            wr = sb("wr", [P, E])
            br4 = sb("br4", [P, GT, E])
            gb = sb("gb", [P, 2])
            ps = ctx.enter_context(nc.psum_tensor(L + "rt_ps", [P, 4, 512], F32))
            s = semaphores(nc, ctx, L + "rt", NORM_SEMS + " w_in hT_ready hi_ready lo_ready routed scores_out")
            block = ctx.enter_context(nc.Block())

            @block.sync
            def _(sp):
                sp.dma_start(wr[:, :], Wr).then_inc(s["w_in"], 16)
                sp.dma_start(b1col[:, :], b1).then_inc(s["w_in"], 16)
                sp.dma_start(b2row[:, :], b2).then_inc(s["w_in"], 16)
                for k in range(GT):
                    sp.dma_start(br4[:, k, :], br.broadcast_to([P, E])).then_inc(s["w_in"], 16)
                if affine:
                    sp.dma_start(gb[:, 0:1], c.ins["L0_gamma"]).then_inc(s["w_in"], 16)
                    sp.dma_start(gb[:, 1:2], c.ins["L0_beta"]).then_inc(s["w_in"], 16)
                sp.wait_ge(s["w_in"], (3 + GT + (2 if affine else 0)) * 16)

            loads = (3 + GT + (2 if affine else 0)) * 16

            @block.vector
            def _(dve):
                dve.sem_inc(s["lo_ready"], 2)
                dve.sem_inc(s["scores_out"], 2)
                dve.wait_ge(s["w_in"], loads)
                with dve.Fori(0, GROUPS // 2) as it:
                    for par in range(2):
                        normalise_group(dve, c, xn, s, it * 2 + par, par)
                    for par in range(2):
                        g = it * 2 + par
                        dve.wait_ge(s["hT_ready"], done(g))
                        dve.tensor_copy(h_hi[:, ds(g * GN, GN)], h[par][:, :]).then_inc(s["hi_ready"], 1)
                        dve.wait_ge(s["hi_ready"], g + 1)
                        dve.tensor_tensor(h_lo[:, ds(g * GN, GN)], h[par][:, :], h_hi[:, ds(g * GN, GN)].bitcast(F32),
                                          ALU.subtract).then_inc(s["lo_ready"], 1)
                        dve.wait_ge(s["routed"], g + 1)
                        dve.tensor_tensor(scores[:, :, :].rearrange("p t e -> p (t e)")[:, ds(g * GT * E, GT * E)],
                                          ps[:, 2 + par, 0:GT * E], br4[:, :, :].rearrange("p t e -> p (t e)"),
                                          ALU.add).then_inc(s["scores_out"], 1)

            @block.scalar
            def _(act):
                act.sem_inc(s["hT_ready"], 2)
                act.wait_ge(s["w_in"], loads)
                with act.Fori(0, GROUPS // 2) as it:
                    for par in range(2):
                        g = it * 2 + par
                        act.wait_ge(s["transposed"], done(g))
                        act.wait_ge(s["lo_ready"], before(g))
                        act.wait_ge(s["scores_out"], before(g))
                        if affine:
                            act.activation(h[par][:, :], ps[:, par, :], ACT.Identity, bias=gb[:, 1:2], scale=gb[:, 0:1]).then_inc(s["hT_ready"], 1)
                        else:
                            act.copy(h[par][:, :], ps[:, par, :]).then_inc(s["hT_ready"], 1)

            @block.tensor
            def _(pe):
                pe.sem_inc(s["transposed"], 2)
                pe.wait_ge(s["w_in"], loads)
                with pe.Fori(0, GROUPS // 2) as it:
                    for par in range(2):
                        transpose_group(pe, c, xn, s, it * 2 + par, par, ps[:, par, :])
                    for par in range(2):
                        g = it * 2 + par
                        pe.wait_ge(s["hT_ready"], done(g))
                        pe.wait_ge(s["scores_out"], before(g))
                        for k in range(GT):
                            m = pe.matmul(ps[:, 2 + par, k * E:(k + 1) * E], h[par][:, k * P:(k + 1) * P], wr[:, :], start=True, stop=True)
                        m.then_inc(s["routed"], 1)

        with ExitStack() as ctx:
            def sb(name, shape, dt=F32):
                return ctx.enter_context(nc.sbuf_tensor(L + name, shape, dt))
            rank = sb("rank", [P, TILES, E])
            eq, seen, first, second, rest = (sb(n, [P, TILES, E]) for n in ("eq", "seen", "first", "second", "rest"))
            top1, top2, at1, at2, gap, ex, den, w1, w2 = (sb(n, [P, TILES]) for n in ("top1", "top2", "at1", "at2", "gap", "ex", "den", "w1", "w2"))
            wcopy = [sb(f"wcopy{i}", [P, E]) for i in range(2)]
            wT = [sb(f"wT{i}", [E, P]) for i in range(2)]
            ps = ctx.enter_context(nc.psum_tensor(L + "gate_ps", [P, 4, 512], F32))
            s = semaphores(nc, ctx, L + "gate", "rank_ready step exp_done weight_ready w_copied w_turned wT_ready mixed x_out")
            block = ctx.enter_context(nc.Block())

            def each(a):
                return a[:, :].unsqueeze(2).broadcast_to([P, TILES, E])

            @block.gpsimd
            def _(pool):
                for e in range(E):
                    last = pool.memset(rank[:, :, e], float(E - e))
                last.then_inc(s["rank_ready"], 1)

            @block.vector
            def _(dve):
                n = [0]

                def step(instruction):
                    n[0] += 1
                    instruction.then_inc(s["step"], 1)
                    dve.wait_ge(s["step"], n[0])

                def pick(values, top, at, chosen):
                    step(dve.tensor_reduce(top[:, :], values[:, :, :], AX.X, ALU.max))
                    step(dve.tensor_tensor(eq[:, :, :], values[:, :, :], each(top), ALU.is_equal))
                    step(dve.tensor_tensor(seen[:, :, :], eq[:, :, :], rank[:, :, :], ALU.mult))
                    step(dve.tensor_reduce(at[:, :], seen[:, :, :], AX.X, ALU.max))
                    step(dve.tensor_tensor(chosen[:, :, :], rank[:, :, :], each(at), ALU.is_equal))

                dve.sem_inc(s["wT_ready"], 2)
                dve.sem_inc(s["x_out"], 2)
                dve.wait_ge(s["rank_ready"], 1)
                pick(scores, top1, at1, first)
                step(dve.scalar_tensor_tensor(rest[:, :, :], first[:, :, :], MASKED, scores[:, :, :], ALU.mult, ALU.add))
                pick(rest, top2, at2, second)
                step(dve.tensor_tensor(gap[:, :], top2[:, :], top1[:, :], ALU.subtract))
                dve.wait_ge(s["exp_done"], 1)
                step(dve.tensor_scalar(den[:, :], ex[:, :], 1.0, None, ALU.add))
                step(dve.reciprocal(w1[:, :], den[:, :]))
                step(dve.tensor_tensor(w2[:, :], ex[:, :], w1[:, :], ALU.mult))
                step(dve.tensor_tensor(eq[:, :, :], first[:, :, :], each(w1), ALU.mult))
                step(dve.tensor_tensor(seen[:, :, :], second[:, :, :], each(w2), ALU.mult))
                dve.tensor_tensor(weight[:, :, :], eq[:, :, :], seen[:, :, :], ALU.add).then_inc(s["weight_ready"], 1)
                with dve.Fori(0, TILES // 2) as it:
                    for par in range(2):
                        i = it * 2 + par
                        dve.wait_ge(s["w_turned"], i + 1)
                        dve.wait_ge(s["x_out"], before(i))
                        dve.tensor_copy(wT[par][:, :], ps[0:E, par, 0:P]).then_inc(s["wT_ready"], 1)
                    for par in range(2):
                        i = it * 2 + par
                        dve.wait_ge(s["mixed"], i + 1)
                        xt = c.x[:, ds(i * P, P)]
                        dve.tensor_tensor(xt, ps[:, 2 + par, 0:P], xt, ALU.add).then_inc(s["x_out"], 1)

            @block.scalar
            def _(act):
                act.wait_ge(s["step"], 12)
                act.activation(ex[:, :], gap[:, :], ACT.Exp).then_inc(s["exp_done"], 1)
                act.wait_ge(s["weight_ready"], 1)
                with act.Fori(0, TILES // 2) as it:
                    for par in range(2):
                        i = it * 2 + par
                        act.wait_ge(s["wT_ready"], before(i))
                        act.copy(wcopy[par][:, :], weight[:, :, :].rearrange("p t e -> p (t e)")[:, ds(i * E, E)]).then_inc(s["w_copied"], 1)

            @block.tensor
            def _(pe):
                with pe.Fori(0, TILES // 2) as it:
                    for par in range(2):
                        i = it * 2 + par
                        pe.wait_ge(s["w_copied"], i + 1)
                        pe.wait_ge(s["wT_ready"], before(i))
                        pe.transpose(ps[0:E, par, 0:P], wcopy[par][:, :], c.ident[:, :]).then_inc(s["w_turned"], 1)
                    for par in range(2):
                        i = it * 2 + par
                        pe.wait_ge(s["wT_ready"], done(i))
                        pe.wait_ge(s["x_out"], before(i))
                        pe.matmul(ps[:, 2 + par, 0:P], wT[par][:, :], b2row[:, :], start=True, stop=True).then_inc(s["mixed"], 1)

        with ExitStack() as ctx:
            def sb(name, shape, dt=F32, n=2):
                return [ctx.enter_context(nc.sbuf_tensor(f"{L}{name}{i}", shape, dt)) for i in range(n)]
            raw1 = sb("raw1", [P, H])
            raw2 = sb("raw2", [P, HC * P])
            w1_hi, w1_lo, w2_hi, w2_lo = (sb(n, [P, H], F32R) for n in ("w1_hi", "w1_lo", "w2_hi", "w2_lo"))
            b1e = sb("b1e", [P, HC])
            u = sb("u", [P, GN])
            u_hi = sb("u_hi", [P, HC, GN], F32R)
            u_lo = sb("u_lo", [P, HC, GN], F32R)
            ps = ctx.enter_context(nc.psum_tensor(L + "ex_ps", [P, 4, 512], F32))
            s = semaphores(nc, ctx, L + "ex", "w_in0 w_in1 whi_ready wlo_ready up u_ready uhi_ready ulo_ready down x_out b1_ready pe_held")
            w_in = (s["w_in0"], s["w_in1"])
            block = ctx.enter_context(nc.Block())

            @block.sync
            def _(sp):
                with sp.Fori(0, E // 2) as ep:
                    for ew in range(2):
                        e = ep * 2 + ew
                        sp.wait_ge(s["wlo_ready"], before(e))
                        sp.dma_start(raw1[ew][:, :], W1.rearrange("e d h -> (e d) h")[ds(e * P, P), :]).then_inc(w_in[ew], 16)
                        sp.dma_start(raw2[ew][:, :], W2.rearrange("e p c d -> (e p) (c d)")[ds(e * P, P), :]).then_inc(w_in[ew], 16)
                sp.wait_ge(s["w_in0"], E // 2 * 32)
                sp.wait_ge(s["w_in1"], E // 2 * 32)

            @block.scalar
            def _(act):
                act.sem_inc(s["whi_ready"], 2)
                act.sem_inc(s["u_ready"], 2)
                with act.Fori(0, E // 2) as ep:
                    for ew in range(2):
                        e = ep * 2 + ew
                        act.wait_ge(w_in[ew], ep * 32 + 32)
                        act.wait_ge(s["down"], e * GROUPS + 2)
                        act.copy(b1e[ew][:, :], b1col[:, ds(e * HC, HC)]).then_inc(s["b1_ready"], 1)
                        act.copy(w1_hi[ew][:, :], raw1[ew][:, :])
                        act.copy(w2_hi[ew][:, :], raw2[ew][:, :]).then_inc(s["whi_ready"], 1)
                        act.wait_ge(s["b1_ready"], e + 1)
                        with act.Fori(0, GROUPS // 2) as it:
                            for par in range(2):
                                g = e * GROUPS + it * 2 + par
                                act.wait_ge(s["down"], before(g))
                                for hc in range(HC):
                                    v = g * HC + hc
                                    act.wait_ge(s["up"], v + 1)
                                    act.wait_ge(s["ulo_ready"], before(v))
                                    last = act.activation(u[hc % 2][:, :], ps[:, hc % 2, :], act_fn, bias=b1e[ew][:, hc:hc + 1])
                                    if hc % 2 == 0:
                                        last = act.activation(u_hi[par][:, hc, :], ps[:, hc % 2, :], act_fn, bias=b1e[ew][:, hc:hc + 1])
                                    last.then_inc(s["u_ready"], 1)

            @block.vector
            def _(dve):
                dve.sem_inc(s["wlo_ready"], 2)
                dve.sem_inc(s["ulo_ready"], 2)
                dve.sem_inc(s["x_out"], 2)
                with dve.Fori(0, E // 2) as ep:
                    for ew in range(2):
                        e = ep * 2 + ew
                        dve.wait_ge(s["whi_ready"], done(e))
                        dve.tensor_tensor(w1_lo[ew][:, :], raw1[ew][:, :], w1_hi[ew][:, :].bitcast(F32), ALU.subtract)
                        dve.tensor_tensor(w2_lo[ew][:, :], raw2[ew][:, :], w2_hi[ew][:, :].bitcast(F32), ALU.subtract).then_inc(s["wlo_ready"], 1)
                        with dve.Fori(0, GROUPS // 2) as it:
                            for par in range(2):
                                g = e * GROUPS + it * 2 + par
                                for hc in range(HC):
                                    v = g * HC + hc
                                    dve.wait_ge(s["u_ready"], done(v))
                                    if hc % 2:
                                        dve.tensor_copy(u_hi[par][:, hc, :], u[hc % 2][:, :]).then_inc(s["uhi_ready"], 1)
                                        dve.wait_ge(s["uhi_ready"], g * (HC // 2) + hc // 2 + 1)
                                    dve.tensor_tensor(u_lo[par][:, hc, :], u[hc % 2][:, :], u_hi[par][:, hc, :].bitcast(F32),
                                                      ALU.subtract).then_inc(s["ulo_ready"], 1)
                            for par in range(2):
                                gt = it * 2 + par
                                g = e * GROUPS + gt
                                dve.wait_ge(s["down"], done(g))
                                dve.wait_ge(s["x_out"], before(g))
                                for k in range(GT):
                                    xt = c.x[:, ds(gt * GN + k * P, P)]
                                    last = dve.scalar_tensor_tensor(
                                        xt, ps[:, 2 + par, k * P:(k + 1) * P],
                                        weight[:, :, :].rearrange("p t e -> p (t e)")[:, ds((gt * GT + k) * E + e, 1)],
                                        xt, ALU.mult, ALU.add)
                                last.then_inc(s["x_out"], 1)

            @block.tensor
            def _(pe):
                pe.sem_inc(s["down"], 2)
                with pe.Fori(0, E // 2) as ep:
                    for ew in range(2):
                        e = ep * 2 + ew
                        pe.wait_ge(s["wlo_ready"], done(e))
                        pe.sem_inc(s["pe_held"], 1)
                        with pe.Fori(0, GROUPS // 2) as it:
                            for par in range(2):
                                g = e * GROUPS + it * 2 + par
                                moving = (h_hi[:, ds((it * 2 + par) * GN, GN)], h_lo[:, ds((it * 2 + par) * GN, GN)])
                                for hc in range(HC):
                                    cs = slice(hc * P, (hc + 1) * P)
                                    pe.wait_ge(s["u_ready"], before(g * HC + hc))
                                    for n, (w, x) in enumerate(passes((w1_hi[ew][:, cs], w1_lo[ew][:, cs]), moving)):
                                        m = pe.matmul(ps[:, hc % 2, :], w, x, start=(n == 0), stop=(n == 2))
                                    m.then_inc(s["up"], 1)
                            for par in range(2):
                                g = e * GROUPS + it * 2 + par
                                pe.wait_ge(s["ulo_ready"], g * HC + HC + 2)
                                pe.wait_ge(s["x_out"], before(g))
                                for k in range(GT):
                                    ks = slice(k * P, (k + 1) * P)
                                    for hc in range(HC):
                                        cs = slice(hc * P, (hc + 1) * P)
                                        for n, (a, w) in enumerate(passes((u_hi[par][:, hc, ks], u_lo[par][:, hc, ks]),
                                                                          (w2_hi[ew][:, cs], w2_lo[ew][:, cs]))):
                                            m = pe.matmul(ps[:, 2 + par, ks], a, w, start=(hc == 0 and n == 0), stop=(hc == HC - 1 and n == 2))
                                m.then_inc(s["down"], 1)


def stage_graph_conv(c):
    nc = c.nc
    T, N, B, GROUPS = c.T, c.N, c.B, c.GROUPS
    NT = N // P
    HALF = B // 2
    with ExitStack() as outer:
        def sbo(name, shape, dt=F32):
            return outer.enter_context(nc.sbuf_tensor("gc_" + name, shape, dt))
        y0 = (sbo("y0_hi", [P, T + 4], F32R), sbo("y0_lo", [P, T + 4], F32R))
        with ExitStack() as conv:
            y1 = tuple(conv.enter_context(nc.sbuf_tensor(f"gc_y1_{n}", [P, T], F32R)) for n in ("hi", "lo"))
            wg = [conv.enter_context(nc.sbuf_tensor(f"gc_wg{i}", [P, P], F32)) for i in range(2)]
            bg = [conv.enter_context(nc.sbuf_tensor(f"gc_bg{i}", [P, HALF, P], F32)) for i in range(2)]

            with ExitStack() as ctx:
                xn = norm_buffers(nc, ctx, "gy")
                hT = [ctx.enter_context(nc.sbuf_tensor(f"gy_hT{i}", [P, GN], F32)) for i in range(2)]
                y = [ctx.enter_context(nc.sbuf_tensor(f"gy_y{i}", [P, GN], F32)) for i in range(2)]
                ps = ctx.enter_context(nc.psum_tensor("gy_ps", [P, 4, 512], F32))
                s = semaphores(nc, ctx, "gy", NORM_SEMS + " w_in hT_ready mapped y_ready hi_ready lo_ready")
                loads = (2 + 2 * HALF) * 16
                block = ctx.enter_context(nc.Block())

                @block.sync
                def _(sp):
                    for i in range(2):
                        sp.dma_start(wg[i][:, :], c.ins[f"Wg{i}"]).then_inc(s["w_in"], 16)
                        for k in range(HALF):
                            sp.dma_start(bg[i][:, k, :], c.ins[f"bg{i}"].broadcast_to([P, P])).then_inc(s["w_in"], 16)
                    sp.wait_ge(s["w_in"], loads)

                @block.vector
                def _(dve):
                    dve.sem_inc(s["y_ready"], 2)
                    dve.sem_inc(s["lo_ready"], 2)
                    dve.wait_ge(s["w_in"], loads)
                    dve.memset(y0[0][:, T:T + 4].bitcast(F32), 0.0)
                    dve.memset(y0[1][:, T:T + 4].bitcast(F32), 0.0)
                    with dve.Fori(0, GROUPS // 2) as it:
                        for par in range(2):
                            normalise_group(dve, c, xn, s, it * 2 + par, par)
                        for par in range(2):
                            g = it * 2 + par
                            dve.wait_ge(s["mapped"], g + 1)
                            dve.tensor_tensor(y[par][:, :], ps[:, 2 + par, :], bg[0][:, :, :].rearrange("p k d -> p (k d)"), ALU.add).then_inc(s["y_ready"], 1)
                            dve.wait_ge(s["hi_ready"], done(g))
                            dve.tensor_tensor(y0[1][:, ds(g * GN, GN)], y[par][:, :], y0[0][:, ds(g * GN, GN)].bitcast(F32),
                                              ALU.subtract).then_inc(s["lo_ready"], 1)

                @block.scalar
                def _(act):
                    act.sem_inc(s["hT_ready"], 2)
                    act.sem_inc(s["hi_ready"], 2)
                    with act.Fori(0, GROUPS // 2) as it:
                        for par in range(2):
                            g = it * 2 + par
                            act.wait_ge(s["transposed"], done(g))
                            act.wait_ge(s["y_ready"], before(g))
                            act.copy(hT[par][:, :], ps[:, par, :]).then_inc(s["hT_ready"], 1)
                        for par in range(2):
                            g = it * 2 + par
                            act.wait_ge(s["y_ready"], done(g))
                            act.copy(y0[0][:, ds(g * GN, GN)], y[par][:, :]).then_inc(s["hi_ready"], 1)

                @block.tensor
                def _(pe):
                    pe.sem_inc(s["transposed"], 2)
                    pe.wait_ge(s["w_in"], loads)
                    with pe.Fori(0, GROUPS // 2) as it:
                        for par in range(2):
                            transpose_group(pe, c, xn, s, it * 2 + par, par, ps[:, par, :])
                        for par in range(2):
                            g = it * 2 + par
                            pe.wait_ge(s["hT_ready"], done(g))
                            pe.wait_ge(s["y_ready"], before(g))
                            for k in range(GT):
                                m = pe.matmul(ps[:, 2 + par, k * P:(k + 1) * P], hT[par][:, k * P:(k + 1) * P], wg[0][:, :], start=True, stop=True)
                            m.then_inc(s["mapped"], 1)

            convolve(c, "gc0", y0, y1, y1, wg[1], bg[1])
            convolve(c, "gc1", y1, y0, y0, None, None)
        recycle_semaphores(nc)
        stage_lstm(c, y0)
        recycle_semaphores(nc)
        add_features(c, y0)


def convolve(c, name, y, _, z, w, b):
    nc = c.nc
    T, N, B = c.T, c.N, c.B
    NT = N // P
    HALF = B // 2
    with ExitStack() as ctx:
        def sb(n, shape, dt=F32, count=2):
            return [ctx.enter_context(nc.sbuf_tensor(f"{name}_{n}{i}", shape, dt)) for i in range(count)]
        adj = sb("adj", [P, N])
        a_hi = sb("a_hi", [P, N], F32R)
        a_lo = sb("a_lo", [P, N], F32R)
        h = sb("h", [P, HALF * P])
        f = sb("f", [P, HALF * P])
        ps = ctx.enter_context(nc.psum_tensor(name + "_ps", [P, 8, 512], F32))
        s = semaphores(nc, ctx, name, "adj_in0 adj_in1 hi_ready lo_ready convolved h_ready turned f_ready mapped z_hi z_lo z_ready")
        adj_in = (s["adj_in0"], s["adj_in1"])
        hi_v = z[0][:, 0:T].rearrange("p (b n) -> p b n", b=B)
        lo_v = z[1][:, 0:T].rearrange("p (b n) -> p b n", b=B)
        block = ctx.enter_context(nc.Block())

        def dest(v, half, t):
            return v[:, half * HALF:(half + 1) * HALF, ds(t * P, P)]

        def by_graph(a):
            return a.rearrange("p (b n) -> p b n", b=HALF)

        @block.sync
        def _(sp):
            rows = c.ins["adjT"].rearrange("t p s j -> (t p) (s j)")
            with sp.Fori(0, NT // 2) as it:
                for par in range(2):
                    t = it * 2 + par
                    sp.wait_ge(s["lo_ready"], before(t))
                    sp.dma_start(adj[par][:, :], rows[ds(t * P, P), :]).then_inc(adj_in[par], 16)
            sp.wait_ge(s["adj_in0"], NT // 2 * 16)
            sp.wait_ge(s["adj_in1"], NT // 2 * 16)

        @block.scalar
        def _(act):
            act.sem_inc(s["hi_ready"], 2)
            act.sem_inc(s["h_ready"], 2)
            act.sem_inc(s["z_hi"], 2)
            with act.Fori(0, NT // 2) as it:
                for par in range(2):
                    t = it * 2 + par
                    act.wait_ge(adj_in[par], it * 16 + 16)
                    act.copy(a_hi[par][:, :], adj[par][:, :]).then_inc(s["hi_ready"], 1)
                    for half in range(2):
                        g = t * 2 + half
                        act.wait_ge(s["convolved"], done(g))
                        act.wait_ge(s["turned"], before(g))
                        act.activation(h[half][:, :], ps[:, half, :], ACT.Relu).then_inc(s["h_ready"], 1)
                    for half in range(2):
                        g = t * 2 + half
                        if w is None:
                            act.wait_ge(s["turned"], done(g))
                            act.copy(dest(hi_v, half, t), by_graph(ps[:, 2 + half, :])).then_inc(s["z_hi"], 1)
                        else:
                            act.wait_ge(s["z_ready"], done(g))
                            act.copy(dest(hi_v, half, t), by_graph(f[half][:, :])).then_inc(s["z_hi"], 1)

        @block.vector
        def _(dve):
            for sem in (s["lo_ready"], s["f_ready"], s["z_ready"], s["z_lo"]):
                dve.sem_inc(sem, 2)
            with dve.Fori(0, NT // 2) as it:
                for par in range(2):
                    t = it * 2 + par
                    dve.wait_ge(s["hi_ready"], done(t))
                    dve.tensor_tensor(a_lo[par][:, :], adj[par][:, :], a_hi[par][:, :].bitcast(F32), ALU.subtract).then_inc(s["lo_ready"], 1)
                    if w is not None:
                        for half in range(2):
                            g = t * 2 + half
                            dve.wait_ge(s["turned"], done(g))
                            dve.wait_ge(s["z_lo"], before(g))
                            dve.tensor_copy(f[half][:, :], ps[:, 2 + half, :]).then_inc(s["f_ready"], 1)
                        for half in range(2):
                            g = t * 2 + half
                            dve.wait_ge(s["mapped"], done(g))
                            dve.tensor_tensor(f[half][:, :], ps[:, 4 + half, :], b[:, :, :].rearrange("p k d -> p (k d)"), ALU.add).then_inc(s["z_ready"], 1)
                    for half in range(2):
                        g = t * 2 + half
                        dve.wait_ge(s["z_hi"], done(g))
                        src = ps[:, 2 + half, :] if w is None else f[half][:, :]
                        dve.tensor_tensor(dest(lo_v, half, t), by_graph(src), dest(hi_v, half, t).bitcast(F32), ALU.subtract).then_inc(s["z_lo"], 1)

        @block.tensor
        def _(pe):
            for sem in (s["convolved"], s["turned"], s["mapped"]):
                pe.sem_inc(sem, 2)
            with pe.Fori(0, NT // 2) as it:
                for par in range(2):
                    t = it * 2 + par
                    pe.wait_ge(s["lo_ready"], done(t))
                    for half in range(2):
                        g = t * 2 + half
                        pe.wait_ge(s["h_ready"], before(g))
                        for st in range(NT):
                            ss = slice(st * P, (st + 1) * P)
                            moving = [v[:, 0:T].rearrange("p (b n) -> p b n", b=B)[:, half * HALF:(half + 1) * HALF, ss] for v in y]
                            for n, (a, m) in enumerate(passes((a_hi[par][:, ss], a_lo[par][:, ss]), moving)):
                                last = pe.matmul(ps[:, half, :], a, m, start=(st == 0 and n == 0), stop=(st == NT - 1 and n == 2))
                        last.then_inc(s["convolved"], 1)
                    for half in range(2):
                        g = t * 2 + half
                        pe.wait_ge(s["h_ready"], done(g))
                        pe.wait_ge(s["z_lo"], before(g))
                        for k in range(HALF):
                            last = pe.transpose(ps[:, 2 + half, k * P:(k + 1) * P], h[half][:, k * P:(k + 1) * P], c.ident[:, :])
                        last.then_inc(s["turned"], 1)
                    if w is not None:
                        for half in range(2):
                            g = t * 2 + half
                            pe.wait_ge(s["f_ready"], done(g))
                            pe.wait_ge(s["z_ready"], before(g))
                            for k in range(HALF):
                                last = pe.matmul(ps[:, 4 + half, k * P:(k + 1) * P], f[half][:, k * P:(k + 1) * P], w[:, :], start=True, stop=True)
                            last.then_inc(s["mapped"], 1)


def add_features(c, h):
    nc = c.nc
    with ExitStack() as ctx:
        f = [ctx.enter_context(nc.sbuf_tensor(f"add_f{i}", [P, GN], F32)) for i in range(2)]
        ps = ctx.enter_context(nc.psum_tensor("add_ps", [P, 2, 512], F32))
        s = semaphores(nc, ctx, "add", "f_ready turned x_out")
        block = ctx.enter_context(nc.Block())

        @block.vector
        def _(dve):
            dve.sem_inc(s["x_out"], 2)
            with dve.Fori(0, c.GROUPS // 2) as it:
                for par in range(2):
                    g = it * 2 + par
                    dve.wait_ge(s["x_out"], before(g))
                    dve.tensor_tensor(f[par][:, :], h[0][:, ds(g * GN, GN)].bitcast(F32), h[1][:, ds(g * GN, GN)].bitcast(F32),
                                      ALU.add).then_inc(s["f_ready"], 1)
                for par in range(2):
                    g = it * 2 + par
                    dve.wait_ge(s["turned"], g + 1)
                    xt = c.x[:, ds(g * GN, GN)]
                    dve.tensor_tensor(xt, ps[:, par, :], xt, ALU.add).then_inc(s["x_out"], 1)

        @block.tensor
        def _(pe):
            with pe.Fori(0, c.GROUPS // 2) as it:
                for par in range(2):
                    g = it * 2 + par
                    pe.wait_ge(s["f_ready"], g + 1)
                    pe.wait_ge(s["x_out"], before(g))
                    for k in range(GT):
                        m = pe.transpose(ps[:, par, k * P:(k + 1) * P], f[par][:, k * P:(k + 1) * P], c.ident[:, :])
                    m.then_inc(s["turned"], 1)


def stage_lstm(c, h):
    nc = c.nc
    N, T = c.N, c.T
    KINDS = 4
    bih, bhh = c.ins["bih"], c.ins["bhh"]
    with ExitStack() as outer:
        bias = outer.enter_context(nc.sbuf_tensor("ls_bias", [P, 4 * KINDS], F32))
        other = outer.enter_context(nc.sbuf_tensor("ls_bias_other", [P, 4 * KINDS], F32))
        for p in range(1, 5):
            with ExitStack() as ctx:
                if p in (1, 2, 4):
                    W = min(GN, T // p // 2)
                    span, blocks, kept = W * p, T // p // W, W
                else:
                    kept = N // p
                    W = kept + kept % 2
                    span, blocks = N, c.B
                lstm_windows(c, ctx, h, p, W, kept, span, blocks, bias, other)


def lstm_windows(c, ctx, h, p, W, kept, span, blocks, bias, other):
    nc = c.nc
    KINDS = 4
    I, F, G, O = range(KINDS)
    name = f"l{p}"

    def sb(n, shape, dt=F32):
        return [ctx.enter_context(nc.sbuf_tensor(f"{name}_{n}{i}", shape, dt)) for i in range(2)]
    raw = sb("raw", [P, KINDS * P])
    w_hi = sb("w_hi", [P, KINDS * P], F32R)
    w_lo = sb("w_lo", [P, KINDS * P], F32R)
    gate = [sb(n, [P, W]) for n in ("gi", "gf", "gc", "go")]
    new, kept_c, cell, tc, state = (sb(n, [P, W]) for n in ("new", "kept", "cell", "tc", "state"))
    s_hi = sb("s_hi", [P, W], F32R)
    s_lo = sb("s_lo", [P, W], F32R)
    ps = ctx.enter_context(nc.psum_tensor(name + "_ps", [P, 8, 512], F32))
    names = "w_in b_in bias_ready whi_ready wlo_ready pe_held"
    pairs = "products gates new_ready kept_ready cell_ready tanh_ready state_ready hi_ready lo_ready"
    s = semaphores(nc, ctx, name, names)
    q = [semaphores(nc, ctx, f"{name}_{i}", pairs) for i in range(2)]
    block = ctx.enter_context(nc.Block())
    steps = [(k, [g for g in (I, G, F, O) if k or g != F]) for k in range(p)]
    before_step = [sum(len(gs) for _, gs in steps[:k]) for k in range(p)]
    per_block = sum(len(gs) for _, gs in steps)

    def node(v, j, k, n):
        return v[:, ds(j * span + k, n, step=p)] if p > 1 else v[:, ds(j * span, n)]

    @block.sync
    def _(sp):
        sp.dma_start(raw[0][:, :], c.ins["WihT"][p - 1]).then_inc(s["w_in"], 16)
        sp.dma_start(raw[1][:, :], c.ins["WhhT"][p - 1]).then_inc(s["w_in"], 16)
        if p == 1:
            sp.dma_start(bias[:, :], c.ins["bih"]).then_inc(s["b_in"], 16)
            sp.dma_start(other[:, :], c.ins["bhh"]).then_inc(s["b_in"], 16)
            sp.wait_ge(s["b_in"], 32)
        sp.wait_ge(s["w_in"], 32)

    @block.scalar
    def _(act):
        act.wait_ge(s["w_in"], 32)
        act.copy(w_hi[0][:, :], raw[0][:, :])
        act.copy(w_hi[1][:, :], raw[1][:, :]).then_inc(s["whi_ready"], 1)
        if p == 1:
            act.wait_ge(s["bias_ready"], 1)
        for par in range(2):
            act.sem_inc(q[par]["gates"], 1)
        with act.Fori(0, blocks // 2) as it:
            for k, gs in steps:
                for par in range(2):
                    z = q[par]
                    for n, g in enumerate(gs):
                        act.wait_ge(z["products"], it * per_block + before_step[k] + n + 1)
                        if n == 0:
                            act.wait_ge(z["lo_ready"], it * p + k + 1)
                        act.activation(gate[g][par][:, :], ps[:, par * KINDS + g, 0:W], ACT.Tanh if g == G else ACT.Sigmoid,
                                       bias=bias[:, (p - 1) * KINDS + g:(p - 1) * KINDS + g + 1]).then_inc(z["gates"], 1)
                for par in range(2):
                    z = q[par]
                    act.wait_ge(z["cell_ready"], it * p + k + 1)
                    act.activation(tc[par][:, :], cell[par][:, :], ACT.Tanh).then_inc(z["tanh_ready"], 1)

    @block.gpsimd
    def _(pool):
        if p > 1:
            with pool.Fori(0, blocks // 2) as it:
                for k, gs in steps[1:]:
                    for par in range(2):
                        z = q[par]
                        pool.wait_ge(z["gates"], it * per_block + before_step[k] + 4)
                        pool.tensor_tensor(kept_c[par][:, :], gate[F][par][:, :], cell[par][:, :], ALU.mult).then_inc(z["kept_ready"], 1)

    @block.vector
    def _(dve):
        if p == 1:
            dve.wait_ge(s["b_in"], 32)
            dve.tensor_tensor(bias[:, :], bias[:, :], other[:, :], ALU.add).then_inc(s["bias_ready"], 1)
        dve.wait_ge(s["whi_ready"], 1)
        dve.tensor_tensor(w_lo[0][:, :], raw[0][:, :], w_hi[0][:, :].bitcast(F32), ALU.subtract)
        dve.tensor_tensor(w_lo[1][:, :], raw[1][:, :], w_hi[1][:, :].bitcast(F32), ALU.subtract).then_inc(s["wlo_ready"], 1)
        for par in range(2):
            dve.sem_inc(q[par]["lo_ready"], 1)
        with dve.Fori(0, blocks // 2) as it:
            for k, gs in steps:
                for par in range(2):
                    z = q[par]
                    dve.wait_ge(z["gates"], it * per_block + before_step[k] + 3)
                    goal = new if k else cell
                    m = dve.tensor_tensor(goal[par][:, :], gate[I][par][:, :], gate[G][par][:, :], ALU.mult)
                    if k:
                        m.then_inc(z["new_ready"], 1)
                        dve.wait_ge(z["new_ready"], it * (p - 1) + k)
                        dve.wait_ge(z["kept_ready"], it * (p - 1) + k)
                        m = dve.tensor_tensor(cell[par][:, :], new[par][:, :], kept_c[par][:, :], ALU.add)
                    m.then_inc(z["cell_ready"], 1)
                for par in range(2):
                    z = q[par]
                    j = it * 2 + par
                    dve.wait_ge(z["tanh_ready"], it * p + k + 1)
                    dve.tensor_tensor(state[par][:, :], gate[O][par][:, :], tc[par][:, :], ALU.mult).then_inc(z["state_ready"], 1)
                    hi, lo = s_hi[par][:, 0:W], s_lo[par][:, 0:W]
                    n = W
                    if k == p - 1:
                        n = kept
                        hi, lo = node(h[0], j, k, n), node(h[1], j, k, n)
                    dve.wait_ge(z["state_ready"], it * p + k + 1)
                    dve.tensor_copy(hi, state[par][:, 0:n]).then_inc(z["hi_ready"], 1)
                    dve.wait_ge(z["hi_ready"], it * p + k + 1)
                    dve.tensor_tensor(lo, state[par][:, 0:n], hi.bitcast(F32), ALU.subtract).then_inc(z["lo_ready"], 1)

    @block.tensor
    def _(pe):
        pe.wait_ge(s["wlo_ready"], 1)
        with pe.Fori(0, blocks // 2) as it:
            for k, gs in steps:
                for par in range(2):
                    z = q[par]
                    j = it * 2 + par
                    moving = (node(h[0], j, k, W), node(h[1], j, k, W))
                    for n, g in enumerate(gs):
                        cs = slice(g * P, (g + 1) * P)
                        if n == 0:
                            pe.wait_ge(z["gates"], it * per_block + before_step[k] + 1)
                        for i, (w, x) in enumerate(passes((w_hi[0][:, cs], w_lo[0][:, cs]), moving)):
                            last = pe.matmul(ps[:, par * KINDS + g, 0:W], w, x, start=(i == 0), stop=(k == 0 and i == 2))
                        if k == 0:
                            last.then_inc(z["products"], 1)
                    if k:
                        pe.wait_ge(z["lo_ready"], it * p + k + 1)
                        for g in gs:
                            cs = slice(g * P, (g + 1) * P)
                            for i, (w, x) in enumerate(passes((w_hi[1][:, cs], w_lo[1][:, cs]), (s_hi[par][:, :], s_lo[par][:, :]))):
                                last = pe.matmul(ps[:, par * KINDS + g, 0:W], w, x, start=False, stop=(i == 2))
                            last.then_inc(z["products"], 1)


def stage_store(c):
    nc = c.nc
    with ExitStack() as ctx:
        s = semaphores(nc, ctx, "store", "out_done")
        block = ctx.enter_context(nc.Block())

        @block.sync
        def _(sp):
            n = c.T // 4
            for q in range(4):
                sp.dma_start(c.out[:, q * n:(q + 1) * n], c.x[:, q * n:(q + 1) * n]).then_inc(s["out_done"], 16)
            sp.wait_ge(s["out_done"], 64)


def build(nc, ins, out):
    RETIRED.clear()
    c = Core()
    c.nc, c.out = nc, out
    c.ins = ins
    c.T, c.N = ins["x"].shape[1], ins["adj"].shape[2]
    c.B = c.T // c.N
    c.TILES, c.GROUPS = c.T // P, c.T // GN
    with ExitStack() as ctx:
        c.x = ctx.enter_context(nc.sbuf_tensor("x_sb", [P, c.T], F32))
        c.ident = ctx.enter_context(nc.sbuf_tensor("ident", [P, P], F32))
        c.ones = ctx.enter_context(nc.sbuf_tensor("ones", [P, P], F32))
        c.mean = ctx.enter_context(nc.sbuf_tensor("row_mean", [P, c.TILES], F32))
        c.rstd = ctx.enter_context(nc.sbuf_tensor("row_rstd", [P, c.TILES], F32))
        stage_load(c)
        stage_row_stats(c, "norm0", False)
        stage_attention(c)
        stage_row_stats(c, "norm1", True)
        stage_experts(c, 0)
        stage_row_stats(c, "norm2", False)
        stage_graph_conv(c)
        stage_row_stats(c, "norm3", False)
        stage_experts(c, 1)
        stage_store(c)


def layouts(v):
    def node_tiles(a):
        return a.reshape(-1, P, a.shape[-1]).transpose(1, 0, 2)

    def rows_in_chunks(w):
        return w.reshape(w.shape[0], -1, P, w.shape[2]).transpose(0, 2, 1, 3)

    def columns(b):
        return b.reshape(-1, P).T

    B, N, D = v["x"].shape
    NT = N // P
    return {
        "x": node_tiles(v["x"].reshape(B * N, D)).reshape(P, B * N),
        "adj": node_tiles(v["adj"]),
        "adjT": v["adj"].reshape(NT, P, NT, P).transpose(0, 3, 2, 1),
        "L0_gnn_W": v["L0_gnn_W"], "L0_gnn_WT": v["L0_gnn_W"].T, "L0_gnn_a": columns(v["L0_gnn_a"].reshape(1, -1)),
        "L0_gamma": columns(v["L0_ffn_gamma"].reshape(1, -1)), "L0_beta": columns(v["L0_ffn_beta"].reshape(1, -1)),
        "L0_Wr": v["L0_ffn_Wr"], "L0_br": v["L0_ffn_br"].reshape(1, -1),
        "L0_W1": v["L0_ffn_W1"], "L0_b1": columns(v["L0_ffn_b1"]),
        "L0_W2": rows_in_chunks(v["L0_ffn_W2"]), "L0_b2": v["L0_ffn_b2"],
        "Wg0": v["L1_gnn_Wg0"], "bg0": v["L1_gnn_bg0"].reshape(1, -1),
        "Wg1": v["L1_gnn_Wg1"], "bg1": v["L1_gnn_bg1"].reshape(1, -1),
        "WihT": v["L1_gnn_Wih"].transpose(0, 2, 1), "WhhT": v["L1_gnn_Whh"].transpose(0, 2, 1),
        "bih": columns(v["L1_gnn_bih"]), "bhh": columns(v["L1_gnn_bhh"]),
        "L1_Wr": v["L1_ffn_Wg"].T, "L1_br": v["L1_ffn_bg"].reshape(1, -1),
        "L1_W1": v["L1_ffn_W1"].transpose(0, 2, 1), "L1_b1": columns(v["L1_ffn_b1"]),
        "L1_W2": rows_in_chunks(v["L1_ffn_W2"].transpose(0, 2, 1)), "L1_b2": v["L1_ffn_b2"],
    }


def kernel(**inputs):
    import numpy as np
    import concourse.bacc as bacc
    from concourse.bass_utils import run_bass_kernel_spmd

    nc = bacc.Bacc("TRN2", target_bir_lowering=False, num_devices=1)
    arrays, aps = {}, {}
    for name, value in layouts({n: np.asarray(a) for n, a in inputs.items()}).items():
        a = np.ascontiguousarray(value)
        arrays[f"in_{name}"] = a
        aps[name] = nc.dram_tensor(f"in_{name}", a.shape, mybir.dt.from_np(a.dtype), kind="ExternalInput").ap()
    out = nc.dram_tensor("out", arrays["in_x"].shape, F32, kind="ExternalOutput").ap()
    build(nc, aps, out)
    got = run_bass_kernel_spmd(nc, [arrays], core_ids=[0]).results[0]["out"]
    B, N, D = inputs["x"].shape
    return np.ascontiguousarray(got.reshape(P, -1, D).transpose(1, 0, 2)).reshape(B, N, D)
```

```python
from contextlib import ExitStack

import concourse.bass as bass
from concourse import mybir

P = 128
ALU = mybir.AluOpType
ACT = mybir.ActivationFunctionType
AX = mybir.AxisListType
F32 = mybir.dt.float32
F32R = mybir.dt.float32r
EPS = 1e-5
ALPHA = 0.2
MASKED = -1e30
GT = 4
GN = GT * P
RETIRED = []


def ds(at, size, step=1):
    return bass.ds(at, size) if step == 1 else bass.ds(at, size, step)


class Core:
    pass


def semaphores(nc, ctx, stage, names):
    made = {n: nc.alloc_semaphore(f"{stage}_{n}") for n in names.split()}
    ctx.callback(RETIRED.extend, made.values())
    return made


def recycle_semaphores(nc):
    with nc.Block() as block:
        @block.gpsimd
        def _(pool):
            for sem in RETIRED:
                pool.sem_clear(sem)
    for sem in RETIRED:
        nc.release_semaphore(sem)
    RETIRED.clear()


def passes(hi_lo_stationary, hi_lo_moving):
    (wh, wl), (mh, ml) = hi_lo_stationary, hi_lo_moving
    return ((wh, mh), (wh, ml), (wl, mh))


def before(n):
    return n + 1


def done(n, credits=2):
    return n + 1 + credits


NORM_SEMS = "xn_ready transposed"


def norm_buffers(nc, ctx, stage):
    return [ctx.enter_context(nc.sbuf_tensor(f"{stage}_xn{i}", [P, GN], F32)) for i in range(2)]


def normalise_group(dve, c, xn, s, g, par):
    dve.wait_ge(s["transposed"], before(g))
    for k in range(GT):
        last = dve.tensor_scalar(xn[par][:, k * P:(k + 1) * P], c.x[:, ds(g * GN + k * P, P)],
                                 c.mean[:, ds(g * GT + k, 1)], c.rstd[:, ds(g * GT + k, 1)], ALU.subtract, ALU.mult)
    last.then_inc(s["xn_ready"], 1)


def transpose_group(pe, c, xn, s, g, par, psum):
    pe.wait_ge(s["xn_ready"], g + 1)
    pe.wait_ge(s["hT_ready"], before(g))
    for k in range(GT):
        m = pe.transpose(psum[:, k * P:(k + 1) * P], xn[par][:, k * P:(k + 1) * P], c.ident[:, :])
    m.then_inc(s["transposed"], 1)


def stage_load(c):
    nc = c.nc
    with ExitStack() as ctx:
        s = semaphores(nc, ctx, "load", "zeroed x_in")
        block = ctx.enter_context(nc.Block())

        @block.sync
        def _(sp):
            n = c.T // 4
            for q in range(4):
                sp.dma_start(c.x[:, q * n:(q + 1) * n], c.ins["x"][:, q * n:(q + 1) * n]).then_inc(s["x_in"], 16)
            sp.wait_ge(s["x_in"], 64)

        @block.vector
        def _(dve):
            dve.memset(c.ones[:, :], 1.0)

        @block.gpsimd
        def _(pool):
            pool.memset(c.ident[:, :], 0.0).then_inc(s["zeroed"], 1)
            pool.wait_ge(s["zeroed"], 1)
            pool.affine_select(out=c.ident[:, :], in_=c.ident[:, :], compare_op=ALU.not_equal, fill=1.0,
                               base=0, pattern=[[-1, P]], channel_multiplier=1)


def stage_row_stats(c, stage, twice):
    nc = c.nc
    NT = c.TILES
    with ExitStack() as ctx:
        halves = ctx.enter_context(nc.sbuf_tensor(stage + "_halves", [P, NT, 6], F32))
        mean2, half, sq, m2, var, sd, v2 = (ctx.enter_context(nc.sbuf_tensor(f"{stage}_{n}", [P, NT], F32))
                                            for n in ("mean2", "half", "sq", "m2", "var", "sd", "v2"))
        s = semaphores(nc, ctx, stage, "stats step deviation")
        rounds = 2 if twice else 1
        block = ctx.enter_context(nc.Block())

        @block.vector
        def _(dve):
            with dve.Fori(0, NT // 4) as it:
                for k in range(4):
                    last = dve.bn_stats(halves[:, :, :].rearrange("p t s -> p (t s)")[:, ds((it * 4 + k) * 6, 6)],
                                        c.x[:, ds((it * 4 + k) * P, P)])
                last.then_inc(s["stats"], 1)
            dve.wait_ge(s["stats"], NT // 4)
            me, mo, qe, qo = (halves[:, :, j] for j in (1, 4, 2, 5))
            dve.tensor_tensor(mean2[:, :], me, mo, ALU.add)
            dve.tensor_tensor(half[:, :], me, mo, ALU.subtract)
            dve.tensor_tensor(m2[:, :], qe, qo, ALU.add).then_inc(s["step"], 1)
            dve.wait_ge(s["step"], 1)
            dve.tensor_scalar(c.mean[:, :], mean2[:, :], 0.5, None, ALU.mult)
            dve.scalar_tensor_tensor(sq[:, :], half[:, :], 0.25, half[:, :], ALU.mult, ALU.mult).then_inc(s["step"], 1)
            dve.wait_ge(s["step"], 2)
            dve.scalar_tensor_tensor(var[:, :], m2[:, :], 1.0 / P, sq[:, :], ALU.mult, ALU.add).then_inc(s["step"], 1)
            dve.wait_ge(s["step"], 3)
            dve.tensor_scalar(v2[:, :], var[:, :], EPS, None, ALU.add).then_inc(s["step"], 1)
            dve.wait_ge(s["deviation"], 1)
            dve.reciprocal(c.rstd[:, :], sd[:, :]).then_inc(s["step"], 1)
            if twice:
                dve.wait_ge(s["step"], 5)
                dve.tensor_tensor(sq[:, :], var[:, :], c.rstd[:, :], ALU.mult).then_inc(s["step"], 1)
                dve.wait_ge(s["step"], 6)
                dve.tensor_tensor(m2[:, :], sq[:, :], c.rstd[:, :], ALU.mult).then_inc(s["step"], 1)
                dve.wait_ge(s["step"], 7)
                dve.tensor_scalar(v2[:, :], m2[:, :], EPS, None, ALU.add).then_inc(s["step"], 1)
                dve.wait_ge(s["deviation"], 2)
                dve.reciprocal(half[:, :], sd[:, :]).then_inc(s["step"], 1)
                dve.wait_ge(s["step"], 9)
                dve.tensor_tensor(c.rstd[:, :], c.rstd[:, :], half[:, :], ALU.mult)

        @block.scalar
        def _(act):
            for n in range(rounds):
                act.wait_ge(s["step"], (4, 8)[n])
                act.activation(sd[:, :], v2[:, :], ACT.Sqrt).then_inc(s["deviation"], 1)


def stage_attention(c):
    nc = c.nc
    N, B, NT = c.N, c.B, c.N // P
    with ExitStack() as outer:
        def sbo(name, shape, dt=F32):
            return outer.enter_context(nc.sbuf_tensor("att_" + name, shape, dt))
        Wh = sbo("Wh", [P, c.T])
        s2row = sbo("s2row", [P, c.T])
        s1col = sbo("s1col", [P, c.TILES])
        s1col8 = sbo("s1col8", [P, c.TILES])
        mask = sbo("mask", [P, NT, N])

        with ExitStack() as ctx:
            def sb(name, shape, dt=F32):
                return ctx.enter_context(nc.sbuf_tensor("prj_" + name, shape, dt))
            xn = norm_buffers(nc, ctx, "prj")
            W = sb("W", [P, P])
            WT = sb("WT", [P, P])
            a12 = sb("a12", [P, 2])
            Wa = sb("Wa", [P, 2])
            Wa2rep = sb("Wa2rep", [P, P])
            hT = [sb(f"hT{i}", [P, GN]) for i in range(2)]
            ps = ctx.enter_context(nc.psum_tensor("prj_ps", [P, 8, 512], F32))
            psT, psW, psR, psS = (lambda i: ps[:, i, :]), (lambda i: ps[:, 2 + i, :]), (lambda i: ps[:, 4 + i, :]), (lambda i: ps[:, 6 + i, 0:8])
            s = semaphores(nc, ctx, "prj", NORM_SEMS + " w_in adj_in wa wa_sb wrep "
                           "hT_ready projected Wh_out row_out s1_out")
            block = ctx.enter_context(nc.Block())

            @block.sync
            def _(sp):
                sp.dma_start(W[:, :], c.ins["L0_gnn_W"]).then_inc(s["w_in"], 16)
                sp.dma_start(WT[:, :], c.ins["L0_gnn_WT"]).then_inc(s["w_in"], 16)
                sp.dma_start(a12[:, :], c.ins["L0_gnn_a"]).then_inc(s["w_in"], 16)
                sp.dma_start(mask[:, :, :], c.ins["adj"]).then_inc(s["adj_in"], 16)

            @block.gpsimd
            def _(pool):
                pool.wait_ge(s["adj_in"], 16)
                for t in range(NT):
                    pool.tensor_scalar(mask[:, t, :], mask[:, t, :], 0.0, MASKED, ALU.is_equal, ALU.mult)

            @block.tensor
            def _(pe):
                pe.wait_ge(s["w_in"], 48)
                pe.matmul(ps[:, 1, 0:2], WT[:, :], a12[:, :], start=True, stop=True).then_inc(s["wa"], 1)
                pe.wait_ge(s["wrep"], 1)
                pe.sem_inc(s["transposed"], 2)
                with pe.Fori(0, c.GROUPS // 2) as it:
                    for par in range(2):
                        transpose_group(pe, c, xn, s, it * 2 + par, par, psT(par))
                    for par in range(2):
                        g = it * 2 + par
                        pe.wait_ge(s["hT_ready"], done(g))
                        pe.wait_ge(s["Wh_out"], before(g))
                        pe.wait_ge(s["row_out"], before(g))
                        pe.wait_ge(s["s1_out"], before(g))
                        for k in range(GT):
                            pe.matmul(psW(par)[:, k * P:(k + 1) * P], hT[par][:, k * P:(k + 1) * P], W[:, :], start=True, stop=True)
                        for k in range(GT):
                            pe.matmul(psS(par)[:, 2 * k:2 * k + 2], hT[par][:, k * P:(k + 1) * P], Wa[:, :], start=True, stop=True)
                        pe.matmul(psR(par), Wa2rep[:, :], hT[par][:, :], start=True, stop=True).then_inc(s["projected"], 1)

            @block.scalar
            def _(act):
                act.sem_inc(s["hT_ready"], 2)
                act.sem_inc(s["row_out"], 2)
                with act.Fori(0, c.GROUPS // 2) as it:
                    for par in range(2):
                        g = it * 2 + par
                        act.wait_ge(s["transposed"], done(g))
                        act.wait_ge(s["row_out"], before(g))
                        act.copy(hT[par][:, :], psT(par)).then_inc(s["hT_ready"], 1)
                    for par in range(2):
                        g = it * 2 + par
                        act.wait_ge(s["projected"], g + 1)
                        act.copy(s2row[:, ds(g * GN, GN)], psR(par)).then_inc(s["row_out"], 1)

            @block.vector
            def _(dve):
                dve.sem_inc(s["Wh_out"], 2)
                dve.sem_inc(s["s1_out"], 2)
                dve.wait_ge(s["wa"], 1)
                dve.tensor_copy(Wa[:, :], ps[:, 1, 0:2]).then_inc(s["wa_sb"], 1)
                dve.wait_ge(s["wa_sb"], 1)
                dve.tensor_scalar(Wa2rep[:, :], c.ones[:, :], Wa[:, 1:2], None, ALU.mult).then_inc(s["wrep"], 1)
                with dve.Fori(0, c.GROUPS // 2) as it:
                    for par in range(2):
                        normalise_group(dve, c, xn, s, it * 2 + par, par)
                    for par in range(2):
                        g = it * 2 + par
                        dve.wait_ge(s["projected"], g + 1)
                        dve.tensor_copy(Wh[:, ds(g * GN, GN)], psW(par)).then_inc(s["Wh_out"], 1)
                        dve.tensor_copy(s1col[:, ds(g * GT, GT)], psS(par).rearrange("p (k c) -> p k c", c=2)[:, :, 0]).then_inc(s["s1_out"], 1)
                dve.wait_ge(s["s1_out"], done(c.GROUPS - 1))
                dve.tensor_scalar(s1col8[:, :], s1col[:, :], 1 - ALPHA, None, ALU.mult)

        with ExitStack() as ctx:
            def sb(name, shape, dt=F32):
                return [ctx.enter_context(nc.sbuf_tensor(f"att_{name}{i}", shape, dt)) for i in range(2)]
            q = sb("q", [P, N])
            e = sb("e", [P, N])
            p = sb("p", [P, N])
            pT = sb("pT", [P, N])
            M, m8, m2, bias, den, rden = (sb(n, [P, 1]) for n in ("M", "m8", "m2", "bias", "den", "rden"))
            ps = ctx.enter_context(nc.psum_tensor("att_ps", [P, 8, 512], F32))
            s = semaphores(nc, ctx, "att", "q_ready max_ready small bias_ready relu_ready e_ready p_ready "
                           "transposed pT_lo pT_hi attended rden_ready x_out")
            H2 = N // 2
            block = ctx.enter_context(nc.Block())

            @block.gpsimd
            def _(pool):
                pool.sem_inc(s["q_ready"], 2)
                with pool.Fori(0, c.TILES // 2) as it:
                    for par in range(2):
                        i = it * 2 + par
                        pool.wait_ge(s["e_ready"], before(i))
                        pool.tensor_tensor(q[par][:, :], s2row[:, ds(it // (NT // 2) * N, N)],
                                           mask[:, :, :].rearrange("p t n -> p (t n)")[:, ds((it * 2 + par) % NT * N, N)],
                                           ALU.add).then_inc(s["q_ready"], 1)

            @block.vector
            def _(dve):
                for sem in (s["e_ready"], s["bias_ready"], s["pT_hi"], s["x_out"]):
                    dve.sem_inc(sem, 2)
                with dve.Fori(0, c.TILES // 2) as it:
                    for par in range(2):
                        i = it * 2 + par
                        dve.wait_ge(s["q_ready"], done(i))
                        dve.wait_ge(s["p_ready"], before(i))
                        dve.tensor_reduce(M[par][:, :], q[par][:, :], AX.X, ALU.max).then_inc(s["max_ready"], 1)
                        dve.wait_ge(s["max_ready"], i + 1)
                        dve.tensor_scalar(m8[par][:, :], M[par][:, :], s1col[:, ds(i, 1)], 0.0, ALU.add, ALU.max).then_inc(s["small"], 1)
                        dve.tensor_scalar(m2[par][:, :], M[par][:, :], -ALPHA, None, ALU.mult).then_inc(s["small"], 1)
                        dve.wait_ge(s["small"], i * 2 + 2)
                        dve.scalar_tensor_tensor(bias[par][:, :], m8[par][:, :], -(1 - ALPHA), m2[par][:, :],
                                                 ALU.mult, ALU.add).then_inc(s["bias_ready"], 1)
                    for par in range(2):
                        i = it * 2 + par
                        dve.wait_ge(s["relu_ready"], i + 1)
                        dve.scalar_tensor_tensor(e[par][:, :], q[par][:, :], ALPHA, e[par][:, :], ALU.mult, ALU.add).then_inc(s["e_ready"], 1)
                    for par in range(2):
                        i = it * 2 + par
                        dve.wait_ge(s["transposed"], done(i))
                        dve.wait_ge(s["attended"], before(i))
                        dve.tensor_copy(pT[par][:, H2:], ps[:, 2 * par + 1, :]).then_inc(s["pT_hi"], 1)
                    for par in range(2):
                        i = it * 2 + par
                        dve.wait_ge(s["p_ready"], done(i))
                        dve.reciprocal(rden[par][:, :], den[par][:, :]).then_inc(s["rden_ready"], 1)
                        dve.wait_ge(s["rden_ready"], i + 1)
                        dve.wait_ge(s["attended"], done(i))
                        xt = c.x[:, ds(i * P, P)]
                        dve.scalar_tensor_tensor(xt, ps[:, 4 + par, 0:P], rden[par][:, 0:1], xt, ALU.mult, ALU.add).then_inc(s["x_out"], 1)

            @block.scalar
            def _(act):
                act.sem_inc(s["p_ready"], 2)
                act.sem_inc(s["pT_lo"], 2)
                with act.Fori(0, c.TILES // 2) as it:
                    for par in range(2):
                        i = it * 2 + par
                        act.wait_ge(s["q_ready"], done(i))
                        act.wait_ge(s["p_ready"], before(i))
                        act.activation(e[par][:, :], q[par][:, :], ACT.Relu, bias=s1col8[:, ds(i, 1)], scale=1 - ALPHA).then_inc(s["relu_ready"], 1)
                    for par in range(2):
                        i = it * 2 + par
                        act.wait_ge(s["e_ready"], done(i))
                        act.wait_ge(s["bias_ready"], done(i))
                        act.wait_ge(s["transposed"], before(i))
                        act.wait_ge(s["x_out"], before(i))
                        act.activation(p[par][:, :], e[par][:, :], ACT.Exp, bias=bias[par][:, 0:1], accum_out=den[par][:, 0:1]).then_inc(s["p_ready"], 1)
                    for par in range(2):
                        i = it * 2 + par
                        act.wait_ge(s["transposed"], done(i))
                        act.wait_ge(s["attended"], before(i))
                        act.copy(pT[par][:, 0:H2], ps[:, 2 * par, :]).then_inc(s["pT_lo"], 1)

            @block.tensor
            def _(pe):
                pe.sem_inc(s["transposed"], 2)
                pe.sem_inc(s["attended"], 2)
                with pe.Fori(0, c.TILES // 2) as it:
                    for par in range(2):
                        i = it * 2 + par
                        pe.wait_ge(s["p_ready"], done(i))
                        pe.wait_ge(s["pT_lo"], before(i))
                        pe.wait_ge(s["pT_hi"], before(i))
                        for j in range(NT):
                            m = pe.transpose(ps[:, 2 * par + j // 4, j % 4 * P:(j % 4 + 1) * P], p[par][:, j * P:(j + 1) * P], c.ident[:, :])
                        m.then_inc(s["transposed"], 1)
                    for par in range(2):
                        i = it * 2 + par
                        pe.wait_ge(s["pT_lo"], done(i))
                        pe.wait_ge(s["pT_hi"], done(i))
                        pe.wait_ge(s["x_out"], before(i))
                        for j in range(NT):
                            m = pe.matmul(ps[:, 4 + par, 0:P], pT[par][:, j * P:(j + 1) * P],
                                          Wh[:, ds((it // (NT // 2) * NT + j) * P, P)], start=(j == 0), stop=(j == NT - 1))
                        m.then_inc(s["attended"], 1)


def stage_turn(c, name):
    nc = c.nc
    with ExitStack() as ctx:
        xs = [ctx.enter_context(nc.sbuf_tensor(f"{name}_xs{i}", [P, GN], F32)) for i in range(2)]
        ps = ctx.enter_context(nc.psum_tensor(name + "_ps", [P, 2, 512], F32))
        s = semaphores(nc, ctx, name, "xs_ready turned x_out")
        block = ctx.enter_context(nc.Block())

        @block.scalar
        def _(act):
            with act.Fori(0, c.GROUPS // 2) as it:
                for par in range(2):
                    g = it * 2 + par
                    act.wait_ge(s["x_out"], before(g))
                    act.copy(xs[par][:, :], c.x[:, ds(g * GN, GN)]).then_inc(s["xs_ready"], 1)

        @block.tensor
        def _(pe):
            with pe.Fori(0, c.GROUPS // 2) as it:
                for par in range(2):
                    g = it * 2 + par
                    pe.wait_ge(s["xs_ready"], g + 1)
                    pe.wait_ge(s["x_out"], before(g))
                    for k in range(GT):
                        m = pe.transpose(ps[:, par, k * P:(k + 1) * P], xs[par][:, k * P:(k + 1) * P], c.ident[:, :])
                    m.then_inc(s["turned"], 1)

        @block.vector
        def _(dve):
            dve.sem_inc(s["x_out"], 2)
            with dve.Fori(0, c.GROUPS // 2) as it:
                for par in range(2):
                    g = it * 2 + par
                    dve.wait_ge(s["turned"], g + 1)
                    dve.tensor_copy(c.x[:, ds(g * GN, GN)], ps[:, par, :]).then_inc(s["x_out"], 1)


def stage_experts(c, layer):
    nc = c.nc
    L = f"L{layer}_"
    W1, b1, W2, b2, Wr, br = (c.ins[L + n] for n in ("W1", "b1", "W2", "b2", "Wr", "br"))
    E, _, H = W1.shape
    HC = H // P
    act_fn = (ACT.Gelu, ACT.Relu)[layer]
    affine = layer == 0
    T, TILES, GROUPS = c.T, c.TILES, c.GROUPS
    with ExitStack() as outer:
        def sbo(name, shape, dt=F32):
            return outer.enter_context(nc.sbuf_tensor(L + name, shape, dt))
        h_hi = sbo("h_hi", [P, T], F32R)
        h_lo = sbo("h_lo", [P, T], F32R)
        scores = sbo("scores", [P, TILES, E])
        weight = sbo("weight", [P, TILES, E])
        b1col = sbo("b1col", [P, E * HC])
        b2col = sbo("b2col", [P, E])
        LOW = 32
        wrow = sbo("wrow", [LOW + E, T], F32R)

        with ExitStack() as ctx:
            def sb(name, shape, dt=F32):
                return ctx.enter_context(nc.sbuf_tensor(L + name, shape, dt))
            xn = norm_buffers(nc, ctx, L + "rt")
            h = [sb(f"h{i}", [P, GN]) for i in range(2)]
            wr = sb("wr", [P, E])
            br4 = sb("br4", [P, GT, E])
            gb = sb("gb", [P, 2])
            xs = [sb(f"xs{i}", [P, GN]) for i in range(2)]
            ps = ctx.enter_context(nc.psum_tensor(L + "rt_ps", [P, 6, 512], F32))
            s = semaphores(nc, ctx, L + "rt", NORM_SEMS + " w_in hT_ready hi_ready lo_ready routed scores_out xs_ready x_turned x_out")
            block = ctx.enter_context(nc.Block())

            @block.sync
            def _(sp):
                sp.dma_start(wr[:, :], Wr).then_inc(s["w_in"], 16)
                sp.dma_start(b1col[:, :], b1).then_inc(s["w_in"], 16)
                sp.dma_start(b2col[:, :], b2).then_inc(s["w_in"], 16)
                for k in range(GT):
                    sp.dma_start(br4[:, k, :], br.broadcast_to([P, E])).then_inc(s["w_in"], 16)
                if affine:
                    sp.dma_start(gb[:, 0:1], c.ins["L0_gamma"]).then_inc(s["w_in"], 16)
                    sp.dma_start(gb[:, 1:2], c.ins["L0_beta"]).then_inc(s["w_in"], 16)
                sp.wait_ge(s["w_in"], (3 + GT + (2 if affine else 0)) * 16)

            loads = (3 + GT + (2 if affine else 0)) * 16

            @block.vector
            def _(dve):
                dve.sem_inc(s["lo_ready"], 2)
                dve.sem_inc(s["scores_out"], 2)
                dve.wait_ge(s["w_in"], loads)
                with dve.Fori(0, GROUPS // 2) as it:
                    for par in range(2):
                        normalise_group(dve, c, xn, s, it * 2 + par, par)
                    for par in range(2):
                        g = it * 2 + par
                        dve.wait_ge(s["hT_ready"], done(g))
                        dve.tensor_copy(h_hi[:, ds(g * GN, GN)], h[par][:, :]).then_inc(s["hi_ready"], 1)
                        dve.wait_ge(s["hi_ready"], g + 1)
                        dve.tensor_tensor(h_lo[:, ds(g * GN, GN)], h[par][:, :], h_hi[:, ds(g * GN, GN)].bitcast(F32),
                                          ALU.subtract).then_inc(s["lo_ready"], 1)
                        dve.wait_ge(s["routed"], g + 1)
                        dve.tensor_tensor(scores[:, :, :].rearrange("p t e -> p (t e)")[:, ds(g * GT * E, GT * E)],
                                          ps[:, 2 + par, 0:GT * E], br4[:, :, :].rearrange("p t e -> p (t e)"),
                                          ALU.add).then_inc(s["scores_out"], 1)

            @block.scalar
            def _(act):
                act.sem_inc(s["hT_ready"], 2)
                act.sem_inc(s["x_out"], 2)
                act.wait_ge(s["w_in"], loads)
                with act.Fori(0, GROUPS // 2) as it:
                    for par in range(2):
                        g = it * 2 + par
                        act.wait_ge(s["transposed"], done(g))
                        act.wait_ge(s["lo_ready"], before(g))
                        act.wait_ge(s["scores_out"], before(g))
                        if affine:
                            act.activation(h[par][:, :], ps[:, par, :], ACT.Identity, bias=gb[:, 1:2], scale=gb[:, 0:1]).then_inc(s["hT_ready"], 1)
                        else:
                            act.copy(h[par][:, :], ps[:, par, :]).then_inc(s["hT_ready"], 1)
                    for par in range(2):
                        g = it * 2 + par
                        act.wait_ge(s["x_turned"], g + 1)
                        act.copy(c.x[:, ds(g * GN, GN)], ps[:, 4 + par, :]).then_inc(s["x_out"], 1)

            @block.gpsimd
            def _(pool):
                with pool.Fori(0, GROUPS // 2) as it:
                    for par in range(2):
                        g = it * 2 + par
                        pool.wait_ge(s["x_out"], before(g))
                        pool.tensor_copy(xs[par][:, :], c.x[:, ds(g * GN, GN)]).then_inc(s["xs_ready"], 1)

            @block.tensor
            def _(pe):
                pe.sem_inc(s["transposed"], 2)
                pe.wait_ge(s["w_in"], loads)
                with pe.Fori(0, GROUPS // 2) as it:
                    for par in range(2):
                        transpose_group(pe, c, xn, s, it * 2 + par, par, ps[:, par, :])
                    for par in range(2):
                        g = it * 2 + par
                        pe.wait_ge(s["hT_ready"], done(g))
                        pe.wait_ge(s["scores_out"], before(g))
                        for k in range(GT):
                            m = pe.matmul(ps[:, 2 + par, k * E:(k + 1) * E], h[par][:, k * P:(k + 1) * P], wr[:, :], start=True, stop=True)
                        m.then_inc(s["routed"], 1)
                        pe.wait_ge(s["xs_ready"], g + 1)
                        pe.wait_ge(s["x_out"], before(g))
                        for k in range(GT):
                            m = pe.transpose(ps[:, 4 + par, k * P:(k + 1) * P], xs[par][:, k * P:(k + 1) * P], c.ident[:, :])
                        m.then_inc(s["x_turned"], 1)

        with ExitStack() as ctx:
            def sb(name, shape, dt=F32):
                return ctx.enter_context(nc.sbuf_tensor(L + name, shape, dt))
            rank = sb("rank", [P, TILES, E])
            eq, seen, first, second, rest = (sb(n, [P, TILES, E]) for n in ("eq", "seen", "first", "second", "rest"))
            top1, top2, at1, at2, gap, ex, den, w1, w2 = (sb(n, [P, TILES]) for n in ("top1", "top2", "at1", "at2", "gap", "ex", "den", "w1", "w2"))
            wcopy = [sb(f"wcopy{i}", [P, GT * E]) for i in range(2)]
            ps = ctx.enter_context(nc.psum_tensor(L + "gate_ps", [P, 2, 512], F32))
            s = semaphores(nc, ctx, L + "gate", "rank_ready zeroed step exp_done weight_ready w_copied w_turned row_hi row_lo")
            block = ctx.enter_context(nc.Block())

            def each(a):
                return a[:, :].unsqueeze(2).broadcast_to([P, TILES, E])

            @block.gpsimd
            def _(pool):
                for e in range(E):
                    last = pool.memset(rank[:, :, e], float(E - e))
                last.then_inc(s["rank_ready"], 1)
                pool.memset(wrow[:, :].bitcast(F32), 0.0).then_inc(s["zeroed"], 1)

            @block.vector
            def _(dve):
                n = [0]

                def step(instruction):
                    n[0] += 1
                    instruction.then_inc(s["step"], 1)
                    dve.wait_ge(s["step"], n[0])

                def pick(values, top, at, chosen):
                    step(dve.tensor_reduce(top[:, :], values[:, :, :], AX.X, ALU.max))
                    step(dve.tensor_tensor(eq[:, :, :], values[:, :, :], each(top), ALU.is_equal))
                    step(dve.tensor_tensor(seen[:, :, :], eq[:, :, :], rank[:, :, :], ALU.mult))
                    step(dve.tensor_reduce(at[:, :], seen[:, :, :], AX.X, ALU.max))
                    step(dve.tensor_tensor(chosen[:, :, :], rank[:, :, :], each(at), ALU.is_equal))

                dve.sem_inc(s["row_lo"], 2)
                dve.wait_ge(s["rank_ready"], 1)
                pick(scores, top1, at1, first)
                step(dve.scalar_tensor_tensor(rest[:, :, :], first[:, :, :], MASKED, scores[:, :, :], ALU.mult, ALU.add))
                pick(rest, top2, at2, second)
                step(dve.tensor_tensor(gap[:, :], top2[:, :], top1[:, :], ALU.subtract))
                dve.wait_ge(s["exp_done"], 1)
                step(dve.tensor_scalar(den[:, :], ex[:, :], 1.0, None, ALU.add))
                step(dve.reciprocal(w1[:, :], den[:, :]))
                step(dve.tensor_tensor(w2[:, :], ex[:, :], w1[:, :], ALU.mult))
                step(dve.tensor_tensor(eq[:, :, :], first[:, :, :], each(w1), ALU.mult))
                step(dve.tensor_tensor(seen[:, :, :], second[:, :, :], each(w2), ALU.mult))
                dve.tensor_tensor(weight[:, :, :], eq[:, :, :], seen[:, :, :], ALU.add).then_inc(s["weight_ready"], 1)
                with dve.Fori(0, GROUPS // 2) as it:
                    for par in range(2):
                        g = it * 2 + par
                        dve.wait_ge(s["row_hi"], g + 1)
                        dve.tensor_tensor(wrow[LOW:LOW + E, ds(g * GN, GN)], ps[0:E, par, :], wrow[0:E, ds(g * GN, GN)].bitcast(F32),
                                          ALU.subtract).then_inc(s["row_lo"], 1)

            @block.scalar
            def _(act):
                act.wait_ge(s["step"], 12)
                act.activation(ex[:, :], gap[:, :], ACT.Exp).then_inc(s["exp_done"], 1)
                act.wait_ge(s["weight_ready"], 1)
                act.wait_ge(s["zeroed"], 1)
                with act.Fori(0, GROUPS // 2) as it:
                    for par in range(2):
                        g = it * 2 + par
                        act.wait_ge(s["row_lo"], before(g))
                        act.copy(wcopy[par][:, :], weight[:, :, :].rearrange("p t e -> p (t e)")[:, ds(g * GT * E, GT * E)]).then_inc(s["w_copied"], 1)
                    for par in range(2):
                        g = it * 2 + par
                        act.wait_ge(s["w_turned"], g + 1)
                        act.copy(wrow[0:E, ds(g * GN, GN)], ps[0:E, par, :]).then_inc(s["row_hi"], 1)

            @block.tensor
            def _(pe):
                with pe.Fori(0, GROUPS // 2) as it:
                    for par in range(2):
                        g = it * 2 + par
                        pe.wait_ge(s["w_copied"], g + 1)
                        pe.wait_ge(s["row_lo"], before(g))
                        for k in range(GT):
                            m = pe.transpose(ps[0:E, par, k * P:(k + 1) * P], wcopy[par][:, k * E:(k + 1) * E], c.ident[:, :])
                        m.then_inc(s["w_turned"], 1)

        with ExitStack() as ctx:
            def sb(name, shape, dt=F32, n=2):
                return [ctx.enter_context(nc.sbuf_tensor(f"{L}{name}{i}", shape, dt)) for i in range(n)]
            UB = 4
            raw1 = sb("raw1", [P, H])
            raw2 = sb("raw2", [P, HC * P])
            w1_hi, w1_lo, w2_hi, w2_lo = (sb(n, [P, H], F32R) for n in ("w1_hi", "w1_lo", "w2_hi", "w2_lo"))
            b1e = sb("b1e", [P, HC])
            u = sb("u", [P, GN], n=UB)
            u_hi = sb("u_hi", [P, HC, GN], F32R)
            u_lo = sb("u_lo", [P, HC, GN], F32R)
            wb = sb("wb", [P, GN])
            yw = sb("yw", [P, GN])
            onehot = ctx.enter_context(nc.sbuf_tensor(L + "onehot", [LOW + E, E], F32))
            pick_e = sb("pick_e", [LOW + E, P], F32R)
            ps = ctx.enter_context(nc.psum_tensor(L + "ex_ps", [P, 8, 512], F32))
            s = semaphores(nc, ctx, L + "ex", "w_in0 w_in1 b1_ready whi_ready wlo_ready up u_ready uhi_ready ulo_ready down spread wb_ready yw_ready x_out pe_held onehot_ready")
            w_in = (s["w_in0"], s["w_in1"])
            block = ctx.enter_context(nc.Block())

            def slot(n, hc):
                return (n % 2 * HC + hc) % UB

            @block.sync
            def _(sp):
                def load(e, ew):
                    sp.wait_ge(s["wlo_ready"], before(e))
                    sp.dma_start(raw1[ew][:, :], W1.rearrange("e d h -> (e d) h")[ds(e % E * P, P), :]).then_inc(w_in[ew], 16)
                    sp.dma_start(raw2[ew][:, :], W2.rearrange("e p c d -> (e p) (c d)")[ds(e % E * P, P), :]).then_inc(w_in[ew], 16)

                with sp.Fori(0, E // 2) as ep:
                    for ew in range(2):
                        load(ep * 2 + ew, ew)
                load(E, 0)
                sp.wait_ge(s["w_in0"], (E // 2 + 1) * 32)
                sp.wait_ge(s["w_in1"], E // 2 * 32)

            @block.scalar
            def _(act):
                def split_weights(e, ew, turn):
                    act.wait_ge(w_in[ew], turn * 32 + 32)
                    act.copy(b1e[ew][:, :], b1col[:, ds(e % E * HC, HC)]).then_inc(s["b1_ready"], 1)
                    act.copy(pick_e[ew][:, :], onehot[:, ds(e % E, 1)].broadcast_to([LOW + E, P]))
                    act.copy(w1_hi[ew][:, :], raw1[ew][:, :])
                    act.copy(w2_hi[ew][:, :], raw2[ew][:, :]).then_inc(s["whi_ready"], 1)

                def activate(e, ew, n, par):
                    g = e * GROUPS + n
                    act.wait_ge(s["down"], before(g))
                    for hc in range(HC):
                        v, j = g * HC + hc, slot(par, hc)
                        act.wait_ge(s["up"], v + 1)
                        act.wait_ge(s["ulo_ready"], before(v))
                        last = act.activation(u[j][:, :], ps[:, j, :], act_fn, bias=b1e[ew][:, hc:hc + 1])
                        if hc % 2 == 0:
                            last = act.activation(u_hi[par][:, hc, :], ps[:, j, :], act_fn, bias=b1e[ew][:, hc:hc + 1])
                        last.then_inc(s["u_ready"], 1)
                    act.wait_ge(s["spread"], g + 1)
                    act.wait_ge(s["yw_ready"], before(g))
                    act.copy(wb[par][:, :], ps[:, UB + 2 + par, :]).then_inc(s["wb_ready"], 1)

                act.sem_inc(s["whi_ready"], 2)
                act.sem_inc(s["u_ready"], UB)
                act.sem_inc(s["wb_ready"], 2)
                act.wait_ge(s["onehot_ready"], 1)
                split_weights(0, 0, 0)
                with act.Fori(0, E // 2) as ep:
                    for ew in range(2):
                        e = ep * 2 + ew
                        act.wait_ge(s["b1_ready"], e + 1)
                        for n in range(2):
                            activate(e, ew, n, n)
                        act.wait_ge(s["down"], done(e * GROUPS - 1))
                        split_weights(e + 1, 1 - ew, ep + ew)
                        with act.Fori(1, GROUPS // 2) as it:
                            for par in range(2):
                                activate(e, ew, it * 2 + par, par)

            @block.vector
            def _(dve):
                def split_weights(e, ew):
                    dve.wait_ge(s["whi_ready"], done(e))
                    dve.tensor_tensor(w1_lo[ew][:, :], raw1[ew][:, :], w1_hi[ew][:, :].bitcast(F32), ALU.subtract)
                    dve.tensor_tensor(w2_lo[ew][:, :], raw2[ew][:, :], w2_hi[ew][:, :].bitcast(F32), ALU.subtract).then_inc(s["wlo_ready"], 1)

                def split(e, n, par):
                    g = e * GROUPS + n
                    for hc in range(HC):
                        v, j = g * HC + hc, slot(par, hc)
                        dve.wait_ge(s["u_ready"], done(v, UB))
                        if hc % 2:
                            dve.tensor_copy(u_hi[par][:, hc, :], u[j][:, :]).then_inc(s["uhi_ready"], 1)
                            dve.wait_ge(s["uhi_ready"], g * (HC // 2) + hc // 2 + 1)
                        dve.tensor_tensor(u_lo[par][:, hc, :], u[j][:, :], u_hi[par][:, hc, :].bitcast(F32),
                                          ALU.subtract).then_inc(s["ulo_ready"], 1)

                def add(e, n, par):
                    g = e * GROUPS + n
                    dve.wait_ge(s["down"], done(g))
                    dve.wait_ge(s["wb_ready"], done(g))
                    dve.wait_ge(s["x_out"], before(g))
                    dve.scalar_tensor_tensor(yw[par][:, :], ps[:, UB + par, :], b2col[:, ds(e, 1)],
                                             wb[par][:, :], ALU.add, ALU.mult).then_inc(s["yw_ready"], 1)

                def pair(ep, first):
                    for ew in range(2):
                        e = ep * 2 + ew
                        for n in range(2):
                            if not (first and ew == 0):
                                add(e - 1, GROUPS - 2 + n, n)
                            split(e, n, n)
                        split_weights(e + 1, 1 - ew)
                        with dve.Fori(1, GROUPS // 2) as it:
                            for par in range(2):
                                add(e, it * 2 + par - 2, par)
                                split(e, it * 2 + par, par)

                dve.sem_inc(s["wlo_ready"], 2)
                dve.sem_inc(s["ulo_ready"], UB)
                dve.sem_inc(s["yw_ready"], 2)
                split_weights(0, 0)
                pair(0, True)
                with dve.Fori(1, E // 2) as ep:
                    pair(ep, False)
                for n in range(2):
                    add(E - 1, GROUPS - 2 + n, n)

            @block.tensor
            def _(pe):
                def up(e, ew, n, par, hc):
                    cs = slice(hc * P, (hc + 1) * P)
                    v, j = (e * GROUPS + n) * HC + hc, slot(par, hc)
                    pe.wait_ge(s["u_ready"], before(v))
                    moving = (h_hi[:, ds(n * GN, GN)], h_lo[:, ds(n * GN, GN)])
                    for i, (w, x) in enumerate(passes((w1_hi[ew][:, cs], w1_lo[ew][:, cs]), moving)):
                        m = pe.matmul(ps[:, j, :], w, x, start=(i == 0), stop=(i == 2))
                    m.then_inc(s["up"], 1)

                def spread(e, ew, n, par):
                    g = e * GROUPS + n
                    pe.wait_ge(s["wb_ready"], before(g))
                    pe.matmul(ps[:, UB + 2 + par, :], pick_e[ew][:, :], wrow[:, ds(n * GN, GN)], start=True, stop=True).then_inc(s["spread"], 1)

                def down(e, ew, n, par, hc):
                    g = e * GROUPS + n
                    if hc == 0:
                        pe.wait_ge(s["yw_ready"], before(g))
                    pe.wait_ge(s["ulo_ready"], done(g * HC + hc, UB))
                    cs = slice(hc * P, (hc + 1) * P)
                    for i, (w, a) in enumerate(passes((w2_hi[ew][:, cs], w2_lo[ew][:, cs]),
                                                      (u_hi[par][:, hc, :], u_lo[par][:, hc, :]))):
                        m = pe.matmul(ps[:, UB + par, :], w, a, start=(hc == 0 and i == 0), stop=(hc == HC - 1 and i == 2))
                    if hc == HC - 1:
                        m.then_inc(s["down"], 1)

                def both(this, other):
                    for hc in range(HC):
                        up(*this, hc)
                        if hc == 0:
                            spread(*this)
                        if other:
                            down(*other, hc)

                def pair(ep, first):
                    for ew in range(2):
                        e = ep * 2 + ew
                        pe.wait_ge(s["wlo_ready"], done(e))
                        pe.sem_inc(s["pe_held"], 1)
                        both((e, ew, 0, 0), None if first and ew == 0 else (e - 1, 1 - ew, GROUPS - 1, 1))
                        with pe.Fori(0, GROUPS // 2 - 1) as it:
                            both((e, ew, it * 2 + 1, 1), (e, ew, it * 2, 0))
                            both((e, ew, it * 2 + 2, 0), (e, ew, it * 2 + 1, 1))
                        both((e, ew, GROUPS - 1, 1), (e, ew, GROUPS - 2, 0))

                pe.sem_inc(s["down"], 2)
                pair(0, True)
                with pe.Fori(1, E // 2) as ep:
                    pair(ep, False)
                for hc in range(HC):
                    down(E - 1, 1, GROUPS - 1, 1, hc)

            @block.gpsimd
            def _(pool):
                pool.tensor_tensor(onehot[:, :], c.ident[0:LOW + E, 0:E], c.ident[0:LOW + E, LOW:LOW + E], ALU.add).then_inc(s["onehot_ready"], 1)
                pool.sem_inc(s["x_out"], 2)
                with pool.Fori(0, E) as e:
                    with pool.Fori(0, GROUPS // 2) as it:
                        for par in range(2):
                            n = it * 2 + par
                            g = e * GROUPS + n
                            pool.wait_ge(s["yw_ready"], done(g))
                            pool.wait_ge(s["x_out"], before(g))
                            xt = c.x[:, ds(n * GN, GN)]
                            pool.tensor_tensor(xt, xt, yw[par][:, :], ALU.add).then_inc(s["x_out"], 1)


def stage_graph_conv(c):
    nc = c.nc
    T, N, B, GROUPS = c.T, c.N, c.B, c.GROUPS
    NT = N // P
    HALF = B // 2
    with ExitStack() as outer:
        def sbo(name, shape, dt=F32):
            return outer.enter_context(nc.sbuf_tensor("gc_" + name, shape, dt))
        y0 = (sbo("y0_hi", [P, T + 4], F32R), sbo("y0_lo", [P, T + 4], F32R))
        with ExitStack() as conv:
            y1 = tuple(conv.enter_context(nc.sbuf_tensor(f"gc_y1_{n}", [P, T], F32R)) for n in ("hi", "lo"))
            wg = [conv.enter_context(nc.sbuf_tensor(f"gc_wg{i}", [P, P], F32)) for i in range(2)]
            bg = [conv.enter_context(nc.sbuf_tensor(f"gc_bg{i}", [P, HALF, P], F32)) for i in range(2)]

            with ExitStack() as ctx:
                xn = norm_buffers(nc, ctx, "gy")
                hT = [ctx.enter_context(nc.sbuf_tensor(f"gy_hT{i}", [P, GN], F32)) for i in range(2)]
                y = [ctx.enter_context(nc.sbuf_tensor(f"gy_y{i}", [P, GN], F32)) for i in range(2)]
                ps = ctx.enter_context(nc.psum_tensor("gy_ps", [P, 4, 512], F32))
                s = semaphores(nc, ctx, "gy", NORM_SEMS + " w_in hT_ready mapped y_ready hi_ready lo_ready")
                loads = (2 + 2 * HALF) * 16
                block = ctx.enter_context(nc.Block())

                @block.sync
                def _(sp):
                    for i in range(2):
                        sp.dma_start(wg[i][:, :], c.ins[f"Wg{i}"]).then_inc(s["w_in"], 16)
                        for k in range(HALF):
                            sp.dma_start(bg[i][:, k, :], c.ins[f"bg{i}"].broadcast_to([P, P])).then_inc(s["w_in"], 16)
                    sp.wait_ge(s["w_in"], loads)

                @block.vector
                def _(dve):
                    dve.sem_inc(s["y_ready"], 2)
                    dve.sem_inc(s["lo_ready"], 2)
                    dve.wait_ge(s["w_in"], loads)
                    dve.memset(y0[0][:, T:T + 4].bitcast(F32), 0.0)
                    dve.memset(y0[1][:, T:T + 4].bitcast(F32), 0.0)
                    with dve.Fori(0, GROUPS // 2) as it:
                        for par in range(2):
                            normalise_group(dve, c, xn, s, it * 2 + par, par)
                        for par in range(2):
                            g = it * 2 + par
                            dve.wait_ge(s["mapped"], g + 1)
                            dve.tensor_tensor(y[par][:, :], ps[:, 2 + par, :], bg[0][:, :, :].rearrange("p k d -> p (k d)"), ALU.add).then_inc(s["y_ready"], 1)
                            dve.wait_ge(s["hi_ready"], done(g))
                            dve.tensor_tensor(y0[1][:, ds(g * GN, GN)], y[par][:, :], y0[0][:, ds(g * GN, GN)].bitcast(F32),
                                              ALU.subtract).then_inc(s["lo_ready"], 1)

                @block.scalar
                def _(act):
                    act.sem_inc(s["hT_ready"], 2)
                    act.sem_inc(s["hi_ready"], 2)
                    with act.Fori(0, GROUPS // 2) as it:
                        for par in range(2):
                            g = it * 2 + par
                            act.wait_ge(s["transposed"], done(g))
                            act.wait_ge(s["y_ready"], before(g))
                            act.copy(hT[par][:, :], ps[:, par, :]).then_inc(s["hT_ready"], 1)
                        for par in range(2):
                            g = it * 2 + par
                            act.wait_ge(s["y_ready"], done(g))
                            act.copy(y0[0][:, ds(g * GN, GN)], y[par][:, :]).then_inc(s["hi_ready"], 1)

                @block.tensor
                def _(pe):
                    pe.sem_inc(s["transposed"], 2)
                    pe.wait_ge(s["w_in"], loads)
                    with pe.Fori(0, GROUPS // 2) as it:
                        for par in range(2):
                            transpose_group(pe, c, xn, s, it * 2 + par, par, ps[:, par, :])
                        for par in range(2):
                            g = it * 2 + par
                            pe.wait_ge(s["hT_ready"], done(g))
                            pe.wait_ge(s["y_ready"], before(g))
                            for k in range(GT):
                                m = pe.matmul(ps[:, 2 + par, k * P:(k + 1) * P], hT[par][:, k * P:(k + 1) * P], wg[0][:, :], start=True, stop=True)
                            m.then_inc(s["mapped"], 1)

            convolve(c, "gc0", y0, y1, y1, wg[1], bg[1])
            convolve(c, "gc1", y1, y0, y0, None, None)
        recycle_semaphores(nc)
        stage_lstm(c, y0)
        recycle_semaphores(nc)
        add_features(c, y0)


def convolve(c, name, y, _, z, w, b):
    nc = c.nc
    T, N, B = c.T, c.N, c.B
    NT = N // P
    HALF = B // 2
    with ExitStack() as ctx:
        def sb(n, shape, dt=F32, count=2):
            return [ctx.enter_context(nc.sbuf_tensor(f"{name}_{n}{i}", shape, dt)) for i in range(count)]
        adj = sb("adj", [P, N])
        a_hi = sb("a_hi", [P, N], F32R)
        a_lo = sb("a_lo", [P, N], F32R)
        h = sb("h", [P, HALF * P])
        f = sb("f", [P, HALF * P])
        ps = ctx.enter_context(nc.psum_tensor(name + "_ps", [P, 8, 512], F32))
        s = semaphores(nc, ctx, name, "adj_in0 adj_in1 hi_ready lo_ready convolved h_ready turned f_ready mapped z_hi z_lo z_ready")
        adj_in = (s["adj_in0"], s["adj_in1"])
        hi_v = z[0][:, 0:T].rearrange("p (b n) -> p b n", b=B)
        lo_v = z[1][:, 0:T].rearrange("p (b n) -> p b n", b=B)
        block = ctx.enter_context(nc.Block())

        def dest(v, half, t):
            return v[:, half * HALF:(half + 1) * HALF, ds(t * P, P)]

        def by_graph(a):
            return a.rearrange("p (b n) -> p b n", b=HALF)

        @block.sync
        def _(sp):
            rows = c.ins["adjT"].rearrange("t p s j -> (t p) (s j)")
            with sp.Fori(0, NT // 2) as it:
                for par in range(2):
                    t = it * 2 + par
                    sp.wait_ge(s["lo_ready"], before(t))
                    sp.dma_start(adj[par][:, :], rows[ds(t * P, P), :]).then_inc(adj_in[par], 16)
            sp.wait_ge(s["adj_in0"], NT // 2 * 16)
            sp.wait_ge(s["adj_in1"], NT // 2 * 16)

        @block.scalar
        def _(act):
            act.sem_inc(s["hi_ready"], 2)
            act.sem_inc(s["h_ready"], 2)
            act.sem_inc(s["z_hi"], 2)
            with act.Fori(0, NT // 2) as it:
                for par in range(2):
                    t = it * 2 + par
                    act.wait_ge(adj_in[par], it * 16 + 16)
                    act.copy(a_hi[par][:, :], adj[par][:, :]).then_inc(s["hi_ready"], 1)
                    for half in range(2):
                        g = t * 2 + half
                        act.wait_ge(s["convolved"], done(g))
                        act.wait_ge(s["turned"], before(g))
                        act.activation(h[half][:, :], ps[:, half, :], ACT.Relu).then_inc(s["h_ready"], 1)
                    for half in range(2):
                        g = t * 2 + half
                        if w is None:
                            act.wait_ge(s["turned"], done(g))
                            act.copy(dest(hi_v, half, t), by_graph(ps[:, 2 + half, :])).then_inc(s["z_hi"], 1)
                        else:
                            act.wait_ge(s["z_ready"], done(g))
                            act.copy(dest(hi_v, half, t), by_graph(f[half][:, :])).then_inc(s["z_hi"], 1)

        @block.vector
        def _(dve):
            for sem in (s["lo_ready"], s["f_ready"], s["z_ready"], s["z_lo"]):
                dve.sem_inc(sem, 2)
            with dve.Fori(0, NT // 2) as it:
                for par in range(2):
                    t = it * 2 + par
                    dve.wait_ge(s["hi_ready"], done(t))
                    dve.tensor_tensor(a_lo[par][:, :], adj[par][:, :], a_hi[par][:, :].bitcast(F32), ALU.subtract).then_inc(s["lo_ready"], 1)
                    if w is not None:
                        for half in range(2):
                            g = t * 2 + half
                            dve.wait_ge(s["turned"], done(g))
                            dve.wait_ge(s["z_lo"], before(g))
                            dve.tensor_copy(f[half][:, :], ps[:, 2 + half, :]).then_inc(s["f_ready"], 1)
                        for half in range(2):
                            g = t * 2 + half
                            dve.wait_ge(s["mapped"], done(g))
                            dve.tensor_tensor(f[half][:, :], ps[:, 4 + half, :], b[:, :, :].rearrange("p k d -> p (k d)"), ALU.add).then_inc(s["z_ready"], 1)
                    for half in range(2):
                        g = t * 2 + half
                        dve.wait_ge(s["z_hi"], done(g))
                        src = ps[:, 2 + half, :] if w is None else f[half][:, :]
                        dve.tensor_tensor(dest(lo_v, half, t), by_graph(src), dest(hi_v, half, t).bitcast(F32), ALU.subtract).then_inc(s["z_lo"], 1)

        @block.tensor
        def _(pe):
            for sem in (s["convolved"], s["turned"], s["mapped"]):
                pe.sem_inc(sem, 2)
            with pe.Fori(0, NT // 2) as it:
                for par in range(2):
                    t = it * 2 + par
                    pe.wait_ge(s["lo_ready"], done(t))
                    for half in range(2):
                        g = t * 2 + half
                        pe.wait_ge(s["h_ready"], before(g))
                        for st in range(NT):
                            ss = slice(st * P, (st + 1) * P)
                            moving = [v[:, 0:T].rearrange("p (b n) -> p b n", b=B)[:, half * HALF:(half + 1) * HALF, ss] for v in y]
                            for n, (a, m) in enumerate(passes((a_hi[par][:, ss], a_lo[par][:, ss]), moving)):
                                last = pe.matmul(ps[:, half, :], a, m, start=(st == 0 and n == 0), stop=(st == NT - 1 and n == 2))
                        last.then_inc(s["convolved"], 1)
                    for half in range(2):
                        g = t * 2 + half
                        pe.wait_ge(s["h_ready"], done(g))
                        pe.wait_ge(s["z_lo"], before(g))
                        for k in range(HALF):
                            last = pe.transpose(ps[:, 2 + half, k * P:(k + 1) * P], h[half][:, k * P:(k + 1) * P], c.ident[:, :])
                        last.then_inc(s["turned"], 1)
                    if w is not None:
                        for half in range(2):
                            g = t * 2 + half
                            pe.wait_ge(s["f_ready"], done(g))
                            pe.wait_ge(s["z_ready"], before(g))
                            for k in range(HALF):
                                last = pe.matmul(ps[:, 4 + half, k * P:(k + 1) * P], f[half][:, k * P:(k + 1) * P], w[:, :], start=True, stop=True)
                            last.then_inc(s["mapped"], 1)


def add_features(c, h):
    nc = c.nc
    with ExitStack() as ctx:
        f = [ctx.enter_context(nc.sbuf_tensor(f"add_f{i}", [P, GN], F32)) for i in range(2)]
        ps = ctx.enter_context(nc.psum_tensor("add_ps", [P, 2, 512], F32))
        s = semaphores(nc, ctx, "add", "f_ready turned x_out")
        block = ctx.enter_context(nc.Block())

        @block.vector
        def _(dve):
            dve.sem_inc(s["x_out"], 2)
            with dve.Fori(0, c.GROUPS // 2) as it:
                for par in range(2):
                    g = it * 2 + par
                    dve.wait_ge(s["x_out"], before(g))
                    dve.tensor_tensor(f[par][:, :], h[0][:, ds(g * GN, GN)].bitcast(F32), h[1][:, ds(g * GN, GN)].bitcast(F32),
                                      ALU.add).then_inc(s["f_ready"], 1)
                for par in range(2):
                    g = it * 2 + par
                    dve.wait_ge(s["turned"], g + 1)
                    xt = c.x[:, ds(g * GN, GN)]
                    dve.tensor_tensor(xt, ps[:, par, :], xt, ALU.add).then_inc(s["x_out"], 1)

        @block.tensor
        def _(pe):
            with pe.Fori(0, c.GROUPS // 2) as it:
                for par in range(2):
                    g = it * 2 + par
                    pe.wait_ge(s["f_ready"], g + 1)
                    pe.wait_ge(s["x_out"], before(g))
                    for k in range(GT):
                        m = pe.transpose(ps[:, par, k * P:(k + 1) * P], f[par][:, k * P:(k + 1) * P], c.ident[:, :])
                    m.then_inc(s["turned"], 1)


def stage_lstm(c, h):
    nc = c.nc
    N, T = c.N, c.T
    KINDS = 4
    bih, bhh = c.ins["bih"], c.ins["bhh"]
    with ExitStack() as outer:
        bias = outer.enter_context(nc.sbuf_tensor("ls_bias", [P, 4 * KINDS], F32))
        other = outer.enter_context(nc.sbuf_tensor("ls_bias_other", [P, 4 * KINDS], F32))
        for p in range(1, 5):
            with ExitStack() as ctx:
                if p in (1, 2, 4):
                    W = min(GN, T // p // 2)
                    span, blocks, kept = W * p, T // p // W, W
                else:
                    kept = N // p
                    W = kept + kept % 2
                    span, blocks = N, c.B
                lstm_windows(c, ctx, h, p, W, kept, span, blocks, bias, other)


def lstm_windows(c, ctx, h, p, W, kept, span, blocks, bias, other):
    nc = c.nc
    KINDS = 4
    I, F, G, O = range(KINDS)
    name = f"l{p}"

    def sb(n, shape, dt=F32):
        return [ctx.enter_context(nc.sbuf_tensor(f"{name}_{n}{i}", shape, dt)) for i in range(2)]
    raw = sb("raw", [P, KINDS * P])
    w_hi = sb("w_hi", [P, KINDS * P], F32R)
    w_lo = sb("w_lo", [P, KINDS * P], F32R)
    gate = [sb(n, [P, W]) for n in ("gi", "gf", "gc", "go")]
    new, kept_c, cell, tc, state = (sb(n, [P, W]) for n in ("new", "kept", "cell", "tc", "state"))
    s_hi = sb("s_hi", [P, W], F32R)
    s_lo = sb("s_lo", [P, W], F32R)
    ps = ctx.enter_context(nc.psum_tensor(name + "_ps", [P, 8, 512], F32))
    names = "w_in b_in bias_ready whi_ready wlo_ready pe_held"
    pairs = "products gates new_ready kept_ready cell_ready tanh_ready state_ready hi_ready lo_ready"
    s = semaphores(nc, ctx, name, names)
    q = [semaphores(nc, ctx, f"{name}_{i}", pairs) for i in range(2)]
    block = ctx.enter_context(nc.Block())
    steps = [(k, [g for g in (I, G, F, O) if k or g != F]) for k in range(p)]
    before_step = [sum(len(gs) for _, gs in steps[:k]) for k in range(p)]
    per_block = sum(len(gs) for _, gs in steps)

    def node(v, j, k, n):
        return v[:, ds(j * span + k, n, step=p)] if p > 1 else v[:, ds(j * span, n)]

    @block.sync
    def _(sp):
        sp.dma_start(raw[0][:, :], c.ins["WihT"][p - 1]).then_inc(s["w_in"], 16)
        sp.dma_start(raw[1][:, :], c.ins["WhhT"][p - 1]).then_inc(s["w_in"], 16)
        if p == 1:
            sp.dma_start(bias[:, :], c.ins["bih"]).then_inc(s["b_in"], 16)
            sp.dma_start(other[:, :], c.ins["bhh"]).then_inc(s["b_in"], 16)
            sp.wait_ge(s["b_in"], 32)
        sp.wait_ge(s["w_in"], 32)

    @block.scalar
    def _(act):
        act.wait_ge(s["w_in"], 32)
        act.copy(w_hi[0][:, :], raw[0][:, :])
        act.copy(w_hi[1][:, :], raw[1][:, :]).then_inc(s["whi_ready"], 1)
        if p == 1:
            act.wait_ge(s["bias_ready"], 1)
        for par in range(2):
            act.sem_inc(q[par]["gates"], 1)
        with act.Fori(0, blocks // 2) as it:
            for k, gs in steps:
                for par in range(2):
                    z = q[par]
                    for n, g in enumerate(gs):
                        act.wait_ge(z["products"], it * per_block + before_step[k] + n + 1)
                        if n == 0:
                            act.wait_ge(z["lo_ready"], it * p + k + 1)
                        act.activation(gate[g][par][:, :], ps[:, par * KINDS + g, 0:W], ACT.Tanh if g == G else ACT.Sigmoid,
                                       bias=bias[:, (p - 1) * KINDS + g:(p - 1) * KINDS + g + 1]).then_inc(z["gates"], 1)
                for par in range(2):
                    z = q[par]
                    act.wait_ge(z["cell_ready"], it * p + k + 1)
                    act.activation(tc[par][:, :], cell[par][:, :], ACT.Tanh).then_inc(z["tanh_ready"], 1)

    @block.gpsimd
    def _(pool):
        if p > 1:
            with pool.Fori(0, blocks // 2) as it:
                for k, gs in steps[1:]:
                    for par in range(2):
                        z = q[par]
                        pool.wait_ge(z["gates"], it * per_block + before_step[k] + 4)
                        pool.tensor_tensor(kept_c[par][:, :], gate[F][par][:, :], cell[par][:, :], ALU.mult).then_inc(z["kept_ready"], 1)

    @block.vector
    def _(dve):
        if p == 1:
            dve.wait_ge(s["b_in"], 32)
            dve.tensor_tensor(bias[:, :], bias[:, :], other[:, :], ALU.add).then_inc(s["bias_ready"], 1)
        dve.wait_ge(s["whi_ready"], 1)
        dve.tensor_tensor(w_lo[0][:, :], raw[0][:, :], w_hi[0][:, :].bitcast(F32), ALU.subtract)
        dve.tensor_tensor(w_lo[1][:, :], raw[1][:, :], w_hi[1][:, :].bitcast(F32), ALU.subtract).then_inc(s["wlo_ready"], 1)
        for par in range(2):
            dve.sem_inc(q[par]["lo_ready"], 1)
        with dve.Fori(0, blocks // 2) as it:
            for k, gs in steps:
                for par in range(2):
                    z = q[par]
                    dve.wait_ge(z["gates"], it * per_block + before_step[k] + 3)
                    goal = new if k else cell
                    m = dve.tensor_tensor(goal[par][:, :], gate[I][par][:, :], gate[G][par][:, :], ALU.mult)
                    if k:
                        m.then_inc(z["new_ready"], 1)
                        dve.wait_ge(z["new_ready"], it * (p - 1) + k)
                        dve.wait_ge(z["kept_ready"], it * (p - 1) + k)
                        m = dve.tensor_tensor(cell[par][:, :], new[par][:, :], kept_c[par][:, :], ALU.add)
                    m.then_inc(z["cell_ready"], 1)
                for par in range(2):
                    z = q[par]
                    j = it * 2 + par
                    dve.wait_ge(z["tanh_ready"], it * p + k + 1)
                    dve.tensor_tensor(state[par][:, :], gate[O][par][:, :], tc[par][:, :], ALU.mult).then_inc(z["state_ready"], 1)
                    hi, lo = s_hi[par][:, 0:W], s_lo[par][:, 0:W]
                    n = W
                    if k == p - 1:
                        n = kept
                        hi, lo = node(h[0], j, k, n), node(h[1], j, k, n)
                    dve.wait_ge(z["state_ready"], it * p + k + 1)
                    dve.tensor_copy(hi, state[par][:, 0:n]).then_inc(z["hi_ready"], 1)
                    dve.wait_ge(z["hi_ready"], it * p + k + 1)
                    dve.tensor_tensor(lo, state[par][:, 0:n], hi.bitcast(F32), ALU.subtract).then_inc(z["lo_ready"], 1)

    @block.tensor
    def _(pe):
        pe.wait_ge(s["wlo_ready"], 1)
        with pe.Fori(0, blocks // 2) as it:
            for k, gs in steps:
                for par in range(2):
                    z = q[par]
                    j = it * 2 + par
                    moving = (node(h[0], j, k, W), node(h[1], j, k, W))
                    for n, g in enumerate(gs):
                        cs = slice(g * P, (g + 1) * P)
                        if n == 0:
                            pe.wait_ge(z["gates"], it * per_block + before_step[k] + 1)
                        for i, (w, x) in enumerate(passes((w_hi[0][:, cs], w_lo[0][:, cs]), moving)):
                            last = pe.matmul(ps[:, par * KINDS + g, 0:W], w, x, start=(i == 0), stop=(k == 0 and i == 2))
                        if k == 0:
                            last.then_inc(z["products"], 1)
                    if k:
                        pe.wait_ge(z["lo_ready"], it * p + k + 1)
                        for g in gs:
                            cs = slice(g * P, (g + 1) * P)
                            for i, (w, x) in enumerate(passes((w_hi[1][:, cs], w_lo[1][:, cs]), (s_hi[par][:, :], s_lo[par][:, :]))):
                                last = pe.matmul(ps[:, par * KINDS + g, 0:W], w, x, start=False, stop=(i == 2))
                            last.then_inc(z["products"], 1)


def stage_store(c):
    nc = c.nc
    with ExitStack() as ctx:
        s = semaphores(nc, ctx, "store", "out_done")
        block = ctx.enter_context(nc.Block())

        @block.sync
        def _(sp):
            n = c.T // 4
            for q in range(4):
                sp.dma_start(c.out[:, q * n:(q + 1) * n], c.x[:, q * n:(q + 1) * n]).then_inc(s["out_done"], 16)
            sp.wait_ge(s["out_done"], 64)


def build(nc, ins, out):
    RETIRED.clear()
    c = Core()
    c.nc, c.out = nc, out
    c.ins = ins
    c.T, c.N = ins["x"].shape[1], ins["adj"].shape[2]
    c.B = c.T // c.N
    c.TILES, c.GROUPS = c.T // P, c.T // GN
    with ExitStack() as ctx:
        c.x = ctx.enter_context(nc.sbuf_tensor("x_sb", [P, c.T], F32))
        c.ident = ctx.enter_context(nc.sbuf_tensor("ident", [P, P], F32))
        c.ones = ctx.enter_context(nc.sbuf_tensor("ones", [P, P], F32))
        c.mean = ctx.enter_context(nc.sbuf_tensor("row_mean", [P, c.TILES], F32))
        c.rstd = ctx.enter_context(nc.sbuf_tensor("row_rstd", [P, c.TILES], F32))
        stage_load(c)
        stage_row_stats(c, "norm0", False)
        stage_attention(c)
        stage_row_stats(c, "norm1", True)
        stage_experts(c, 0)
        stage_turn(c, "turn0")
        stage_row_stats(c, "norm2", False)
        stage_graph_conv(c)
        stage_row_stats(c, "norm3", False)
        stage_experts(c, 1)
        stage_store(c)


def layouts(v):
    def node_tiles(a):
        return a.reshape(-1, P, a.shape[-1]).transpose(1, 0, 2)

    def rows_in_chunks(w):
        return w.reshape(w.shape[0], -1, P, w.shape[2]).transpose(0, 2, 1, 3)

    def columns(b):
        return b.reshape(-1, P).T

    B, N, D = v["x"].shape
    NT = N // P
    return {
        "x": node_tiles(v["x"].reshape(B * N, D)).reshape(P, B * N),
        "adj": node_tiles(v["adj"]),
        "adjT": v["adj"].reshape(NT, P, NT, P).transpose(0, 3, 2, 1),
        "L0_gnn_W": v["L0_gnn_W"], "L0_gnn_WT": v["L0_gnn_W"].T, "L0_gnn_a": columns(v["L0_gnn_a"].reshape(1, -1)),
        "L0_gamma": columns(v["L0_ffn_gamma"].reshape(1, -1)), "L0_beta": columns(v["L0_ffn_beta"].reshape(1, -1)),
        "L0_Wr": v["L0_ffn_Wr"], "L0_br": v["L0_ffn_br"].reshape(1, -1),
        "L0_W1": v["L0_ffn_W1"], "L0_b1": columns(v["L0_ffn_b1"]),
        "L0_W2": rows_in_chunks(v["L0_ffn_W2"]), "L0_b2": v["L0_ffn_b2"].T,
        "Wg0": v["L1_gnn_Wg0"], "bg0": v["L1_gnn_bg0"].reshape(1, -1),
        "Wg1": v["L1_gnn_Wg1"], "bg1": v["L1_gnn_bg1"].reshape(1, -1),
        "WihT": v["L1_gnn_Wih"].transpose(0, 2, 1), "WhhT": v["L1_gnn_Whh"].transpose(0, 2, 1),
        "bih": columns(v["L1_gnn_bih"]), "bhh": columns(v["L1_gnn_bhh"]),
        "L1_Wr": v["L1_ffn_Wg"].T, "L1_br": v["L1_ffn_bg"].reshape(1, -1),
        "L1_W1": v["L1_ffn_W1"].transpose(0, 2, 1), "L1_b1": columns(v["L1_ffn_b1"]),
        "L1_W2": rows_in_chunks(v["L1_ffn_W2"].transpose(0, 2, 1)), "L1_b2": v["L1_ffn_b2"].T,
    }


def kernel(**inputs):
    import numpy as np
    import concourse.bacc as bacc
    from concourse.bass_utils import run_bass_kernel_spmd

    nc = bacc.Bacc("TRN2", target_bir_lowering=False, num_devices=1)
    arrays, aps = {}, {}
    for name, value in layouts({n: np.asarray(a) for n, a in inputs.items()}).items():
        a = np.ascontiguousarray(value)
        arrays[f"in_{name}"] = a
        aps[name] = nc.dram_tensor(f"in_{name}", a.shape, mybir.dt.from_np(a.dtype), kind="ExternalInput").ap()
    out = nc.dram_tensor("out", arrays["in_x"].shape, F32, kind="ExternalOutput").ap()
    build(nc, aps, out)
    got = run_bass_kernel_spmd(nc, [arrays], core_ids=[0]).results[0]["out"]
    return np.ascontiguousarray(got.T).reshape(inputs["x"].shape)
```

```python
from contextlib import ExitStack, contextmanager

import concourse.bass as bass
from concourse import mybir

P = 128
ALU = mybir.AluOpType
ACT = mybir.ActivationFunctionType
AX = mybir.AxisListType
F32 = mybir.dt.float32
F32R = mybir.dt.float32r
EPS = 1e-5
ALPHA = 0.2
MASKED = -1e30
GT = 4
GN = GT * P
RETIRED = []


def ds(at, size, step=1):
    return bass.ds(at, size) if step == 1 else bass.ds(at, size, step)


class Core:
    pass


def semaphores(nc, ctx, stage, names):
    made = {n: nc.alloc_semaphore(f"{stage}_{n}") for n in names.split()}
    ctx.callback(RETIRED.extend, made.values())
    return made


def recycle_semaphores(nc):
    with nc.Block() as block:
        @block.gpsimd
        def _(pool):
            for sem in RETIRED[0::4]:
                pool.sem_clear(sem)

        @block.scalar
        def _(act):
            for sem in RETIRED[1::4]:
                act.sem_clear(sem)

        @block.vector
        def _(dve):
            for sem in RETIRED[2::4]:
                dve.sem_clear(sem)

        @block.tensor
        def _(pe):
            for sem in RETIRED[3::4]:
                pe.sem_clear(sem)
    for sem in RETIRED:
        nc.release_semaphore(sem)
    RETIRED.clear()


def passes(hi_lo_stationary, hi_lo_moving):
    (wh, wl), (mh, ml) = hi_lo_stationary, hi_lo_moving
    return ((wh, mh), (wh, ml), (wl, mh))


def before(n):
    return n + 1


def rounds(eng, steps, lag, body):
    peeled = (lag + 1) // 2 * 2
    for i in range(peeled):
        body(i, i % 2, lambda n, i=i: i >= n)
    with eng.Fori(peeled // 2, steps // 2) as it:
        for par in range(2):
            body(it * 2 + par, par, lambda n: True)
    for i in range(steps, steps + lag):
        body(i, i % 2, lambda n, i=i: i - n < steps)


def done(n, credits=2):
    return n + 1 + credits


NORM_SEMS = "xn_ready transposed"


def norm_buffers(nc, ctx, stage):
    return [ctx.enter_context(nc.sbuf_tensor(f"{stage}_xn{i}", [P, GN], F32)) for i in range(2)]


def normalise_group(dve, c, xn, s, g, par):
    dve.wait_ge(s["transposed"], before(g))
    for k in range(GT):
        last = dve.tensor_scalar(xn[par][:, k * P:(k + 1) * P], c.x[:, ds(g * GN + k * P, P)],
                                 c.mean[:, ds(g * GT + k, 1)], c.rstd[:, ds(g * GT + k, 1)], ALU.subtract, ALU.mult)
    last.then_inc(s["xn_ready"], 1)


def transpose_group(pe, c, xn, s, g, par, psum):
    pe.wait_ge(s["xn_ready"], g + 1)
    pe.wait_ge(s["hT_ready"], before(g))
    for k in range(GT):
        m = pe.transpose(psum[:, k * P:(k + 1) * P], xn[par][:, k * P:(k + 1) * P], c.ident[:, :])
    m.then_inc(s["transposed"], 1)


@contextmanager
def taking_statistics(c, stage):
    with c.nc.sbuf_tensor(stage + "_halves", [P, c.TILES, 6], F32) as c.halves:
        yield


def tile_stats(dve, c, t):
    return dve.bn_stats(c.halves[:, :, :].rearrange("p t s -> p (t s)")[:, ds(t * 6, 6)], c.x[:, ds(t * P, P)])


def group_stats(dve, c, g):
    for k in range(GT):
        last = tile_stats(dve, c, g * GT + k)
    return last


def stage_load(c):
    nc = c.nc
    with ExitStack() as ctx:
        PARTS = 4
        s = semaphores(nc, ctx, "load", "zeroed constants " + " ".join(f"x_in{q}" for q in range(PARTS)))
        block = ctx.enter_context(nc.Block())

        @block.sync
        def _(sp):
            n = c.T // PARTS
            for q in range(PARTS):
                sp.dma_start(c.x[:, q * n:(q + 1) * n], c.ins["x"][:, q * n:(q + 1) * n]).then_inc(s[f"x_in{q}"], 16)
            loads = 0
            for to, source in c.constants:
                sp.dma_start(to, source).then_inc(s["constants"], 16)
                loads += 1
            for q in range(PARTS):
                sp.wait_ge(s[f"x_in{q}"], 16)
            sp.wait_ge(s["constants"], loads * 16)

        @block.vector
        def _(dve):
            dve.memset(c.ones[:, :], 1.0)
            n = c.GROUPS // PARTS
            for q in range(PARTS):
                dve.wait_ge(s[f"x_in{q}"], 16)
                with dve.Fori(q * n // 2, (q + 1) * n // 2) as pair:
                    for par in range(2):
                        group_stats(dve, c, pair * 2 + par)

        @block.gpsimd
        def _(pool):
            pool.memset(c.ident[:, :], 0.0).then_inc(s["zeroed"], 1)
            pool.wait_ge(s["zeroed"], 1)
            pool.affine_select(out=c.ident[:, :], in_=c.ident[:, :], compare_op=ALU.not_equal, fill=1.0,
                               base=0, pattern=[[-1, P]], channel_multiplier=1)


def stage_row_stats(c, stage, twice):
    nc = c.nc
    NT = c.TILES
    with ExitStack() as ctx:
        halves = c.halves
        mean2, half, sq, m2, var, sd, v2 = (ctx.enter_context(nc.sbuf_tensor(f"{stage}_{n}", [P, NT], F32))
                                            for n in ("mean2", "half", "sq", "m2", "var", "sd", "v2"))
        warm = ctx.enter_context(nc.sbuf_tensor(stage + "_warm", [P, 1], F32))
        s = semaphores(nc, ctx, stage, "step deviation")
        norms = 2 if twice else 1
        block = ctx.enter_context(nc.Block())

        @block.vector
        def _(dve):
            me, mo, qe, qo = (halves[:, :, j] for j in (1, 4, 2, 5))
            dve.tensor_tensor(mean2[:, :], me, mo, ALU.add)
            dve.tensor_tensor(half[:, :], me, mo, ALU.subtract)
            dve.tensor_tensor(m2[:, :], qe, qo, ALU.add).then_inc(s["step"], 1)
            dve.wait_ge(s["step"], 1)
            dve.tensor_scalar(c.mean[:, :], mean2[:, :], 0.5, None, ALU.mult)
            dve.scalar_tensor_tensor(sq[:, :], half[:, :], 0.25, half[:, :], ALU.mult, ALU.mult).then_inc(s["step"], 1)
            dve.wait_ge(s["step"], 2)
            dve.scalar_tensor_tensor(var[:, :], m2[:, :], 1.0 / P, sq[:, :], ALU.mult, ALU.add).then_inc(s["step"], 1)
            dve.wait_ge(s["step"], 3)
            dve.tensor_scalar(v2[:, :], var[:, :], EPS, None, ALU.add).then_inc(s["step"], 1)
            dve.wait_ge(s["deviation"], 1)
            dve.reciprocal(c.rstd[:, :], sd[:, :]).then_inc(s["step"], 1)
            if twice:
                dve.wait_ge(s["step"], 5)
                dve.tensor_tensor(sq[:, :], var[:, :], c.rstd[:, :], ALU.mult).then_inc(s["step"], 1)
                dve.wait_ge(s["step"], 6)
                dve.tensor_tensor(m2[:, :], sq[:, :], c.rstd[:, :], ALU.mult).then_inc(s["step"], 1)
                dve.wait_ge(s["step"], 7)
                dve.tensor_scalar(v2[:, :], m2[:, :], EPS, None, ALU.add).then_inc(s["step"], 1)
                dve.wait_ge(s["deviation"], 2)
                dve.reciprocal(half[:, :], sd[:, :]).then_inc(s["step"], 1)
                dve.wait_ge(s["step"], 9)
                dve.tensor_tensor(c.rstd[:, :], c.rstd[:, :], half[:, :], ALU.mult)

        @block.scalar
        def _(act):
            act.activation(warm[:, :], c.ones[:, 0:1], ACT.Sqrt)
            for n in range(norms):
                act.wait_ge(s["step"], (4, 8)[n])
                act.activation(sd[:, :], v2[:, :], ACT.Sqrt).then_inc(s["deviation"], 1)


def stage_attention(c):
    nc = c.nc
    N, B, NT = c.N, c.B, c.N // P
    with ExitStack() as outer:
        def sbo(name, shape, dt=F32):
            return outer.enter_context(nc.sbuf_tensor("att_" + name, shape, dt))
        Wh = sbo("Wh", [P, c.T])
        s2row = sbo("s2row", [P, c.T])
        s1col = sbo("s1col", [P, c.TILES])
        s1col8 = sbo("s1col8", [P, c.TILES])
        mask = sbo("mask", [P, NT, N])

        with ExitStack() as ctx:
            def sb(name, shape, dt=F32):
                return ctx.enter_context(nc.sbuf_tensor("prj_" + name, shape, dt))
            xn = norm_buffers(nc, ctx, "prj")
            PW = P + 2
            W = sb("W", [P, PW])
            WT = sb("WT", [P, P])
            a12 = sb("a12", [P, 2])
            Wa2rep = sb("Wa2rep", [P, P])
            hT = [sb(f"hT{i}", [P, GN]) for i in range(2)]
            ps = ctx.enter_context(nc.psum_tensor("prj_ps", [P, 8, 512], F32))
            def psT(i):
                return ps[:, i, :]

            def psR(i):
                return ps[:, 2 + i, :]

            def psW(i, k):
                return ps[:, 4 + 2 * i + k // 2, k % 2 * PW:(k % 2 + 1) * PW]

            def columns(i, at, n):
                return [ps[:, 4 + 2 * i + b, 0:2 * PW].rearrange("p (k c) -> p k c", c=PW)[:, :, at:at + n] for b in range(2)]
            s = semaphores(nc, ctx, "prj", NORM_SEMS + " w_in adj_in wa wa_sb wrep "
                           "hT_ready projected Wh_out row_out")
            block = ctx.enter_context(nc.Block())

            @block.sync
            def _(sp):
                sp.dma_start(W[:, 0:P], c.ins["L0_gnn_W"]).then_inc(s["w_in"], 16)
                sp.dma_start(WT[:, :], c.ins["L0_gnn_WT"]).then_inc(s["w_in"], 16)
                sp.dma_start(a12[:, :], c.ins["L0_gnn_a"]).then_inc(s["w_in"], 16)
                sp.dma_start(mask[:, :, :], c.ins["adj"]).then_inc(s["adj_in"], 16)

            @block.gpsimd
            def _(pool):
                pool.wait_ge(s["adj_in"], 16)
                for t in range(NT):
                    pool.tensor_scalar(mask[:, t, :], mask[:, t, :], 0.0, MASKED, ALU.is_equal, ALU.mult)

            @block.tensor
            def _(pe):
                pe.wait_ge(s["w_in"], 48)
                pe.matmul(ps[:, 1, 0:2], WT[:, :], a12[:, :], start=True, stop=True).then_inc(s["wa"], 1)
                pe.wait_ge(s["wrep"], 1)
                pe.sem_inc(s["transposed"], 2)

                def body(g, par, wanted):
                    was = 1 - par
                    if wanted(0):
                        transpose_group(pe, c, xn, s, g, par, psT(par))
                    if wanted(1):
                        pe.wait_ge(s["hT_ready"], done(g - 1))
                        pe.wait_ge(s["Wh_out"], before(g - 1))
                        pe.wait_ge(s["row_out"], before(g - 1))
                        for k in range(GT):
                            pe.matmul(psW(was, k), hT[was][:, k * P:(k + 1) * P], W[:, :], start=True, stop=True)
                        pe.matmul(psR(was), Wa2rep[:, :], hT[was][:, :], start=True, stop=True).then_inc(s["projected"], 1)

                rounds(pe, c.GROUPS, 1, body)

            @block.scalar
            def _(act):
                act.sem_inc(s["hT_ready"], 2)
                act.sem_inc(s["row_out"], 2)

                def body(g, par, wanted):
                    was = 1 - par
                    if wanted(0):
                        act.wait_ge(s["transposed"], done(g))
                        act.wait_ge(s["row_out"], before(g))
                        act.copy(hT[par][:, :], psT(par)).then_inc(s["hT_ready"], 1)
                    if wanted(1):
                        act.wait_ge(s["projected"], g)
                        act.copy(s2row[:, ds((g - 1) * GN, GN)], psR(was)).then_inc(s["row_out"], 1)

                rounds(act, c.GROUPS, 1, body)

            @block.vector
            def _(dve):
                dve.sem_inc(s["Wh_out"], 2)
                dve.wait_ge(s["wa"], 1)
                dve.wait_ge(s["w_in"], 48)
                dve.tensor_copy(W[:, P:PW], ps[:, 1, 0:2]).then_inc(s["wa_sb"], 1)
                dve.wait_ge(s["wa_sb"], 1)
                dve.tensor_scalar(Wa2rep[:, :], c.ones[:, :], W[:, P + 1:P + 2], None, ALU.mult).then_inc(s["wrep"], 1)

                def body(g, par, wanted):
                    if wanted(0):
                        normalise_group(dve, c, xn, s, g, par)
                    if wanted(2):
                        dve.wait_ge(s["projected"], g - 1)
                        for half, (wh, s1) in enumerate(zip(columns(par, 0, P), columns(par, P, 1))):
                            dve.tensor_copy(s1col[:, ds((g - 2) * GT + 2 * half, 2)], s1[:, :, 0])
                            last = dve.tensor_copy(Wh[:, ds((g - 2) * GN + half * 2 * P, 2 * P)].rearrange("p (k d) -> p k d", k=2), wh)
                        last.then_inc(s["Wh_out"], 1)

                rounds(dve, c.GROUPS, 2, body)
                dve.wait_ge(s["Wh_out"], done(c.GROUPS - 1))
                dve.tensor_scalar(s1col8[:, :], s1col[:, :], 1 - ALPHA, None, ALU.mult)

        with ExitStack() as ctx:
            def sb(name, shape, dt=F32):
                return [ctx.enter_context(nc.sbuf_tensor(f"att_{name}{i}", shape, dt)) for i in range(2)]
            q = sb("q", [P, N])
            e = sb("e", [P, N])
            p = sb("p", [P, N])
            pT = sb("pT", [P, N])
            M, m8, m2, bias, den, rden = (sb(n, [P, 1]) for n in ("M", "m8", "m2", "bias", "den", "rden"))
            warm = sb("warm", [P, 1])
            ps = ctx.enter_context(nc.psum_tensor("att_ps", [P, 8, 512], F32))
            s = semaphores(nc, ctx, "att", "q_ready max_ready small bias_ready relu_ready e_ready p_ready "
                           "transposed pT_ready attended rden_ready x_out")
            block = ctx.enter_context(nc.Block())
            TILES = c.TILES
            @block.gpsimd
            def _(pool):
                pool.sem_inc(s["q_ready"], 2)
                with pool.Fori(0, TILES // 2) as it:
                    for par in range(2):
                        i = it * 2 + par
                        pool.wait_ge(s["e_ready"], before(i))
                        pool.tensor_tensor(q[par][:, :], s2row[:, ds(it // (NT // 2) * N, N)],
                                           mask[:, :, :].rearrange("p t n -> p (t n)")[:, ds((it * 2 + par) % NT * N, N)],
                                           ALU.add).then_inc(s["q_ready"], 1)

            @block.vector
            def _(dve):
                for sem in (s["e_ready"], s["bias_ready"], s["x_out"]):
                    dve.sem_inc(sem, 2)

                def body(i, par, wanted):
                    was = 1 - par
                    if wanted(0):
                        dve.wait_ge(s["q_ready"], done(i))
                        if wanted(2):
                            dve.wait_ge(s["p_ready"], before(i))
                        dve.tensor_reduce(M[par][:, :], q[par][:, :], AX.X, ALU.max).then_inc(s["max_ready"], 1)
                        dve.wait_ge(s["relu_ready"], i + 1)
                        dve.scalar_tensor_tensor(e[par][:, :], q[par][:, :], ALPHA, e[par][:, :], ALU.mult, ALU.add).then_inc(s["e_ready"], 1)
                        dve.wait_ge(s["max_ready"], i + 1)
                        dve.tensor_scalar(m8[par][:, :], M[par][:, :], s1col[:, ds(i, 1)], 0.0, ALU.add, ALU.max)
                        dve.tensor_scalar(m2[par][:, :], M[par][:, :], -ALPHA, None, ALU.mult).then_inc(s["small"], 1)
                    if wanted(2):
                        dve.wait_ge(s["p_ready"], done(i - 2))
                        if wanted(4):
                            dve.wait_ge(s["x_out"], done(i - 4))
                        dve.reciprocal(rden[par][:, :], den[par][:, :]).then_inc(s["rden_ready"], 1)
                    if wanted(0):
                        dve.wait_ge(s["small"], i + 1)
                        dve.scalar_tensor_tensor(bias[par][:, :], m8[par][:, :], -(1 - ALPHA), m2[par][:, :],
                                                 ALU.mult, ALU.add).then_inc(s["bias_ready"], 1)
                    if wanted(3):
                        dve.wait_ge(s["rden_ready"], i - 2)
                        dve.wait_ge(s["attended"], done(i - 3))
                        xt = c.x[:, ds((i - 3) * P, P)]
                        dve.scalar_tensor_tensor(xt, ps[:, 4 + was, 0:P], rden[was][:, 0:1], xt, ALU.mult, ALU.add).then_inc(s["x_out"], 1)
                    if wanted(4):
                        dve.wait_ge(s["x_out"], done(i - 4))
                        tile_stats(dve, c, i - 4)

                rounds(dve, TILES, 4, body)

            @block.scalar
            def _(act):
                act.sem_inc(s["p_ready"], 2)
                act.sem_inc(s["pT_ready"], 2)
                act.activation(warm[0][:, :], c.ones[:, 0:1], ACT.Exp)

                def body(i, par, wanted):
                    was = 1 - par
                    if wanted(0):
                        act.wait_ge(s["q_ready"], done(i))
                        if wanted(2):
                            act.wait_ge(s["p_ready"], before(i))
                        act.activation(e[par][:, :], q[par][:, :], ACT.Relu, bias=s1col8[:, ds(i, 1)], scale=1 - ALPHA).then_inc(s["relu_ready"], 1)
                    if wanted(2):
                        act.wait_ge(s["transposed"], done(i - 2))
                        if wanted(4):
                            act.wait_ge(s["attended"], done(i - 4))
                        act.copy(pT[par][:, :], ps[:, 2 * par:2 * par + 2, :].rearrange("p b n -> p (b n)")).then_inc(s["pT_ready"], 1)
                    if wanted(1):
                        act.wait_ge(s["e_ready"], done(i - 1))
                        act.wait_ge(s["bias_ready"], done(i - 1))
                        if wanted(3):
                            act.wait_ge(s["rden_ready"], i - 2)
                        act.activation(p[was][:, :], e[was][:, :], ACT.Exp, bias=bias[was][:, 0:1], accum_out=den[was][:, 0:1]).then_inc(s["p_ready"], 1)

                rounds(act, TILES, 3, body)

            @block.tensor
            def _(pe):
                pe.sem_inc(s["transposed"], 2)
                pe.sem_inc(s["attended"], 2)

                def body(i, par, wanted):
                    was = 1 - par
                    if wanted(1):
                        pe.wait_ge(s["p_ready"], done(i - 1))
                        pe.wait_ge(s["pT_ready"], done(i - 3))
                        for j in range(NT):
                            m = pe.transpose(ps[:, 2 * was + j // 4, j % 4 * P:(j % 4 + 1) * P], p[was][:, j * P:(j + 1) * P], c.ident[:, :])
                        m.then_inc(s["transposed"], 1)
                    if wanted(2):
                        pe.wait_ge(s["pT_ready"], done(i - 2))
                        if wanted(4):
                            pe.wait_ge(s["x_out"], done(i - 4))
                        graph = (i - 2) // NT
                        for j in range(NT):
                            m = pe.matmul(ps[:, 4 + par, 0:P], pT[par][:, j * P:(j + 1) * P],
                                          Wh[:, ds((graph * NT + j) * P, P)], start=(j == 0), stop=(j == NT - 1))
                        m.then_inc(s["attended"], 1)

                rounds(pe, TILES, 3, body)


def stage_turn(c, name, loads):
    nc = c.nc
    with ExitStack() as ctx:
        xs = [ctx.enter_context(nc.sbuf_tensor(f"{name}_xs{i}", [P, GN], F32)) for i in range(2)]
        ps = ctx.enter_context(nc.psum_tensor(name + "_ps", [P, 2, 512], F32))
        s = semaphores(nc, ctx, name, "constants xs_ready turned x_out")
        block = ctx.enter_context(nc.Block())

        @block.sync
        def _(sp):
            for to, source in loads:
                sp.dma_start(to, source).then_inc(s["constants"], 16)
            if loads:
                sp.wait_ge(s["constants"], len(loads) * 16)

        @block.vector
        def _(dve):
            def body(g, par, wanted):
                if wanted(0):
                    dve.wait_ge(s["turned"], before(g))
                    dve.tensor_copy(xs[par][:, :], c.x[:, ds(g * GN, GN)]).then_inc(s["xs_ready"], 1)
                if wanted(2):
                    dve.wait_ge(s["x_out"], done(g - 2))
                    group_stats(dve, c, g - 2)

            rounds(dve, c.GROUPS, 2, body)

        @block.tensor
        def _(pe):
            pe.sem_inc(s["turned"], 2)
            with pe.Fori(0, c.GROUPS // 2) as it:
                for par in range(2):
                    g = it * 2 + par
                    pe.wait_ge(s["xs_ready"], g + 1)
                    pe.wait_ge(s["x_out"], before(g))
                    for k in range(GT):
                        m = pe.transpose(ps[:, par, k * P:(k + 1) * P], xs[par][:, k * P:(k + 1) * P], c.ident[:, :])
                    m.then_inc(s["turned"], 1)

        @block.scalar
        def _(act):
            act.sem_inc(s["x_out"], 2)
            with act.Fori(0, c.GROUPS // 2) as it:
                for par in range(2):
                    g = it * 2 + par
                    act.wait_ge(s["turned"], done(g))
                    act.copy(c.x[:, ds(g * GN, GN)], ps[:, par, :]).then_inc(s["x_out"], 1)


def router_constants(c, ctx, layer):
    L = f"L{layer}_"
    W1, b1, b2, Wr, br = (c.ins[L + n] for n in ("W1", "b1", "b2", "Wr", "br"))
    E, _, H = W1.shape
    b1col, b2col, wr, br4, gb = (ctx.enter_context(c.nc.sbuf_tensor(L + name, shape, F32)) for name, shape in (
        ("b1col", [P, E * H // P]), ("b2col", [P, E]), ("wr", [P, E]),
        ("br4", [P, GT, E]),
        ("gb", [P, 2])))
    loads = [(b1col[:, :], b1), (b2col[:, :], b2), (wr[:, :], Wr)]
    loads += [(br4[:, k, :], br.broadcast_to([P, E])) for k in range(GT)]
    if layer == 0:
        loads += [(gb[:, 0:1], c.ins["L0_gamma"]), (gb[:, 1:2], c.ins["L0_beta"])]
    return (b1col, b2col, wr, br4, gb), loads


def stage_experts(c, layer, out=None):
    nc = c.nc
    L = f"L{layer}_"
    W1, W2 = c.ins[L + "W1"], c.ins[L + "W2"]
    b1col, b2col, wr, br4, gb = c.router[layer][0]
    E, _, H = W1.shape
    HC = H // P
    act_fn = (ACT.Gelu, ACT.Relu)[layer]
    affine = layer == 0
    T, TILES, GROUPS = c.T, c.TILES, c.GROUPS
    with ExitStack() as outer:
        def sbo(name, shape, dt=F32):
            return outer.enter_context(nc.sbuf_tensor(L + name, shape, dt))
        h_hi = sbo("h_hi", [P, T], F32R)
        h_lo = sbo("h_lo", [P, T], F32R)
        scores = sbo("scores", [P, TILES, E])
        weight = sbo("weight", [P, TILES, E])
        raw1, raw2 = ([sbo(f"{n}{i}", [P, H]) for i in range(2)]
                      for n in ("raw1_", "raw2_"))
        LOW = 32
        wrow = sbo("wrow", [LOW + E, T], F32R)

        with ExitStack() as ctx:
            def sb(name, shape, dt=F32):
                return ctx.enter_context(nc.sbuf_tensor(L + name, shape, dt))
            xn = norm_buffers(nc, ctx, L + "rt")
            h = [sb(f"h{i}", [P, GN]) for i in range(2)]
            ps = ctx.enter_context(nc.psum_tensor(L + "rt_ps", [P, 4, 512], F32))
            s = semaphores(nc, ctx, L + "rt", NORM_SEMS + " hT_ready lo_ready routed scores_out")
            block = ctx.enter_context(nc.Block())

            @block.vector
            def _(dve):
                dve.sem_inc(s["lo_ready"], 2)
                dve.sem_inc(s["scores_out"], 2)

                def body(g, par, wanted):
                    was = 1 - par
                    if wanted(0):
                        normalise_group(dve, c, xn, s, g, par)
                    if wanted(1):
                        dve.wait_ge(s["hT_ready"], done(g - 1))
                        at = ds((g - 1) * GN, GN)
                        dve.tensor_tensor(h_lo[:, at], h[was][:, :], h_hi[:, at].bitcast(F32), ALU.subtract).then_inc(s["lo_ready"], 1)
                    if wanted(2):
                        dve.wait_ge(s["routed"], g - 1)
                        dve.tensor_tensor(scores[:, :, :].rearrange("p t e -> p (t e)")[:, ds((g - 2) * GT * E, GT * E)],
                                          ps[:, 2 + par, 0:GT * E], br4[:, :, :].rearrange("p t e -> p (t e)"),
                                          ALU.add).then_inc(s["scores_out"], 1)

                rounds(dve, GROUPS, 2, body)

            @block.scalar
            def _(act):
                act.sem_inc(s["hT_ready"], 2)

                def body(g, par, wanted):
                    if wanted(0):
                        act.wait_ge(s["transposed"], done(g))
                        act.wait_ge(s["lo_ready"], before(g))
                        act.wait_ge(s["scores_out"], before(g))
                        for out in (h[par][:, :], h_hi[:, ds(g * GN, GN)]):
                            if affine:
                                last = act.activation(out, ps[:, par, :], ACT.Identity, bias=gb[:, 1:2], scale=gb[:, 0:1])
                            else:
                                last = act.copy(out, ps[:, par, :])
                        last.then_inc(s["hT_ready"], 1)

                rounds(act, GROUPS, 0, body)

            @block.gpsimd
            def _(pool):
                pool.memset(wrow[:, :].bitcast(F32), 0.0)

            @block.tensor
            def _(pe):
                pe.sem_inc(s["transposed"], 2)

                def body(g, par, wanted):
                    was = 1 - par
                    if wanted(0):
                        transpose_group(pe, c, xn, s, g, par, ps[:, par, :])
                    if wanted(1):
                        pe.wait_ge(s["hT_ready"], done(g - 1))
                        pe.wait_ge(s["scores_out"], before(g - 1))
                        for k in range(GT):
                            m = pe.matmul(ps[:, 2 + was, k * E:(k + 1) * E], h[was][:, k * P:(k + 1) * P], wr[:, :], start=True, stop=True)
                        m.then_inc(s["routed"], 1)

                rounds(pe, GROUPS, 1, body)

        with ExitStack() as ctx:
            def sb(name, shape, dt=F32):
                return ctx.enter_context(nc.sbuf_tensor(L + name, shape, dt))
            EARLY = GROUPS // 2
            SLOTS = 4
            rank = sb("rank", [P, TILES, E])
            eq, seen, first, second, rest = (sb(n, [P, TILES, E]) for n in ("eq", "seen", "first", "second", "rest"))
            top1, top2, at1, at2, gap, ex, den, w1, w2 = (sb(n, [P, TILES]) for n in ("top1", "top2", "at1", "at2", "gap", "ex", "den", "w1", "w2"))
            wcopy = [sb(f"wcopy{i}", [P, GT * E]) for i in range(SLOTS)]
            xs = [sb(f"xs{i}", [P, GN]) for i in range(2)]
            ps = ctx.enter_context(nc.psum_tensor(L + "gate_ps", [P, SLOTS + 2, 512], F32))
            s = semaphores(nc, ctx, L + "gate", "rank_ready step exp_done weight_ready w_copied w_turned row_hi row_lo first_in xs_ready x_turned x_out")
            block = ctx.enter_context(nc.Block())

            @block.sync
            def _(sp):
                sp.dma_start(raw1[0][:, :], W1[0]).then_inc(s["first_in"], 16)
                sp.dma_start(raw2[0][:, :], W2[0].rearrange("p c d -> p (c d)")).then_inc(s["first_in"], 16)
                sp.wait_ge(s["first_in"], 32)

            def each(a):
                return a[:, :].unsqueeze(2).broadcast_to([P, TILES, E])

            @block.gpsimd
            def _(pool):
                for e in range(E):
                    last = pool.memset(rank[:, :, e], float(E - e))
                last.then_inc(s["rank_ready"], 1)
                with pool.Fori(0, GROUPS // 2) as it:
                    for par in range(2):
                        g = it * 2 + par
                        pool.wait_ge(s["x_out"], before(g))
                        pool.tensor_copy(xs[par][:, :], c.x[:, ds(g * GN, GN)]).then_inc(s["xs_ready"], 1)

            @block.vector
            def _(dve):
                n = [0]

                def step(instruction):
                    n[0] += 1
                    instruction.then_inc(s["step"], 1)
                    dve.wait_ge(s["step"], n[0])

                def pick(values, top, at, chosen):
                    step(dve.tensor_reduce(top[:, :], values[:, :, :], AX.X, ALU.max))
                    step(dve.tensor_tensor(eq[:, :, :], values[:, :, :], each(top), ALU.is_equal))
                    step(dve.tensor_tensor(seen[:, :, :], eq[:, :, :], rank[:, :, :], ALU.mult))
                    step(dve.tensor_reduce(at[:, :], seen[:, :, :], AX.X, ALU.max))
                    step(dve.tensor_tensor(chosen[:, :, :], rank[:, :, :], each(at), ALU.is_equal))

                dve.sem_inc(s["row_lo"], SLOTS)
                dve.wait_ge(s["rank_ready"], 1)
                pick(scores, top1, at1, first)
                step(dve.scalar_tensor_tensor(rest[:, :, :], first[:, :, :], MASKED, scores[:, :, :], ALU.mult, ALU.add))
                pick(rest, top2, at2, second)
                step(dve.tensor_tensor(gap[:, :], top2[:, :], top1[:, :], ALU.subtract))
                dve.wait_ge(s["exp_done"], 1)
                step(dve.tensor_scalar(den[:, :], ex[:, :], 1.0, None, ALU.add))
                step(dve.reciprocal(w1[:, :], den[:, :]))
                step(dve.tensor_tensor(w2[:, :], ex[:, :], w1[:, :], ALU.mult))
                step(dve.tensor_tensor(eq[:, :, :], first[:, :, :], each(w1), ALU.mult))
                step(dve.tensor_tensor(seen[:, :, :], second[:, :, :], each(w2), ALU.mult))
                dve.tensor_tensor(weight[:, :, :], eq[:, :, :], seen[:, :, :], ALU.add).then_inc(s["weight_ready"], 1)
                with dve.Fori(0, GROUPS // SLOTS) as it:
                    for slot in range(SLOTS):
                        g = it * SLOTS + slot
                        dve.wait_ge(s["row_hi"], g + 1)
                        dve.tensor_tensor(wrow[LOW:LOW + E, ds(g * GN, GN)], ps[0:E, slot, :], wrow[0:E, ds(g * GN, GN)].bitcast(F32),
                                          ALU.subtract).then_inc(s["row_lo"], 1)

            @block.scalar
            def _(act):
                def take_x(g, par):
                    act.wait_ge(s["x_turned"], g + 1)
                    act.copy(c.x[:, ds(g * GN, GN)], ps[:, SLOTS + par, :]).then_inc(s["x_out"], 1)

                def copy(g, slot):
                    act.copy(wcopy[slot][:, :], weight[:, :, :].rearrange("p t e -> p (t e)")[:, ds(g * GT * E, GT * E)]).then_inc(s["w_copied"], 1)

                def round_row(g, slot):
                    act.wait_ge(s["w_turned"], g + 1)
                    act.copy(wrow[0:E, ds(g * GN, GN)], ps[0:E, slot, :]).then_inc(s["row_hi"], 1)

                act.sem_inc(s["x_out"], 2)
                with act.Fori(0, EARLY // 4) as it:
                    for par in range(2):
                        take_x(it * 2 + par, par)
                act.wait_ge(s["step"], 12)
                act.activation(ex[:, :], gap[:, :], ACT.Exp).then_inc(s["exp_done"], 1)
                with act.Fori(EARLY // 4, EARLY // 2) as it:
                    for par in range(2):
                        take_x(it * 2 + par, par)
                act.wait_ge(s["weight_ready"], 1)
                for slot in range(SLOTS):
                    copy(slot, slot)

                def serve(it, more):
                    for slot in range(SLOTS):
                        round_row(it * SLOTS + slot, slot)
                        if more:
                            copy(it * SLOTS + SLOTS + slot, slot)
                        if slot % 2:
                            take_x(EARLY + it * 2 + slot // 2, slot // 2)

                with act.Fori(0, GROUPS // SLOTS - 1) as it:
                    serve(it, True)
                serve(GROUPS // SLOTS - 1, False)

            @block.tensor
            def _(pe):
                def turn_x(g, par):
                    pe.wait_ge(s["xs_ready"], g + 1)
                    pe.wait_ge(s["x_out"], before(g))
                    for k in range(GT):
                        m = pe.transpose(ps[:, SLOTS + par, k * P:(k + 1) * P], xs[par][:, k * P:(k + 1) * P], c.ident[:, :])
                    m.then_inc(s["x_turned"], 1)

                with pe.Fori(0, EARLY // 2) as it:
                    for par in range(2):
                        turn_x(it * 2 + par, par)
                with pe.Fori(0, GROUPS // SLOTS) as it:
                    for slot in range(SLOTS):
                        g = it * SLOTS + slot
                        pe.wait_ge(s["w_copied"], g + 1)
                        pe.wait_ge(s["row_lo"], before(g))
                        for k in range(GT):
                            m = pe.transpose(ps[0:E, slot, k * P:(k + 1) * P], wcopy[slot][:, k * E:(k + 1) * E], c.ident[:, :])
                        m.then_inc(s["w_turned"], 1)
                        if slot % 2:
                            turn_x(EARLY + it * 2 + slot // 2, slot // 2)

        with ExitStack() as ctx:
            def sb(name, shape, dt=F32, n=2):
                return [ctx.enter_context(nc.sbuf_tensor(f"{L}{name}{i}", shape, dt)) for i in range(n)]
            UB = 4
            w1_hi, w1_lo, w2_hi, w2_lo = (sb(n, [P, H], F32R) for n in ("w1_hi", "w1_lo", "w2_hi", "w2_lo"))
            b1e = sb("b1e", [P, HC])
            u = sb("u", [P, GN], n=UB)
            u_hi = sb("u_hi", [P, HC, GN], F32R)
            u_lo = sb("u_lo", [P, HC, GN], F32R)
            wb = sb("wb", [P, GN])
            yw = sb("yw", [P, GN])
            onehot = ctx.enter_context(nc.sbuf_tensor(L + "onehot", [LOW + E, E], F32))
            pick_e = sb("pick_e", [LOW + E, P], F32R)
            ps = ctx.enter_context(nc.psum_tensor(L + "ex_ps", [P, 8, 512], F32))
            s = semaphores(nc, ctx, L + "ex", "w_in0 w_in1 b1_ready whi_ready wlo_ready up u_ready uhi_ready ulo_ready down spread wb_ready yw_ready x_out pe_held onehot_ready stored")
            w_in = (s["w_in0"], s["w_in1"])
            block = ctx.enter_context(nc.Block())

            def slot(n, hc):
                return (n % 2 * HC + hc) % UB

            @block.sync
            def _(sp):
                def load(e, ew):
                    sp.wait_ge(s["wlo_ready"], before(e))
                    sp.dma_start(raw1[ew][:, :], W1.rearrange("e d h -> (e d) h")[ds(e % E * P, P), :]).then_inc(w_in[ew], 16)
                    sp.dma_start(raw2[ew][:, :], W2.rearrange("e p c d -> (e p) (c d)")[ds(e % E * P, P), :]).then_inc(w_in[ew], 16)

                load(1, 1)
                with sp.Fori(1, E // 2) as ep:
                    for ew in range(2):
                        load(ep * 2 + ew, ew)
                load(E, 0)
                sp.wait_ge(s["w_in0"], E // 2 * 32)
                sp.wait_ge(s["w_in1"], E // 2 * 32)
                if out is not None:
                    for g in range(0, GROUPS, 2):
                        sp.wait_ge(s["x_out"], done((E - 1) * GROUPS + g + 1))
                        sp.dma_start(out[:, g * GN:(g + 2) * GN], c.x[:, g * GN:(g + 2) * GN]).then_inc(s["stored"], 16)
                    sp.wait_ge(s["stored"], GROUPS // 2 * 16)

            @block.scalar
            def _(act):
                def split_weights(e, ew, loads):
                    if loads is not None:
                        act.wait_ge(w_in[ew], loads * 32)
                    act.copy(b1e[ew][:, :], b1col[:, ds(e % E * HC, HC)]).then_inc(s["b1_ready"], 1)
                    act.copy(pick_e[ew][:, :], onehot[:, ds(e % E, 1)].broadcast_to([LOW + E, P]))
                    act.copy(w1_hi[ew][:, :], raw1[ew][:, :])
                    act.copy(w2_hi[ew][:, :], raw2[ew][:, :]).then_inc(s["whi_ready"], 1)

                def activate(e, ew, n, par):
                    g = e * GROUPS + n
                    act.wait_ge(s["down"], before(g))
                    for hc in range(HC):
                        v, j = g * HC + hc, slot(par, hc)
                        act.wait_ge(s["up"], v + 1)
                        act.wait_ge(s["ulo_ready"], before(v))
                        last = act.activation(u[j][:, :], ps[:, j, :], act_fn, bias=b1e[ew][:, hc:hc + 1])
                        if hc % 2 == 0:
                            last = act.activation(u_hi[par][:, hc, :], ps[:, j, :], act_fn, bias=b1e[ew][:, hc:hc + 1])
                        last.then_inc(s["u_ready"], 1)
                    act.wait_ge(s["spread"], g + 1)
                    act.wait_ge(s["yw_ready"], before(g))
                    act.copy(wb[par][:, :], ps[:, UB + 2 + par, :]).then_inc(s["wb_ready"], 1)

                act.sem_inc(s["whi_ready"], 2)
                act.sem_inc(s["u_ready"], UB)
                act.sem_inc(s["wb_ready"], 2)
                act.wait_ge(s["onehot_ready"], 1)
                split_weights(0, 0, None)
                with act.Fori(0, E // 2) as ep:
                    for ew in range(2):
                        e = ep * 2 + ew
                        act.wait_ge(s["b1_ready"], e + 1)
                        for n in range(2):
                            activate(e, ew, n, n)
                        act.wait_ge(s["down"], done(e * GROUPS - 1))
                        split_weights(e + 1, 1 - ew, ep + 1)
                        with act.Fori(1, GROUPS // 2) as it:
                            for par in range(2):
                                activate(e, ew, it * 2 + par, par)

            @block.vector
            def _(dve):
                def split_weights(e, ew):
                    dve.wait_ge(s["whi_ready"], done(e))
                    dve.tensor_tensor(w1_lo[ew][:, :], raw1[ew][:, :], w1_hi[ew][:, :].bitcast(F32), ALU.subtract)
                    dve.tensor_tensor(w2_lo[ew][:, :], raw2[ew][:, :], w2_hi[ew][:, :].bitcast(F32), ALU.subtract).then_inc(s["wlo_ready"], 1)

                def split(e, n, par):
                    g = e * GROUPS + n
                    for hc in range(HC):
                        v, j = g * HC + hc, slot(par, hc)
                        dve.wait_ge(s["u_ready"], done(v, UB))
                        if hc % 2:
                            dve.tensor_copy(u_hi[par][:, hc, :], u[j][:, :]).then_inc(s["uhi_ready"], 1)
                            dve.wait_ge(s["uhi_ready"], g * (HC // 2) + hc // 2 + 1)
                        dve.tensor_tensor(u_lo[par][:, hc, :], u[j][:, :], u_hi[par][:, hc, :].bitcast(F32),
                                          ALU.subtract).then_inc(s["ulo_ready"], 1)

                def add(e, n, par):
                    g = e * GROUPS + n
                    dve.wait_ge(s["down"], done(g))
                    dve.wait_ge(s["wb_ready"], done(g))
                    dve.wait_ge(s["x_out"], before(g))
                    dve.scalar_tensor_tensor(yw[par][:, :], ps[:, UB + par, :], b2col[:, ds(e, 1)],
                                             wb[par][:, :], ALU.add, ALU.mult).then_inc(s["yw_ready"], 1)

                def pair(ep, first):
                    for ew in range(2):
                        e = ep * 2 + ew
                        for n in range(2):
                            if not (first and ew == 0):
                                add(e - 1, GROUPS - 2 + n, n)
                            split(e, n, n)
                        split_weights(e + 1, 1 - ew)
                        with dve.Fori(1, GROUPS // 2) as it:
                            for par in range(2):
                                add(e, it * 2 + par - 2, par)
                                split(e, it * 2 + par, par)

                dve.sem_inc(s["wlo_ready"], 2)
                dve.sem_inc(s["ulo_ready"], UB)
                dve.sem_inc(s["yw_ready"], 2)
                split_weights(0, 0)
                pair(0, True)
                with dve.Fori(1, E // 2) as ep:
                    pair(ep, False)
                for n in range(2):
                    add(E - 1, GROUPS - 2 + n, n)

            @block.tensor
            def _(pe):
                def up(e, ew, n, par, hc):
                    cs = slice(hc * P, (hc + 1) * P)
                    v, j = (e * GROUPS + n) * HC + hc, slot(par, hc)
                    pe.wait_ge(s["u_ready"], before(v))
                    moving = (h_hi[:, ds(n * GN, GN)], h_lo[:, ds(n * GN, GN)])
                    for i, (w, x) in enumerate(passes((w1_hi[ew][:, cs], w1_lo[ew][:, cs]), moving)):
                        m = pe.matmul(ps[:, j, :], w, x, start=(i == 0), stop=(i == 2))
                    m.then_inc(s["up"], 1)

                def spread(e, ew, n, par):
                    g = e * GROUPS + n
                    pe.wait_ge(s["wb_ready"], before(g))
                    pe.matmul(ps[:, UB + 2 + par, :], pick_e[ew][:, :], wrow[:, ds(n * GN, GN)], start=True, stop=True).then_inc(s["spread"], 1)

                def down(e, ew, n, par, hc):
                    g = e * GROUPS + n
                    if hc == 0:
                        pe.wait_ge(s["yw_ready"], before(g))
                    pe.wait_ge(s["ulo_ready"], done(g * HC + hc, UB))
                    cs = slice(hc * P, (hc + 1) * P)
                    for i, (w, a) in enumerate(passes((w2_hi[ew][:, cs], w2_lo[ew][:, cs]),
                                                      (u_hi[par][:, hc, :], u_lo[par][:, hc, :]))):
                        m = pe.matmul(ps[:, UB + par, :], w, a, start=(hc == 0 and i == 0), stop=(hc == HC - 1 and i == 2))
                    if hc == HC - 1:
                        m.then_inc(s["down"], 1)

                def both(this, other):
                    for hc in range(HC):
                        up(*this, hc)
                        if hc == 0:
                            spread(*this)
                        if other:
                            down(*other, hc)

                def pair(ep, first):
                    for ew in range(2):
                        e = ep * 2 + ew
                        pe.wait_ge(s["wlo_ready"], done(e))
                        pe.sem_inc(s["pe_held"], 1)
                        both((e, ew, 0, 0), None if first and ew == 0 else (e - 1, 1 - ew, GROUPS - 1, 1))
                        with pe.Fori(0, GROUPS // 2 - 1) as it:
                            both((e, ew, it * 2 + 1, 1), (e, ew, it * 2, 0))
                            both((e, ew, it * 2 + 2, 0), (e, ew, it * 2 + 1, 1))
                        both((e, ew, GROUPS - 1, 1), (e, ew, GROUPS - 2, 0))

                pe.sem_inc(s["down"], 2)
                pair(0, True)
                with pe.Fori(1, E // 2) as ep:
                    pair(ep, False)
                for hc in range(HC):
                    down(E - 1, 1, GROUPS - 1, 1, hc)

            @block.gpsimd
            def _(pool):
                pool.tensor_tensor(onehot[:, :], c.ident[0:LOW + E, 0:E], c.ident[0:LOW + E, LOW:LOW + E], ALU.add).then_inc(s["onehot_ready"], 1)
                pool.sem_inc(s["x_out"], 2)
                with pool.Fori(0, E) as e:
                    with pool.Fori(0, GROUPS // 2) as it:
                        for par in range(2):
                            n = it * 2 + par
                            g = e * GROUPS + n
                            pool.wait_ge(s["yw_ready"], done(g))
                            pool.wait_ge(s["x_out"], before(g))
                            xt = c.x[:, ds(n * GN, GN)]
                            pool.tensor_tensor(xt, xt, yw[par][:, :], ALU.add).then_inc(s["x_out"], 1)


def stage_graph_conv(c):
    nc = c.nc
    T, N, B, GROUPS = c.T, c.N, c.B, c.GROUPS
    NT = N // P
    HALF = B // 2
    with ExitStack() as outer:
        def sbo(name, shape, dt=F32):
            return outer.enter_context(nc.sbuf_tensor("gc_" + name, shape, dt))
        y0 = (sbo("y0_hi", [P, T + 4], F32R), sbo("y0_lo", [P, T + 4], F32R))
        with ExitStack() as conv:
            y1 = tuple(conv.enter_context(nc.sbuf_tensor(f"gc_y1_{n}", [P, T], F32R)) for n in ("hi", "lo"))
            wg, bg = c.maps
            adj = [conv.enter_context(nc.sbuf_tensor(f"gc_adj{i}", [P, N], F32)) for i in range(2)]

            with ExitStack() as ctx:
                xn = norm_buffers(nc, ctx, "gy")
                hT = [ctx.enter_context(nc.sbuf_tensor(f"gy_hT{i}", [P, GN], F32)) for i in range(2)]
                y = [ctx.enter_context(nc.sbuf_tensor(f"gy_y{i}", [P, GN], F32)) for i in range(2)]
                ps = ctx.enter_context(nc.psum_tensor("gy_ps", [P, 4, 512], F32))
                s = semaphores(nc, ctx, "gy", NORM_SEMS + " adj_in hT_ready mapped y_ready hi_ready lo_ready")
                block = ctx.enter_context(nc.Block())

                @block.sync
                def _(sp):
                    load_adj(c, sp, adj, s["adj_in"])

                @block.vector
                def _(dve):
                    dve.sem_inc(s["y_ready"], 2)
                    dve.sem_inc(s["lo_ready"], 2)
                    dve.memset(y0[0][:, T:T + 4].bitcast(F32), 0.0)
                    dve.memset(y0[1][:, T:T + 4].bitcast(F32), 0.0)

                    def body(g, par, wanted):
                        was = 1 - par
                        if wanted(0):
                            normalise_group(dve, c, xn, s, g, par)
                        if wanted(2):
                            dve.wait_ge(s["mapped"], g - 1)
                            dve.wait_ge(s["lo_ready"], before(g - 2))
                            dve.tensor_tensor(y[par][:, :], ps[:, 2 + par, :], bg[0][:, :, :].rearrange("p k d -> p (k d)"), ALU.add).then_inc(s["y_ready"], 1)
                        if wanted(3):
                            dve.wait_ge(s["hi_ready"], done(g - 3))
                            at = ds((g - 3) * GN, GN)
                            dve.tensor_tensor(y0[1][:, at], y[was][:, :], y0[0][:, at].bitcast(F32), ALU.subtract).then_inc(s["lo_ready"], 1)

                    rounds(dve, GROUPS, 3, body)

                @block.scalar
                def _(act):
                    act.sem_inc(s["hT_ready"], 2)
                    act.sem_inc(s["hi_ready"], 2)

                    def body(g, par, wanted):
                        if wanted(0):
                            act.wait_ge(s["transposed"], done(g))
                            act.wait_ge(s["y_ready"], before(g))
                            act.copy(hT[par][:, :], ps[:, par, :]).then_inc(s["hT_ready"], 1)
                        if wanted(2):
                            act.wait_ge(s["y_ready"], done(g - 2))
                            act.copy(y0[0][:, ds((g - 2) * GN, GN)], y[par][:, :]).then_inc(s["hi_ready"], 1)

                    rounds(act, GROUPS, 2, body)

                @block.tensor
                def _(pe):
                    pe.sem_inc(s["transposed"], 2)

                    def body(g, par, wanted):
                        was = 1 - par
                        if wanted(0):
                            transpose_group(pe, c, xn, s, g, par, ps[:, par, :])
                        if wanted(1):
                            pe.wait_ge(s["hT_ready"], done(g - 1))
                            pe.wait_ge(s["y_ready"], before(g - 1))
                            for k in range(GT):
                                m = pe.matmul(ps[:, 2 + was, k * P:(k + 1) * P], hT[was][:, k * P:(k + 1) * P], wg[0][:, :], start=True, stop=True)
                            m.then_inc(s["mapped"], 1)

                    rounds(pe, GROUPS, 1, body)

            convolve(c, "gc0", y0, y1, adj, wg[1], bg[1])
            convolve(c, "gc1", y1, y0, adj, None, None)
        recycle_semaphores(nc)
        stage_lstm(c, y0)
        recycle_semaphores(nc)
        with taking_statistics(c, "gc"):
            add_features(c, y0)
            stage_row_stats(c, "norm3", False)


def map_constants(c, ctx):
    HALF = c.B // 2
    wg = [ctx.enter_context(c.nc.sbuf_tensor(f"gc_wg{i}", [P, P], F32)) for i in range(2)]
    bg = [ctx.enter_context(c.nc.sbuf_tensor(f"gc_bg{i}", [P, HALF, P], F32)) for i in range(2)]
    loads = []
    for i in range(2):
        loads.append((wg[i][:, :], c.ins[f"Wg{i}"]))
        loads += [(bg[i][:, k, :], c.ins[f"bg{i}"].broadcast_to([P, P])) for k in range(HALF)]
    return (wg, bg), loads


def load_adj(c, sp, adj, arrived):
    rows = c.ins["adjT"].rearrange("t p s j -> (t p) (s j)")
    for t in range(2):
        sp.dma_start(adj[t][:, :], rows[t * P:(t + 1) * P, :]).then_inc(arrived, 16)
    sp.wait_ge(arrived, 32)


def convolve(c, name, y, z, adj, w, b):
    nc = c.nc
    T, N, B = c.T, c.N, c.B
    NT = N // P
    HALF = B // 2
    with ExitStack() as ctx:
        def sb(n, shape, dt=F32, count=2):
            return [ctx.enter_context(nc.sbuf_tensor(f"{name}_{n}{i}", shape, dt)) for i in range(count)]
        a_hi = sb("a_hi", [P, N], F32R)
        a_lo = sb("a_lo", [P, N], F32R)
        h = sb("h", [P, HALF * P])
        f = sb("f", [P, HALF * P])
        ps = ctx.enter_context(nc.psum_tensor(name + "_ps", [P, 8, 512], F32))
        s = semaphores(nc, ctx, name, "adj_in0 adj_in1 adj_next hi_ready lo_ready convolved h_ready turned f_ready mapped z_hi z_lo z_ready")
        adj_in = (s["adj_in0"], s["adj_in1"])
        hi_v = z[0][:, 0:T].rearrange("p (b n) -> p b n", b=B)
        lo_v = z[1][:, 0:T].rearrange("p (b n) -> p b n", b=B)
        block = ctx.enter_context(nc.Block())

        def dest(v, half, t):
            return v[:, half * HALF:(half + 1) * HALF, ds(t * P, P)]

        def by_graph(a):
            return a.rearrange("p (b n) -> p b n", b=HALF)

        @block.sync
        def _(sp):
            rows = c.ins["adjT"].rearrange("t p s j -> (t p) (s j)")
            with sp.Fori(1, NT // 2) as it:
                for par in range(2):
                    t = it * 2 + par
                    sp.wait_ge(s["lo_ready"], before(t))
                    sp.dma_start(adj[par][:, :], rows[ds(t * P, P), :]).then_inc(adj_in[par], 16)
            sp.wait_ge(s["adj_in0"], (NT // 2 - 1) * 16)
            sp.wait_ge(s["adj_in1"], (NT // 2 - 1) * 16)
            if w is not None:
                sp.wait_ge(s["lo_ready"], done(NT - 1))
                load_adj(c, sp, adj, s["adj_next"])

        @block.scalar
        def _(act):
            act.sem_inc(s["hi_ready"], 2)
            act.sem_inc(s["h_ready"], 2)
            act.sem_inc(s["z_hi"], 2)

            def body(t, par, wanted):
                if wanted(0):
                    if wanted(2):
                        act.wait_ge(adj_in[par], t // 2 * 16)
                        act.wait_ge(s["convolved"], done(t * 2 - 3))
                    act.copy(a_hi[par][:, :], adj[par][:, :]).then_inc(s["hi_ready"], 1)
                if wanted(1):
                    for half in range(2):
                        g = (t - 1) * 2 + half
                        act.wait_ge(s["convolved"], done(g))
                        act.wait_ge(s["turned"], before(g))
                        act.activation(h[half][:, :], ps[:, half, :], ACT.Relu).then_inc(s["h_ready"], 1)
                if wanted(2):
                    for half in range(2):
                        g = (t - 2) * 2 + half
                        if w is None:
                            act.wait_ge(s["turned"], done(g))
                            act.copy(dest(hi_v, half, t - 2), by_graph(ps[:, 2 + half, :])).then_inc(s["z_hi"], 1)
                        else:
                            act.wait_ge(s["z_ready"], done(g))
                            act.copy(dest(hi_v, half, t - 2), by_graph(f[half][:, :])).then_inc(s["z_hi"], 1)

            rounds(act, NT, 2, body)

        @block.vector
        def _(dve):
            for sem in (s["lo_ready"], s["f_ready"], s["z_ready"], s["z_lo"]):
                dve.sem_inc(sem, 2)

            def body(t, par, wanted):
                if wanted(0):
                    dve.wait_ge(s["hi_ready"], done(t))
                    dve.tensor_tensor(a_lo[par][:, :], adj[par][:, :], a_hi[par][:, :].bitcast(F32), ALU.subtract).then_inc(s["lo_ready"], 1)
                if wanted(2):
                    gs = [((t - 2) * 2 + half, half) for half in range(2)]
                    if w is not None:
                        for g, half in gs:
                            dve.wait_ge(s["turned"], done(g))
                            dve.wait_ge(s["z_lo"], before(g))
                            dve.tensor_copy(f[half][:, :], ps[:, 2 + half, :]).then_inc(s["f_ready"], 1)
                        for g, half in gs:
                            dve.wait_ge(s["mapped"], done(g))
                            dve.tensor_tensor(f[half][:, :], ps[:, 4 + half, :], b[:, :, :].rearrange("p k d -> p (k d)"), ALU.add).then_inc(s["z_ready"], 1)
                    for g, half in gs:
                        dve.wait_ge(s["z_hi"], done(g))
                        src = ps[:, 2 + half, :] if w is None else f[half][:, :]
                        dve.tensor_tensor(dest(lo_v, half, t - 2), by_graph(src), dest(hi_v, half, t - 2).bitcast(F32), ALU.subtract).then_inc(s["z_lo"], 1)

            rounds(dve, NT, 2, body)

        @block.tensor
        def _(pe):
            for sem in (s["convolved"], s["turned"], s["mapped"]):
                pe.sem_inc(sem, 2)

            def products(t, par, half):
                g = t * 2 + half
                pe.wait_ge(s["h_ready"], before(g))
                for st in range(NT):
                    ss = slice(st * P, (st + 1) * P)
                    moving = [v[:, 0:T].rearrange("p (b n) -> p b n", b=B)[:, half * HALF:(half + 1) * HALF, ss] for v in y]
                    for n, (a, m) in enumerate(passes((a_hi[par][:, ss], a_lo[par][:, ss]), moving)):
                        last = pe.matmul(ps[:, half, :], a, m, start=(st == 0 and n == 0), stop=(st == NT - 1 and n == 2))
                last.then_inc(s["convolved"], 1)

            def body(t, par, wanted):
                if wanted(1):
                    pe.wait_ge(s["lo_ready"], done(t - 1))
                    products(t - 1, 1 - par, 0)
                if wanted(2):
                    for half in range(2):
                        g = (t - 2) * 2 + half
                        pe.wait_ge(s["h_ready"], done(g))
                        pe.wait_ge(s["z_lo"], before(g))
                        for k in range(HALF):
                            last = pe.transpose(ps[:, 2 + half, k * P:(k + 1) * P], h[half][:, k * P:(k + 1) * P], c.ident[:, :])
                        last.then_inc(s["turned"], 1)
                if wanted(1):
                    products(t - 1, 1 - par, 1)
                if wanted(2) and w is not None:
                    for half in range(2):
                        g = (t - 2) * 2 + half
                        pe.wait_ge(s["f_ready"], done(g))
                        pe.wait_ge(s["z_ready"], before(g))
                        for k in range(HALF):
                            last = pe.matmul(ps[:, 4 + half, k * P:(k + 1) * P], f[half][:, k * P:(k + 1) * P], w[:, :], start=True, stop=True)
                        last.then_inc(s["mapped"], 1)

            rounds(pe, NT, 2, body)


def add_features(c, h):
    nc = c.nc
    with ExitStack() as ctx:
        f = [ctx.enter_context(nc.sbuf_tensor(f"add_f{i}", [P, GN], F32)) for i in range(2)]
        ps = ctx.enter_context(nc.psum_tensor("add_ps", [P, 2, 512], F32))
        s = semaphores(nc, ctx, "add", "f_ready turned x_out")
        block = ctx.enter_context(nc.Block())

        @block.gpsimd
        def _(pool):
            with pool.Fori(0, c.GROUPS // 2) as it:
                for par in range(2):
                    g = it * 2 + par
                    pool.wait_ge(s["turned"], before(g))
                    pool.tensor_tensor(f[par][:, :], h[0][:, ds(g * GN, GN)].bitcast(F32), h[1][:, ds(g * GN, GN)].bitcast(F32),
                                       ALU.add).then_inc(s["f_ready"], 1)

        @block.vector
        def _(dve):
            dve.sem_inc(s["x_out"], 2)

            def body(g, par, wanted):
                if wanted(0):
                    dve.wait_ge(s["turned"], done(g))
                    xt = c.x[:, ds(g * GN, GN)]
                    dve.tensor_tensor(xt, ps[:, par, :], xt, ALU.add).then_inc(s["x_out"], 1)
                if wanted(1):
                    dve.wait_ge(s["x_out"], done(g - 1))
                    group_stats(dve, c, g - 1)

            rounds(dve, c.GROUPS, 1, body)

        @block.tensor
        def _(pe):
            pe.sem_inc(s["turned"], 2)
            with pe.Fori(0, c.GROUPS // 2) as it:
                for par in range(2):
                    g = it * 2 + par
                    pe.wait_ge(s["f_ready"], g + 1)
                    pe.wait_ge(s["x_out"], before(g))
                    for k in range(GT):
                        m = pe.transpose(ps[:, par, k * P:(k + 1) * P], f[par][:, k * P:(k + 1) * P], c.ident[:, :])
                    m.then_inc(s["turned"], 1)


def stage_lstm(c, h):
    nc = c.nc
    N, T = c.N, c.T
    KINDS = 4
    bih, bhh = c.ins["bih"], c.ins["bhh"]
    with ExitStack() as outer:
        bias = outer.enter_context(nc.sbuf_tensor("ls_bias", [P, 4 * KINDS], F32))
        other = outer.enter_context(nc.sbuf_tensor("ls_bias_other", [P, 4 * KINDS], F32))
        raw, w_hi, w_lo = ([outer.enter_context(nc.sbuf_tensor(f"ls_{n}{i}", [P, 2 * KINDS * P], dt)) for i in range(2)]
                           for n, dt in (("raw", F32), ("w_hi", F32R), ("w_lo", F32R)))
        warm = outer.enter_context(nc.sbuf_tensor("ls_warm", [P, 1], F32))
        for p in range(1, 5):
            with ExitStack() as ctx:
                if p in (1, 2, 4):
                    W = min(GN, T // p // 2)
                    span, blocks, kept = W * p, T // p // W, W
                else:
                    kept = N // p
                    W = kept + kept % 2
                    span, blocks = N, c.B
                lstm_windows(c, ctx, h, p, W, kept, span, blocks, bias, other, raw, w_hi, w_lo, warm)


def lstm_windows(c, ctx, h, p, W, kept, span, blocks, bias, other, raw, w_hi, w_lo, warm):
    nc = c.nc
    KINDS = 4
    I, F, G, O = range(KINDS)
    name = f"l{p}"

    def sb(n, shape, dt=F32):
        return [ctx.enter_context(nc.sbuf_tensor(f"{name}_{n}{i}", shape, dt)) for i in range(2)]
    GW = KINDS * P
    this, other_slot = (p - 1) % 2, p % 2
    wih = [w[this][:, 0:GW] for w in (w_hi, w_lo)]
    whh = [w[this][:, GW:] for w in (w_hi, w_lo)]
    share = 2 * GW // (blocks // 2)
    gate = [sb(n, [P, W]) for n in ("gi", "gf", "gc", "go")]
    new, kept_c, cell, tc, state = (sb(n, [P, W]) for n in ("new", "kept", "cell", "tc", "state"))
    s_hi = sb("s_hi", [P, W], F32R)
    s_lo = sb("s_lo", [P, W], F32R)
    ps = ctx.enter_context(nc.psum_tensor(name + "_ps", [P, 8, 512], F32))
    names = "w_in next_in b_in bias_ready whi_ready wlo_ready next_hi next_ready"
    pairs = "products gates new_ready kept_ready cell_ready tanh_ready state_ready hi_ready lo_ready"
    s = semaphores(nc, ctx, name, names)
    q = [semaphores(nc, ctx, f"{name}_{i}", pairs) for i in range(2)]
    block = ctx.enter_context(nc.Block())
    steps = [(k, [g for g in (I, G, F, O) if k or g != F]) for k in range(p)]
    before_step = [sum(len(gs) for _, gs in steps[:k]) for k in range(p)]
    per_block = sum(len(gs) for _, gs in steps)

    def run_steps(start, finish):
        for k, gs in steps:
            if p > 1:
                for par in range(2):
                    start(k, gs, par)
                    finish(k, gs, par)
            else:
                for part in (start, finish):
                    for par in range(2):
                        part(k, gs, par)

    def node(v, j, k, n):
        return v[:, ds(j * span + k, n, step=p)] if p > 1 else v[:, ds(j * span, n)]

    @block.sync
    def _(sp):
        if p == 1:
            sp.dma_start(bias[:, :], c.ins["bih"]).then_inc(s["b_in"], 16)
            sp.dma_start(other[:, :], c.ins["bhh"]).then_inc(s["b_in"], 16)
            sp.dma_start(raw[this][:, 0:GW], c.ins["WihT"][p - 1]).then_inc(s["w_in"], 16)
            sp.dma_start(raw[this][:, GW:], c.ins["WhhT"][p - 1]).then_inc(s["w_in"], 16)
            sp.wait_ge(s["b_in"], 32)
            sp.wait_ge(s["w_in"], 32)
        if p < 4:
            sp.dma_start(raw[other_slot][:, 0:GW], c.ins["WihT"][p]).then_inc(s["next_in"], 16)
            sp.dma_start(raw[other_slot][:, GW:], c.ins["WhhT"][p]).then_inc(s["next_in"], 16)
            sp.wait_ge(s["next_in"], 32)

    @block.scalar
    def _(act):
        act.activation(warm[:, :], c.ones[:, 0:1], ACT.Sigmoid)
        if p == 1:
            act.wait_ge(s["w_in"], 32)
            act.copy(w_hi[this][:, :], raw[this][:, :]).then_inc(s["whi_ready"], 1)
            act.wait_ge(s["bias_ready"], 1)
        for par in range(2):
            act.sem_inc(q[par]["gates"], 1)
        with act.Fori(0, blocks // 2) as it:
            def gates(k, gs, par):
                z = q[par]
                for n, g in enumerate(gs):
                    act.wait_ge(z["products"], it * per_block + before_step[k] + n + 1)
                    if n == 0:
                        act.wait_ge(z["cell_ready"], it * p + k + 1)
                    if g == O:
                        act.wait_ge(z["state_ready"], it * p + k + 1)
                    act.activation(gate[g][par][:, :], ps[:, par * KINDS + g, 0:W], ACT.Tanh if g == G else ACT.Sigmoid,
                                   bias=bias[:, (p - 1) * KINDS + g:(p - 1) * KINDS + g + 1]).then_inc(z["gates"], 1)

            def squash(k, gs, par):
                z = q[par]
                act.wait_ge(z["cell_ready"], it * p + k + 2)
                act.activation(tc[par][:, :], cell[par][:, :], ACT.Tanh).then_inc(z["tanh_ready"], 1)

            run_steps(gates, squash)

    @block.gpsimd
    def _(pool):
        def split_share(it):
            cols = ds(it * share, share)
            pool.tensor_copy(w_hi[other_slot][:, cols], raw[other_slot][:, cols]).then_inc(s["next_hi"], 1)
            pool.wait_ge(s["next_hi"], it + 1)
            pool.tensor_tensor(w_lo[other_slot][:, cols], raw[other_slot][:, cols], w_hi[other_slot][:, cols].bitcast(F32),
                               ALU.subtract).then_inc(s["next_ready"], 1)

        if p < 4:
            pool.wait_ge(s["next_in"], 32)
        with pool.Fori(0, blocks // 2) as it:
            for k, gs in steps[1:]:
                for par in range(2):
                    z = q[par]
                    pool.wait_ge(z["gates"], it * per_block + before_step[k] + 4)
                    pool.tensor_tensor(kept_c[par][:, :], gate[F][par][:, :], cell[par][:, :], ALU.mult).then_inc(z["kept_ready"], 1)
            if p < 4:
                split_share(it)

    @block.vector
    def _(dve):
        if p == 1:
            dve.wait_ge(s["b_in"], 32)
            dve.tensor_tensor(bias[:, :], bias[:, :], other[:, :], ALU.add).then_inc(s["bias_ready"], 1)
            dve.wait_ge(s["whi_ready"], 1)
            dve.tensor_tensor(w_lo[this][:, :], raw[this][:, :], w_hi[this][:, :].bitcast(F32), ALU.subtract).then_inc(s["wlo_ready"], 1)
        for par in range(2):
            for n in ("lo_ready", "cell_ready", "state_ready"):
                dve.sem_inc(q[par][n], 1)
        with dve.Fori(0, blocks // 2) as it:
            def advance(k, gs, par):
                z = q[par]
                dve.wait_ge(z["gates"], it * per_block + before_step[k] + 3)
                goal = new if k else cell
                m = dve.tensor_tensor(goal[par][:, :], gate[I][par][:, :], gate[G][par][:, :], ALU.mult)
                if k:
                    m.then_inc(z["new_ready"], 1)
                    dve.wait_ge(z["new_ready"], it * (p - 1) + k)
                    dve.wait_ge(z["kept_ready"], it * (p - 1) + k)
                    m = dve.tensor_tensor(cell[par][:, :], new[par][:, :], kept_c[par][:, :], ALU.add)
                m.then_inc(z["cell_ready"], 1)

            def emit(k, gs, par):
                z = q[par]
                j = it * 2 + par
                dve.wait_ge(z["tanh_ready"], it * p + k + 1)
                dve.tensor_tensor(state[par][:, :], gate[O][par][:, :], tc[par][:, :], ALU.mult).then_inc(z["state_ready"], 1)
                hi, lo = s_hi[par][:, 0:W], s_lo[par][:, 0:W]
                n = W
                if k == p - 1:
                    n = kept
                    hi, lo = node(h[0], j, k, n), node(h[1], j, k, n)
                dve.wait_ge(z["state_ready"], it * p + k + 2)
                dve.tensor_copy(hi, state[par][:, 0:n]).then_inc(z["hi_ready"], 1)
                dve.wait_ge(z["hi_ready"], it * p + k + 1)
                dve.tensor_tensor(lo, state[par][:, 0:n], hi.bitcast(F32), ALU.subtract).then_inc(z["lo_ready"], 1)

            run_steps(advance, emit)

    @block.tensor
    def _(pe):
        if p == 1:
            pe.wait_ge(s["wlo_ready"], 1)
        with pe.Fori(0, blocks // 2) as it:
            for k, gs in steps:
                for par in range(2):
                    z = q[par]
                    j = it * 2 + par
                    moving = (node(h[0], j, k, W), node(h[1], j, k, W))
                    for n, g in enumerate(gs):
                        cs = slice(g * P, (g + 1) * P)
                        if n == 0:
                            pe.wait_ge(z["gates"], it * per_block + before_step[k] + 1)
                        for i, (w, x) in enumerate(passes((wih[0][:, cs], wih[1][:, cs]), moving)):
                            last = pe.matmul(ps[:, par * KINDS + g, 0:W], w, x, start=(i == 0), stop=(k == 0 and i == 2))
                        if k == 0:
                            last.then_inc(z["products"], 1)
                    if k:
                        pe.wait_ge(z["lo_ready"], it * p + k + 1)
                        for g in gs:
                            cs = slice(g * P, (g + 1) * P)
                            for i, (w, x) in enumerate(passes((whh[0][:, cs], whh[1][:, cs]), (s_hi[par][:, :], s_lo[par][:, :]))):
                                last = pe.matmul(ps[:, par * KINDS + g, 0:W], w, x, start=False, stop=(i == 2))
                            last.then_inc(z["products"], 1)


def build(nc, ins, out):
    RETIRED.clear()
    c = Core()
    c.nc, c.out = nc, out
    c.ins = ins
    c.T, c.N = ins["x"].shape[1], ins["adj"].shape[2]
    c.B = c.T // c.N
    c.TILES, c.GROUPS = c.T // P, c.T // GN
    with ExitStack() as ctx:
        c.x = ctx.enter_context(nc.sbuf_tensor("x_sb", [P, c.T], F32))
        c.ident = ctx.enter_context(nc.sbuf_tensor("ident", [P, P], F32))
        c.ones = ctx.enter_context(nc.sbuf_tensor("ones", [P, P], F32))
        c.mean = ctx.enter_context(nc.sbuf_tensor("row_mean", [P, c.TILES], F32))
        c.rstd = ctx.enter_context(nc.sbuf_tensor("row_rstd", [P, c.TILES], F32))
        c.router = [router_constants(c, ctx, layer) for layer in range(2)]
        c.constants = [pair for _, loads in c.router for pair in loads]
        with taking_statistics(c, "load"):
            stage_load(c)
            stage_row_stats(c, "norm0", False)
        with taking_statistics(c, "att"):
            stage_attention(c)
            stage_row_stats(c, "norm1", True)
        stage_experts(c, 0)
        with ExitStack() as maps:
            c.maps, loads = map_constants(c, maps)
            with taking_statistics(c, "turn0"):
                stage_turn(c, "turn0", loads)
                stage_row_stats(c, "norm2", False)
                stage_graph_conv(c)
        stage_experts(c, 1, c.out)


def layouts(v):
    def node_tiles(a):
        return a.reshape(-1, P, a.shape[-1]).transpose(1, 0, 2)

    def rows_in_chunks(w):
        return w.reshape(w.shape[0], -1, P, w.shape[2]).transpose(0, 2, 1, 3)

    def columns(b):
        return b.reshape(-1, P).T

    B, N, D = v["x"].shape
    NT = N // P
    return {
        "x": node_tiles(v["x"].reshape(B * N, D)).reshape(P, B * N),
        "adj": node_tiles(v["adj"]),
        "adjT": v["adj"].reshape(NT, P, NT, P).transpose(0, 3, 2, 1),
        "L0_gnn_W": v["L0_gnn_W"], "L0_gnn_WT": v["L0_gnn_W"].T, "L0_gnn_a": columns(v["L0_gnn_a"].reshape(1, -1)),
        "L0_gamma": columns(v["L0_ffn_gamma"].reshape(1, -1)), "L0_beta": columns(v["L0_ffn_beta"].reshape(1, -1)),
        "L0_Wr": v["L0_ffn_Wr"], "L0_br": v["L0_ffn_br"].reshape(1, -1),
        "L0_W1": v["L0_ffn_W1"], "L0_b1": columns(v["L0_ffn_b1"]),
        "L0_W2": rows_in_chunks(v["L0_ffn_W2"]), "L0_b2": v["L0_ffn_b2"].T,
        "Wg0": v["L1_gnn_Wg0"], "bg0": v["L1_gnn_bg0"].reshape(1, -1),
        "Wg1": v["L1_gnn_Wg1"], "bg1": v["L1_gnn_bg1"].reshape(1, -1),
        "WihT": v["L1_gnn_Wih"].transpose(0, 2, 1), "WhhT": v["L1_gnn_Whh"].transpose(0, 2, 1),
        "bih": columns(v["L1_gnn_bih"]), "bhh": columns(v["L1_gnn_bhh"]),
        "L1_Wr": v["L1_ffn_Wg"].T, "L1_br": v["L1_ffn_bg"].reshape(1, -1),
        "L1_W1": v["L1_ffn_W1"].transpose(0, 2, 1), "L1_b1": columns(v["L1_ffn_b1"]),
        "L1_W2": rows_in_chunks(v["L1_ffn_W2"].transpose(0, 2, 1)), "L1_b2": v["L1_ffn_b2"].T,
    }


def kernel(**inputs):
    import numpy as np
    import concourse.bacc as bacc
    from concourse.bass_utils import run_bass_kernel_spmd

    nc = bacc.Bacc("TRN2", target_bir_lowering=False, num_devices=1)
    arrays, aps = {}, {}
    for name, value in layouts({n: np.asarray(a) for n, a in inputs.items()}).items():
        a = np.ascontiguousarray(value)
        arrays[f"in_{name}"] = a
        aps[name] = nc.dram_tensor(f"in_{name}", a.shape, mybir.dt.from_np(a.dtype), kind="ExternalInput").ap()
    out = nc.dram_tensor("out", arrays["in_x"].shape, F32, kind="ExternalOutput").ap()
    build(nc, aps, out)
    got = run_bass_kernel_spmd(nc, [arrays], core_ids=[0]).results[0]["out"]
    return np.ascontiguousarray(got.T).reshape(inputs["x"].shape)
```
